# Optimizing a Trainium2 kernel written in Bass

```python
import numpy as np
import jax
import jax.numpy as jnp

def _softmax(x, axis=-1):
    return jax.nn.softmax(x, axis=axis)

def _gelu(x):
    return jax.nn.gelu(x, approximate=True)

def _silu(x):
    return jax.nn.silu(x)

def _sigmoid(x):
    return jax.nn.sigmoid(x)

def _layernorm(x, axis=-1, eps=1e-05):
    m = jnp.mean(x, axis=axis, keepdims=True)
    v = jnp.var(x, axis=axis, keepdims=True)
    return (x - m) / jnp.sqrt(v + eps)

def _scatter_add(tgt, idx, src, axis=0):
    return tgt.at[idx].add(src)

def _segment_sum(src, seg, n):
    return jax.ops.segment_sum(src, seg, n)
kernel_name = 'mk_decoder_postln_d1_seqx_r4_b71158'

def setup_inputs(seed: int=0):
    np.random.seed(seed)
    _w = jnp.asarray

    def _rec_inputs():
        import jax
        import jax.numpy as jnp
        _rk = jax.random.key(seed)
        x = 7.22e-05 + 1 * jax.random.normal(jax.random.fold_in(_rk, 1), (16, 256, 512), jnp.float32)
        _lenS = 256 - jax.random.randint(jax.random.fold_in(_rk, 7), (16,), 0, max(1, 256 // 4) + 1, jnp.int32)
        _lenS2 = 256 - jax.random.randint(jax.random.fold_in(_rk, 8), (16,), 0, max(1, 256 // 4) + 1, jnp.int32)
        _ctx_2048P = jax.random.normal(jax.random.fold_in(_rk, 11), (16, 16, 512), jnp.float32)
        _ctx_2048c = jax.random.dirichlet(jax.random.fold_in(_rk, 511), 0.3 * jnp.ones((16,), jnp.float32), (16, 256))
        _ctx_2048t = jnp.einsum('bsk,bkd->bsd', _ctx_2048c, _ctx_2048P)
        _ctx_2048t = _ctx_2048t * jax.lax.rsqrt(jnp.mean(jnp.square(_ctx_2048t)) + 1e-12) * 0.953939
        ctx_2048 = 4.13588e-05 + 0.999923 * (_ctx_2048t + 0.3 * jax.random.normal(jax.random.fold_in(_rk, 611), (16, 256, 512), jnp.float32))
        return (x, ctx_2048)
    x, ctx_2048 = _rec_inputs()

    def _L0_attn_setup():
        import jax, jax.numpy as jnp
        import numpy as np
        BATCH, SEQ, D_MODEL, N_HEADS, D_HEAD = (2, 512, 512, 16, 128)
        ATTN_SCALE = np.sqrt(D_HEAD).astype(np.float32)
        IGNORE = jnp.float32(-100000.0)
        key = jax.random.key(seed)
        ks = jax.random.split(key, 5)
        init = 1.0 / np.sqrt(D_MODEL)
        return {'x': jax.random.normal(ks[0], (BATCH, SEQ, D_MODEL), jnp.float32), 'W_Q': jax.random.normal(ks[1], (N_HEADS, D_MODEL, D_HEAD), jnp.float32) * init, 'W_K': jax.random.normal(ks[2], (N_HEADS, D_MODEL, D_HEAD), jnp.float32) * init, 'W_V': jax.random.normal(ks[3], (N_HEADS, D_MODEL, D_HEAD), jnp.float32) * init, 'W_O': jax.random.normal(ks[4], (N_HEADS, D_HEAD, D_MODEL), jnp.float32) * init, 'b_Q': jnp.zeros((N_HEADS, D_HEAD), jnp.float32), 'b_K': jnp.zeros((N_HEADS, D_HEAD), jnp.float32), 'b_V': jnp.zeros((N_HEADS, D_HEAD), jnp.float32), 'b_O': jnp.zeros((D_MODEL,), jnp.float32)}
    _L0_attn_all = _L0_attn_setup()
    _L0_attn_in = {k: v for k, v in _L0_attn_all.items() if k in ('W_Q', 'W_K', 'W_V', 'W_O', 'b_Q', 'b_K', 'b_V', 'b_O')}
    del _L0_attn_all

    def _L0_xattn_setup():
        import jax, jax.numpy as jnp
        import numpy as np
        B, S, DIM, HD = (4, 256, 512, 128)
        H = DIM // HD
        GN_EPS = 0.001

        def _decay_masks(n_heads, seq_len):
            gam = 1.0 - 2.0 ** (-5.0 - jnp.arange(n_heads, dtype=jnp.float32))
            idx = jnp.arange(seq_len, dtype=jnp.float32)
            expo = idx[None, :] - idx[:, None]
            D = jnp.where(expo[None, :, :] <= 0, gam[:, None, None] ** expo[None, :, :], 0.0)
            return D / jnp.sqrt(D.sum(axis=-1))[:, None, :]
        key = jax.random.key(seed)
        ks = jax.random.split(key, 8)
        x = jax.random.normal(ks[0], (B, S, DIM), dtype=jnp.float32)
        k = jax.random.normal(ks[1], (B, S, DIM), dtype=jnp.float32)
        v = jax.random.normal(ks[2], (B, S, DIM), dtype=jnp.float32)
        Wh = jax.random.normal(ks[3], (H, HD, HD), dtype=jnp.float32) / np.sqrt(HD)
        wg_w = jax.random.normal(ks[4], (DIM, DIM), dtype=jnp.float32) / np.sqrt(DIM)
        wo_w = jax.random.normal(ks[5], (DIM, DIM), dtype=jnp.float32) / np.sqrt(DIM)
        gn_gamma = jnp.ones((DIM,), dtype=jnp.float32)
        gn_beta = jnp.zeros((DIM,), dtype=jnp.float32)
        return {'x': x, 'k': k, 'v': v, 'Wh': Wh, 'wg_w': wg_w, 'wo_w': wo_w, 'gn_gamma': gn_gamma, 'gn_beta': gn_beta}
    _L0_xattn_all = _L0_xattn_setup()
    _L0_xattn_in = {k: v for k, v in _L0_xattn_all.items() if k in ('Wh', 'wg_w', 'wo_w', 'gn_gamma', 'gn_beta')}
    del _L0_xattn_all

    def _L0_ffn_setup():
        import jax, jax.numpy as jnp
        import numpy as np
        EPS = 1e-08

        def _quantize(w):
            gamma = jnp.mean(jnp.abs(w))
            return jnp.clip(jnp.round(w / (gamma + EPS)), -1.0, 1.0)

        def _bitlinear(x, w):
            return jnp.matmul(x, _quantize(w).T)
        key = jax.random.key(seed)
        k1, k2, k3, k4 = jax.random.split(key, 4)
        d, h = (512, 1408)
        x = jax.random.normal(k1, (4, 512, d), dtype=jnp.float32)
        w1 = jax.random.normal(k2, (h, d), dtype=jnp.float32)
        w2 = jax.random.normal(k3, (h, d), dtype=jnp.float32)
        w3 = jax.random.normal(k4, (d, h), dtype=jnp.float32)
        return {'x': x, 'w1': w1, 'w2': w2, 'w3': w3}
    _L0_ffn_all = _L0_ffn_setup()
    _L0_ffn_in = {k: v for k, v in _L0_ffn_all.items() if k in ('w1', 'w2', 'w3')}
    del _L0_ffn_all
    return {'x': x, 'ctx_2048': ctx_2048, 'L0_attn_W_Q': _L0_attn_in['W_Q'], 'L0_attn_W_K': _L0_attn_in['W_K'], 'L0_attn_W_V': _L0_attn_in['W_V'], 'L0_attn_W_O': _L0_attn_in['W_O'], 'L0_attn_b_Q': _L0_attn_in['b_Q'], 'L0_attn_b_K': _L0_attn_in['b_K'], 'L0_attn_b_V': _L0_attn_in['b_V'], 'L0_attn_b_O': _L0_attn_in['b_O'], 'L0_xattn_Wh': _L0_xattn_in['Wh'], 'L0_xattn_wg_w': _L0_xattn_in['wg_w'], 'L0_xattn_wo_w': _L0_xattn_in['wo_w'], 'L0_xattn_gn_gamma': _L0_xattn_in['gn_gamma'], 'L0_xattn_gn_beta': _L0_xattn_in['gn_beta'], 'L0_ffn_w1': _L0_ffn_in['w1'], 'L0_ffn_w2': _L0_ffn_in['w2'], 'L0_ffn_w3': _L0_ffn_in['w3']}

def reference(x, ctx_2048, L0_attn_W_Q, L0_attn_W_K, L0_attn_W_V, L0_attn_W_O, L0_attn_b_Q, L0_attn_b_K, L0_attn_b_V, L0_attn_b_O, L0_xattn_Wh, L0_xattn_wg_w, L0_xattn_wo_w, L0_xattn_gn_gamma, L0_xattn_gn_beta, L0_ffn_w1, L0_ffn_w2, L0_ffn_w3):
    import jax
    import jax.numpy as jnp

    def _L0_attn_ref(x, W_Q, W_K, W_V, W_O, b_Q, b_K, b_V, b_O):
        import jax, jax.numpy as jnp
        import numpy as np
        BATCH, SEQ, D_MODEL, N_HEADS, D_HEAD = (2, 512, 512, 16, 128)
        ATTN_SCALE = np.sqrt(D_HEAD).astype(np.float32)
        IGNORE = jnp.float32(-100000.0)
        q = jnp.einsum('bpd,hde->bphe', x, W_Q) + b_Q
        k = jnp.einsum('bpd,hde->bphe', x, W_K) + b_K
        v = jnp.einsum('bpd,hde->bphe', x, W_V) + b_V
        scores = jnp.einsum('bqhe,bkhe->bhqk', q, k) / ATTN_SCALE
        S = x.shape[1]
        causal = jnp.tril(jnp.ones((S, S), bool))
        scores = jnp.where(causal, scores, IGNORE)
        attn = jax.nn.softmax(scores, axis=-1)
        z = jnp.einsum('bkhe,bhqk->bqhe', v, attn)
        out = jnp.einsum('bqhe,hed->bqd', z, W_O) + b_O
        return out

    def _L0_xattn_ref(x, k, v, Wh, wg_w, wo_w, gn_gamma, gn_beta):
        import jax, jax.numpy as jnp
        import numpy as np
        B, S, DIM, HD = (4, 256, 512, 128)
        H = DIM // HD
        GN_EPS = 0.001

        def _decay_masks(n_heads, seq_len):
            gam = 1.0 - 2.0 ** (-5.0 - jnp.arange(n_heads, dtype=jnp.float32))
            idx = jnp.arange(seq_len, dtype=jnp.float32)
            expo = idx[None, :] - idx[:, None]
            D = jnp.where(expo[None, :, :] <= 0, gam[:, None, None] ** expo[None, :, :], 0.0)
            return D / jnp.sqrt(D.sum(axis=-1))[:, None, :]
        b, s, dim = x.shape
        h, hd, _ = Wh.shape
        xh = x.reshape(b, s, h, hd)
        kh = k.reshape(b, s, h, hd)
        vh = v.reshape(b, s, h, hd)
        Q = jnp.einsum('bshd,hde->bshe', xh, Wh)
        K = jnp.einsum('bshd,hde->bshe', kh, Wh)
        V = jnp.einsum('bshd,hde->bshe', vh, Wh)
        scores = jnp.einsum('bshe,bthe->bhst', Q, K) / jnp.sqrt(jnp.float32(hd))
        Dn = _decay_masks(h, s)
        masked = scores * Dn[None, :, :, :]
        A = jnp.maximum(jnp.abs(masked.sum(axis=0)), 1.0)
        O = jnp.einsum('hst,bthe->bshe', A, V).reshape(b, s, dim)
        mu = O.mean(axis=-1, keepdims=True)
        var = O.var(axis=-1, keepdims=True)
        Y = (O - mu) / jnp.sqrt(var + GN_EPS) * gn_gamma + gn_beta
        W = jax.nn.relu(x @ wg_w)
        return W * Y @ wo_w

    def _L0_ffn_ref(x, w1, w2, w3):
        import jax, jax.numpy as jnp
        import numpy as np
        EPS = 1e-08

        def _quantize(w):
            gamma = jnp.mean(jnp.abs(w))
            return jnp.clip(jnp.round(w / (gamma + EPS)), -1.0, 1.0)

        def _bitlinear(x, w):
            return jnp.matmul(x, _quantize(w).T)
        x1 = _bitlinear(x, w1)
        x2 = _bitlinear(x, w2)
        hidden = jax.nn.sigmoid(x1) * x2
        return _bitlinear(hidden, w3)
    x = _layernorm(x + _L0_attn_ref(x, L0_attn_W_Q, L0_attn_W_K, L0_attn_W_V, L0_attn_W_O, L0_attn_b_Q, L0_attn_b_K, L0_attn_b_V, L0_attn_b_O), axis=-1)
    x = _layernorm(x + _L0_xattn_ref(x, ctx_2048, ctx_2048, L0_xattn_Wh, L0_xattn_wg_w, L0_xattn_wo_w, L0_xattn_gn_gamma, L0_xattn_gn_beta), axis=-1)
    x = _layernorm(x + _L0_ffn_ref(x, L0_ffn_w1, L0_ffn_w2, L0_ffn_w3), axis=-1)
    return x

_drawn_inputs = setup_inputs


def setup_inputs(seed=0):
    import zlib

    import numpy as np

    out = dict(_drawn_inputs(seed))
    spreads = {'L0_attn_b_Q': (0.0, 0.1),
     'L0_attn_b_K': (0.0, 0.1),
     'L0_attn_b_V': (0.0, 0.1),
     'L0_attn_b_O': (0.0, 0.1),
     'L0_xattn_gn_gamma': (1.0, 0.2),
     'L0_xattn_gn_beta': (0.0, 0.1)}
    factors = {}
    for name, (base, spread) in spreads.items():
        noise = np.random.default_rng([zlib.crc32(name.encode()), seed]).standard_normal(out[name].shape)
        drawn = base * np.exp(spread * noise) if base else spread * noise
        out[name] = jnp.asarray(drawn.astype(out[name].dtype))
    for name, factor in factors.items():
        out[name] = (out[name] * factor).astype(out[name].dtype)
    return out
```

```python
from contextlib import ExitStack

import concourse.bass as bass
from concourse import mybir

F32 = mybir.dt.float32
F32R = mybir.dt.float32r
ACT = mybir.ActivationFunctionType
ALU = mybir.AluOpType
AX_X = mybir.AxisListType.X

P = 128
BATCH, SEQ, DIM = 16, 256, 512
HEADS, DH = 16, 128
CH = DIM // P
TPB = SEQ // P
TILES = BATCH * TPB
GROUPS, GH = 4, 4
STEPS = BATCH * GH
UNITS = 16
RING = 4
KEYS = P + SEQ
MASKED = -1e30
LN_EPS = 1e-5
GN_EPS = 1e-3
XH = DIM // DH
PAIRS = BATCH // 2
FF = 1408
FC = FF // P
ABS_COLS = DIM * FF // P // (GROUPS * BATCH)
HALVES = (range(0, 2), range(2, 4))


def after(events):
    return events + 1


class Batch:

    def __init__(self, c, it=0):
        self.slot = c % 2
        self.half = it + c // 2
        self.index = 2 * it + c
        at = c if isinstance(it, int) else None
        self.first, self.second, self.last = (at == 0), (at == 1), (at == BATCH - 1)
        self.c, self.it = c, it

    def next(self):
        return Batch(self.c + 1, self.it)

    def prev(self):
        return Batch(self.c - 1, self.it)


def over_batches(eng, body):
    body(Batch(0))
    with eng.Fori(0, (BATCH - 2) // 2) as it:
        body(Batch(1, it))
        body(Batch(2, it))
    body(Batch(BATCH - 1))


def pick(tensor, n, count=1):
    if isinstance(n, int):
        return tensor[:, n, :] if count == 1 else tensor[:, n:n + count, :]
    found = tensor[:, bass.ds(n, count), :]
    return found.rearrange("p o n -> p (o n)") if count == 1 else found


def decoder_kernel(nc, t, out):
    with ExitStack() as ctx:
        def sb(name, shape, dt=F32, scope=ctx):
            return scope.enter_context(nc.sbuf_tensor(name, shape, dt))

        def sem(name):
            return ctx.enter_context(nc.semaphore(name))

        psum = ctx.enter_context(nc.psum_tensor("psum", [P, 8, 512], F32))
        bank = [psum[:, i, :] for i in range(8)]
        ps_q, ps_k, ps_v, ps_o, ps_s, ps_pt, ps_z = bank[:7]

        acc = sb("acc", [P, TILES, DIM])
        ident = sb("ident", [P, P])
        mask = sb("mask", [P, SEQ])
        bias_all = sb("bias_all", [P, GROUPS * 3 * GH])
        bias = sb("bias", [P, 3, GH])
        stats = [sb(f"stats{i}", [P, TILES, 2]) for i in range(2)]
        ones_f = sb("ones_f", [P, P])
        zeros = sb("zeros", [P, P])
        wsum = sb("wsum", [P, GROUPS * BATCH, 3])
        wtot = sb("wtot", [P, 3])
        thr = sb("thr", [P, 2, 3])
        bn_raw = sb("bn_raw", [P, 4, 6])
        bn = sb("bn", [P, 4, 2])
        variance = sb("variance", [P, 4, 1])
        rdev = sb("rdev", [P, 4, 1])
        power = sb("power", [P, 2, 1])

        phase_a = ExitStack()
        w_raw = sb("w_raw", [P, RING, 512], F32, phase_a)
        w_hi = sb("w_hi", [P, UNITS, 512], F32R, phase_a)
        w_lo = sb("w_lo", [P, UNITS, 512], F32R, phase_a)
        x_raw = sb("x_raw", [P, 2, CH * SEQ], F32, phase_a)
        x_hi = sb("x_hi", [P, 2, CH, SEQ], F32R, phase_a)
        x_lo = sb("x_lo", [P, 2, CH, SEQ], F32R, phase_a)
        q_hi = sb("q_hi", [P, SEQ], F32R, phase_a)
        q_lo = sb("q_lo", [P, SEQ], F32R, phase_a)
        k_hi = sb("k_hi", [P, SEQ], F32R, phase_a)
        k_lo = sb("k_lo", [P, SEQ], F32R, phase_a)
        v_hi = sb("v_hi", [P, 2, TPB, GH * DH], F32R, phase_a)
        v_lo = sb("v_lo", [P, 2, TPB, GH * DH], F32R, phase_a)
        z_hi = sb("z_hi", [P, 2, GH, SEQ], F32R, phase_a)
        z_lo = sb("z_lo", [P, 2, GH, SEQ], F32R, phase_a)
        probs = sb("probs", [P, KEYS], F32, phase_a)
        pt_hi = sb("pt_hi", [P, KEYS], F32R, phase_a)
        pt_lo = sb("pt_lo", [P, KEYS], F32R, phase_a)
        negmax = sb("negmax", [P, TPB], F32, phase_a)
        rowsum = sb("rowsum", [P, TPB], F32, phase_a)
        inv = sb("inv", [P, TPB], F32, phase_a)
        w_abs = sb("w_abs", [P, 2, 3 * ABS_COLS], F32, phase_a)
        phase_a.close()

        cross = ExitStack()
        ctx_raw = sb("ctx_raw", [P, 2, CH * SEQ], F32, cross)
        ctx_hi = sb("ctx_hi", [P, 2, CH, SEQ], F32R, cross)
        ctx_lo = sb("ctx_lo", [P, 2, CH, SEQ], F32R, cross)
        xn = sb("xn", [P, 2, TPB, DIM], F32, cross)
        xt_hi = sb("xt_hi", [P, 2, CH, SEQ], F32R, cross)
        xt_lo = sb("xt_lo", [P, 2, CH, SEQ], F32R, cross)
        a_hi = sb("a_hi", [P, XH, KEYS], F32R, cross)
        a_lo = sb("a_lo", [P, XH, KEYS], F32R, cross)
        ones_r = sb("ones_r", [P, P], F32R, cross)
        wh_hi = sb("wh_hi", [P, XH, DH], F32R, cross)
        wh_lo = sb("wh_lo", [P, XH, DH], F32R, cross)
        cross_1 = ExitStack()
        wx_raw = sb("wx_raw", [P, 2, XH * DH], F32, cross_1)
        decay = sb("decay", [P, XH, KEYS], F32, cross_1)
        a_raw = sb("a_raw", [P, XH, KEYS], F32, cross_1)
        bo_rows = sb("bo_rows", [P, DIM], F32, cross_1)
        g_hi = sb("g_hi", [P, XH, DH], F32R, cross_1)
        g_lo = sb("g_lo", [P, XH, DH], F32R, cross_1)
        xq_hi = sb("xq_hi", [P, 2, XH, SEQ], F32R, cross_1)
        xq_lo = sb("xq_lo", [P, 2, XH, SEQ], F32R, cross_1)
        cross_1.close()
        cross_2 = ExitStack()
        wgo_hi = sb("wgo_hi", [P, 2, CH, DIM], F32R, cross_2)
        wgo_lo = sb("wgo_lo", [P, 2, CH, DIM], F32R, cross_2)
        gamma = sb("gamma", [P, DIM], F32, cross_2)
        beta = sb("beta", [P, DIM], F32, cross_2)
        xv_hi = sb("xv_hi", [P, TPB, XH, 2, DH], F32R, cross_2)
        xv_lo = sb("xv_lo", [P, TPB, XH, 2, DH], F32R, cross_2)
        gate = sb("gate", [P, 4, DIM], F32, cross_2)
        wgo_raw = gate
        y_raw = sb("y_raw", [P, 2, DIM], F32, cross_2)
        wyt_hi = sb("wyt_hi", [P, 2, CH, P], F32R, cross_2)
        wyt_lo = sb("wyt_lo", [P, 2, CH, P], F32R, cross_2)
        cross_2.close()
        cross.close()

        ffn = ExitStack()
        f_raw = sb("f_raw", [P, RING, 512], F32, ffn)
        f_neg = sb("f_neg", [P, 2, 512], F32, ffn)
        f_w = sb("f_w", [P, 3 * FC, 512], F32R, ffn)
        xn2 = sb("xn2", [P, 2, TPB, DIM], F32, ffn)
        xt2_hi = sb("xt2_hi", [P, 2, CH, SEQ], F32R, ffn)
        xt2_lo = sb("xt2_lo", [P, 2, CH, SEQ], F32R, ffn)
        sig = sb("sig", [P, 2, 512], F32, ffn)
        hid = sb("hid", [P, 2, 512], F32, ffn)
        hid_hi = sb("hid_hi", [P, 2, 512], F32R, ffn)
        hid_lo = sb("hid_lo", [P, 2, 512], F32R, ffn)
        y3 = sb("y3", [P, 4, DIM], F32, ffn)
        ffn.close()

        def unit_qk(kind, h):
            return kind if h == 0 else 6 + 2 * (h - 1) + kind

        UNIT_V, UNIT_O = 2, 12

        s_const = sem("s_const")
        s_wdma = [sem(f"s_wdma{i}") for i in range(RING)]
        s_xdma = [sem(f"s_xdma{i}") for i in range(2)]
        s_accin = [sem(f"s_accin{i}") for i in range(2)]
        progress = (s_bias, s_whi, s_wlo, s_x, s_q, s_k, s_v, s_o, s_scores, s_pt, s_z,
         s_qhi, s_khi, s_vhi, s_exp, s_pthi, s_zhi,
         s_max, s_qlo, s_klo, s_vlo, s_inv, s_norm, s_ptlo, s_zlo, s_acc, s_xhi) = tuple(
            sem(n) for n in
            "s_bias s_whi s_wlo s_x s_q s_k s_v s_o s_scores s_pt s_z "
            "s_qhi s_khi s_vhi s_exp s_pthi s_zhi "
            "s_max s_qlo s_klo s_vlo s_inv s_norm s_ptlo s_zlo s_acc s_xhi".split())
        s_out = sem("s_out")
        s_ctxdma = [sem(f"s_ctxdma{i}") for i in range(2)]
        s_const2, s_gdma, s_odma = (sem(n) for n in "s_const2 s_gdma s_odma".split())
        s_absdma = [sem(f"s_absdma{i}") for i in range(2)]
        s_fdma = [sem(f"s_fdma{i}") for i in range(RING)]
        names = ("s_bo s_bn s_aggr s_var s_rdev s_mean s_xn s_xt s_xthi s_xtlo s_ctxhi s_ctxlo s_xq s_xqhi s_xqlo s_xs "
                 "s_g s_ghi s_glo s_whsplit s_wh s_araw s_ahi s_alo s_back s_xv s_xvhi s_xvlo s_xo s_gate s_relu "
                 "s_yc s_ys s_wy s_wyt s_wythi s_wytlo s_xout s_res s_gohi s_golo s_abs s_ones "
                 "s_tot s_totps s_thr s_neg s_fw s_up s_sig s_hid s_hhi s_hlo s_down s_y3 s_y3n s_yout").split()
        (s_bo, s_bn, s_aggr, s_var, s_rdev, s_mean, s_xn, s_xt, s_xthi, s_xtlo, s_ctxhi, s_ctxlo, s_xq, s_xqhi, s_xqlo, s_xs,
         s_g, s_ghi, s_glo, s_whsplit, s_wh, s_araw, s_ahi, s_alo, s_back, s_xv, s_xvhi, s_xvlo, s_xo, s_gate,
         s_relu, s_yc, s_ys, s_wy, s_wyt, s_wythi, s_wytlo, s_xout, s_res, s_gohi, s_golo, s_abs, s_ones,
         s_tot, s_totps, s_thr, s_neg, s_fw, s_up, s_sig, s_hid, s_hhi, s_hlo, s_down, s_y3, s_y3n,
         s_yout) = later = tuple(sem(n) for n in names)

        block = ctx.enter_context(nc.Block())

        @block.sync
        def _(sp):
            for dst, src in ((bias_all, "biases"), (ident, "identity"), (mask, "causal")):
                sp.dma_start(dst[:, :], t[src]).then_inc(s_const, 16)

            def group(hg, first):
                def load_w(u):
                    if not (first and u < RING):
                        sp.wait_ge(s_wlo, after(hg * UNITS + u - RING + 1))
                    sp.dma_start(w_raw[:, u % RING, :], t["w_attn"][hg * UNITS + u, :, :] if first else
                                 t["w_attn"][bass.ds(hg * UNITS + u, 1), :, :].rearrange("o p n -> (o p) n")
                                 ).then_inc(s_wdma[u % RING], 16)

                def load_x(b):
                    if not (first and (b.first or b.second)):
                        sp.wait_ge(s_x, after(hg * BATCH + b.index - 1))
                    src = t["xT"][b.index, :, :] if isinstance(b.index, int) else \
                        t["xT"][bass.ds(b.index, 1), :, :].rearrange("o p n -> (o p) n")
                    sp.dma_start(x_raw[:, b.slot, :], src).then_inc(s_xdma[b.slot], 16)
                    if not (first and (b.first or b.second)):
                        sp.wait_ge(s_abs, after(hg * BATCH + b.index - 1))
                    sp.dma_start(w_abs[:, b.slot, :], pick(t["w_abs"].rearrange("b p n -> p b n"),
                                                           hg * BATCH + b.index)).then_inc(s_absdma[b.slot], 16)
                    if first:
                        if not (b.first or b.second):
                            sp.wait_ge(s_accin[b.slot], 16 * b.half)
                        if isinstance(b.index, int):
                            a, s = acc[:, 2 * b.index:2 * b.index + 2, :], t["x"][:, 2 * b.index:2 * b.index + 2, :]
                        else:
                            a, s = acc[:, bass.ds(2 * b.index, 2), :], t["x"][:, bass.ds(2 * b.index, 2), :]
                        sp.dma_start(a, s).then_inc(s_accin[b.slot], 16)

                for u in range(2):
                    load_w(u)
                load_x(Batch(0))
                for u in range(2, UNITS):
                    load_w(u)
                    if u == 9:
                        load_x(Batch(1))
                with sp.Fori(0, (BATCH - 2) // 2) as it:
                    load_x(Batch(2, it))
                    load_x(Batch(3, it))

            group(0, True)
            with sp.Fori(1, GROUPS) as hg:
                group(hg, False)

            sp.wait_ge(s_acc, after(GROUPS * TILES))
            for dst, src in ((wx_raw, "w_head"), (decay, "decay")):
                sp.dma_start(dst[:, :, :], t[src]).then_inc(s_const2, 16)
            sp.dma_start(bo_rows[:, :], t["b_o"]).then_inc(s_const2, 16)

            def load_ctx(n, b):
                if not isinstance(n, int) or n >= 2:
                    sp.wait_ge(s_ctxlo, after(n - 1))
                sp.dma_start(ctx_raw[:, b.slot, :], pick(t["ctxT"].rearrange("b p n -> p b n"), b.index)
                             ).then_inc(s_ctxdma[b.slot], 16)

            over_batches(sp, lambda b: load_ctx(b.index, b))
            load_ctx(BATCH, Batch(0))
            load_ctx(BATCH + 1, Batch(1))
            sp.wait_ge(s_xs, after(BATCH))
            sp.wait_ge(s_alo, after(1))
            for dst, src in ((gamma, "gamma"), (beta, "beta")):
                sp.dma_start(dst[:, :], t[src]).then_inc(s_gdma, 16)
            sp.dma_start(wgo_raw[:, :, :], t["w_gate"]).then_inc(s_gdma, 16)

            sp.wait_ge(s_golo, after(1))
            sp.dma_start(wgo_raw[:, :, :], t["w_out"]).then_inc(s_odma, 16)
            with sp.Fori(0, PAIRS - 1) as p:
                load_ctx(2 * p + BATCH + 2, Batch(2, p))
                load_ctx(2 * p + BATCH + 3, Batch(3, p))

            sp.wait_ge(s_res, after(TILES))
            for u in range(3 * FC):
                if u >= RING:
                    sp.wait_ge(s_fw, after(u - RING + 1))
                sp.dma_start(f_raw[:, u % RING, :], t["w_ffn"][u, :, :]).then_inc(s_fdma[u % RING], 16)

            def store(p):
                for k in range(4):
                    sp.wait_ge(s_y3n, after(4 * p + k + 1))
                    sp.dma_start(pick(out, 4 * p + k), y3[:, k, :]).then_inc(s_yout, 16)

            with sp.Fori(0, PAIRS) as p:
                store(p)
            sp.wait_ge(s_yout, after(16 * TILES))

        @block.gpsimd
        def _(pool):
            for s in progress + later:
                pool.sem_inc(s, 1)

            def split_x(hg, b):
                pool.wait_ge(s_xdma[b.slot], (hg * (BATCH // 2) + b.half + 1) * 16)
                pool.wait_ge(s_k, after(hg * STEPS + (0 if b.first else GH * (b.index - 1))))
                hi = x_hi[:, b.slot, :, :].rearrange("p c n -> p (c n)")
                pool.nop(nofuse=True)
                nc.gpsimd.tensor_copy(hi, x_raw[:, b.slot, :]).then_inc(s_xhi, 1)
                pool.wait_ge(s_xhi, after(hg * BATCH + b.index + 1))
                nc.gpsimd.tensor_tensor(out=x_lo[:, b.slot, :, :].rearrange("p c n -> p (c n)"),
                                        in0=x_raw[:, b.slot, :], in1=hi.bitcast(F32),
                                        op=ALU.subtract).then_inc(s_x, 1)

            with pool.Fori(0, GROUPS) as hg:
                over_batches(pool, lambda b: split_x(hg, b))

            nc.gpsimd.memset(ones_f[:, :], 1.0).then_inc(s_ones, 1)
            nc.gpsimd.memset(power[:, :, :], -0.5).then_inc(s_ones, 1)
            nc.gpsimd.memset(zeros[:, :], 0.0).then_inc(s_ones, 1)
            pool.wait_ge(s_acc, after(GROUPS * TILES))
            nc.gpsimd.memset(ones_r[:, :].bitcast(F32), 1.0).then_inc(s_ones, 1)
            pool.wait_ge(s_const2, 48)

            def inverse_root(n, k, count, out_ap):
                pool.wait_ge(s_var, after(n + 1))
                nc.gpsimd.tensor_tensor(out=out_ap, in0=variance[:, k:k + count, :], in1=power[:, 0:count, :],
                                        op=ALU.pow).then_inc(s_rdev, 1)

            def stat_column(which, tile, count, column):
                st = stats[which][:, tile:tile + count, :] if isinstance(tile, int) else \
                    stats[which][:, bass.ds(tile, count), :]
                return st[:, :, column:column + 1]

            def ctx_split(n, b):
                pool.wait_ge(s_ctxhi, after(n + 1))
                nc.gpsimd.tensor_tensor(out=ctx_lo[:, b.slot, :, :].rearrange("p c n -> p (c n)"),
                                        in0=ctx_raw[:, b.slot, :],
                                        in1=ctx_hi[:, b.slot, :, :].rearrange("p c n -> p (c n)").bitcast(F32),
                                        op=ALU.subtract).then_inc(s_ctxlo, 1)

            pool.wait_ge(s_ones, after(2))

            def add_bo(b):
                for tt in range(TPB):
                    a = pick(acc, TPB * b.index + tt)
                    nc.gpsimd.tensor_tensor(out=a, in0=a, in1=bo_rows[:, :], op=ALU.add).then_inc(s_bo, 1)

            def inverse_1(b):
                inverse_root(b.index, 0, TPB, stat_column(0, TPB * b.index, TPB, 1))

            add_bo(Batch(0))
            inverse_1(Batch(0))

            def pass_1(b):
                if not b.last:
                    add_bo(b.next())
                ctx_split(b.index, b)
                if not b.last:
                    inverse_1(b.next())

            over_batches(pool, pass_1)
            ctx_split(BATCH, Batch(0))
            ctx_split(BATCH + 1, Batch(1))

            def pass_2(p, more):
                n = BATCH + 8 * p
                for k in range(4):
                    inverse_root(n + k, 2 + k % 2, 1, rdev[:, k % 2:k % 2 + 1, :])
                    if more and k < 2:
                        ctx_split(2 * p + BATCH + 2 + k, Batch(2 + k, p))
                for k in range(4):
                    inverse_root(n + 4 + k, k % 2, 1, stat_column(1, 4 * p + k, 1, 1))

            with pool.Fori(0, PAIRS - 1) as p:
                pass_2(p, True)
            pass_2(PAIRS - 1, False)

            with pool.Fori(0, PAIRS) as p:
                for k in range(0, 4, 2):
                    inverse_root(BATCH + 2 * TILES + 2 * p + k // 2, k, 2, rdev[:, k:k + 2, :])

        @block.tensor
        def _(pe):
            def mm3(out_ap, left, right, first, last):
                (lh, ll), (rh, rl) = left, right
                pe.matmul(out_ap, lh, rh, start=first, stop=False, skip_group_check=True)
                pe.matmul(out_ap, lh, rl, start=False, stop=False, skip_group_check=True)
                return pe.matmul(out_ap, ll, rh, start=False, stop=last, skip_group_check=True)

            def project(ps, kind, h, b, done):
                u = unit_qk(kind, h)
                for c in range(CH):
                    w = [x[:, u, c * DH:(c + 1) * DH] for x in (w_hi, w_lo)]
                    x = [x[:, b.slot, c, :] for x in (x_hi, x_lo)]
                    mm = mm3(ps[:, 0:SEQ], w, x, c == 0, c == CH - 1)
                mm.then_inc(done, 1)

            def queries_keys(hg, b, h, part):
                n = hg * STEPS + GH * b.index + h
                if b.first:
                    pe.wait_ge(s_wlo, after(hg * UNITS + unit_qk(part, h) + 1))
                pe.wait_ge(s_x, after(hg * BATCH + b.index + 1))
                pe.wait_ge(s_klo if part else s_qlo, after(n))
                project(ps_k if part else ps_q, part, h, b, s_k if part else s_q)

            def values(hg, b, tt, part):
                n = hg * TILES + TPB * b.index + tt
                if part == 0 and b.first:
                    pe.wait_ge(s_wlo, after(hg * UNITS + UNIT_V + CH))
                if part == 0:
                    pe.wait_ge(s_x, after(hg * BATCH + b.index + 1))
                    pe.wait_ge(s_vlo, after(n))
                for c in HALVES[part]:
                    x = [x[:, b.slot, c, tt * P:(tt + 1) * P] for x in (x_hi, x_lo)]
                    w = [w[:, UNIT_V + c, :] for w in (w_hi, w_lo)]
                    mm = mm3(ps_v[:, :], x, w, c == 0, c == CH - 1)
                if part == 1:
                    mm.then_inc(s_v, 1)

            def scores(hg, b, h):
                n = hg * STEPS + GH * b.index + h
                pe.wait_ge(s_qlo, after(n + 1))
                pe.wait_ge(s_klo, after(n + 1))
                pe.wait_ge(s_exp, after(n))
                for qt in range(TPB):
                    q = [x[:, qt * P:(qt + 1) * P] for x in (q_hi, q_lo)]
                    k = [x[:, 0:(qt + 1) * P] for x in (k_hi, k_lo)]
                    mm = mm3(ps_s[:, qt * P:qt * P + (qt + 1) * P], q, k, qt == 0, qt == TPB - 1)
                mm.then_inc(s_scores, 1)

            def transposes(hg, b, h):
                n = hg * STEPS + GH * b.index + h
                pe.wait_ge(s_norm, after(n + 1))
                pe.wait_ge(s_ptlo, after(n))
                for i in range(KEYS // P):
                    mm = pe.transpose(ps_pt[:, i * P:(i + 1) * P], probs[:, i * P:(i + 1) * P], ident[:, :])
                mm.then_inc(s_pt, 1)

            def mix(hg, b, h):
                n = hg * STEPS + GH * b.index + h
                pe.wait_ge(s_ptlo, after(n + 1))
                pe.wait_ge(s_vlo, after(hg * TILES + TPB * b.index + TPB))
                pe.wait_ge(s_zlo, after(n))
                for kt in range(TPB):
                    v = [x[:, b.slot, kt, h * DH:(h + 1) * DH] for x in (v_hi, v_lo)]
                    p = [x[:, 0:SEQ] if kt == 0 else x[:, SEQ:KEYS] for x in (pt_hi, pt_lo)]
                    mm = mm3(ps_z[:, kt * P:SEQ], v, p, kt == 0, kt == TPB - 1)
                mm.then_inc(s_z, 1)

            def outputs(hg, b, tt, part):
                if part == 0:
                    if b.first:
                        pe.wait_ge(s_wlo, after(hg * UNITS + UNIT_O + GH))
                    pe.wait_ge(s_zlo, after(hg * STEPS + GH * b.index + GH))
                    pe.wait_ge(s_acc, after(hg * TILES + TPB * b.index + tt))
                for h in HALVES[part]:
                    z = [x[:, b.slot, h, tt * P:(tt + 1) * P] for x in (z_hi, z_lo)]
                    w = [x[:, UNIT_O + h, :] for x in (w_hi, w_lo)]
                    mm = mm3(ps_o[:, :], z, w, h == 0, h == GH - 1)
                if part == 1:
                    mm.then_inc(s_o, 1)

            with pe.Fori(0, GROUPS) as hg:
                queries_keys(hg, Batch(0), 0, 0)
                queries_keys(hg, Batch(0), 0, 1)
                for tt in range(TPB):
                    values(hg, Batch(0), tt, 0)
                    values(hg, Batch(0), tt, 1)

                def body(b):
                    for h in range(GH):
                        scores(hg, b, h)
                        nb, nh = (b, h + 1) if h + 1 < GH else (b.next(), 0)
                        more = not (b.last and h + 1 == GH)
                        if more:
                            queries_keys(hg, nb, nh, 0)
                            queries_keys(hg, nb, nh, 1)
                        for part in range(2):
                            if h < TPB and not b.first:
                                outputs(hg, b.prev(), h, part)
                            if h >= TPB and not b.last:
                                values(hg, b.next(), h - TPB, part)
                            if part == 0:
                                transposes(hg, b, h)
                        mix(hg, b, h)

                over_batches(pe, body)
                for tt in range(TPB):
                    outputs(hg, Batch(BATCH - 1), tt, 0)
                    outputs(hg, Batch(BATCH - 1), tt, 1)

            def transpose_rows(rows, slot, base):
                for c in range(CH):
                    for tt in range(TPB):
                        mm = pe.transpose(bank[base + c // 2][:, c % 2 * SEQ + tt * P:c % 2 * SEQ + (tt + 1) * P],
                                          rows[:, slot, tt, c * P:(c + 1) * P], ident[:, :])
                mm.then_inc(s_xt, 1)

            pe.wait_ge(s_acc, after(GROUPS * TILES))
            pe.wait_ge(s_const2, 48)
            for h in range(XH):
                w = wx_raw[:, 1, h * DH:(h + 1) * DH]
                mm = pe.matmul(bank[2][:, h * DH:(h + 1) * DH], w, w, start=True, stop=True, skip_group_check=True)
            mm.then_inc(s_g, 1)

            def cross_rows(b):
                pe.wait_ge(s_xn, after(b.index + 1))
                pe.wait_ge(s_xtlo, after(b.index))
                transpose_rows(xn, b.slot, 0)

            def cross_queries(b):
                pe.wait_ge(s_xtlo, after(b.index + 1))
                pe.wait_ge(s_xqlo, after(b.index))
                for h in range(XH):
                    g = [x[:, h, :] for x in (g_hi, g_lo)]
                    x = [x[:, 0, h, :] for x in (xt_hi, xt_lo)]
                    mm = mm3(bank[2 + h // 2][:, h % 2 * SEQ:(h % 2 + 1) * SEQ], g, x, True, True)
                mm.then_inc(s_xq, 1)

            def cross_scores(b):
                pe.wait_ge(s_xqlo, after(b.index + 1))
                pe.wait_ge(s_ctxlo, after(b.index + 1))
                for h in range(XH):
                    for kt in range(TPB):
                        c = [x[:, b.slot, h, kt * P:(kt + 1) * P] for x in (ctx_hi, ctx_lo)]
                        q = [x[:, b.slot, h, kt * P:SEQ] for x in (xq_hi, xq_lo)]
                        mm = mm3(bank[4 + h][:, kt * SEQ:kt * SEQ + SEQ - kt * P], c, q, False, b.last)
                mm.then_inc(s_xs, 1)

            cross_rows(Batch(0))
            pe.wait_ge(s_ones, after(3))
            for h in range(XH):
                pe.matmul(bank[4 + h][:, 0:KEYS], zeros[:, :], decay[:, h, :], start=True, stop=False,
                          skip_group_check=True)
            pe.wait_ge(s_glo, after(1))

            def pass_1(b):
                cross_queries(b)
                if not b.last:
                    cross_rows(b.next())
                if not b.first:
                    cross_scores(b.prev())

            over_batches(pe, pass_1)
            cross_scores(Batch(BATCH - 1))

            def cross_values(p, j, tt):
                pe.wait_ge(s_ctxlo, after(2 * p + BATCH + j + 1))
                for h in range(XH):
                    c = [x[:, j, h, tt * P:(tt + 1) * P] for x in (ctx_hi, ctx_lo)]
                    w = [x[:, h, :] for x in (wh_hi, wh_lo)]
                    mm = mm3(bank[2 + tt][:, h * DH:(h + 1) * DH], c, w, True, True)
                mm.then_inc(s_xv, 1)

            def rows_2(p, j):
                pe.wait_ge(s_xn, after(2 * p + BATCH + j + 1))
                transpose_rows(xn, j, 2)

            def cross_mix(p, st):
                for h in range(XH):
                    ps = bank[4 + 2 * st + h // 2][:, h % 2 * 2 * DH:(h % 2 + 1) * 2 * DH]
                    v = [x[:, :, h, :, :].rearrange("p t j e -> p t (j e)") for x in (xv_hi, xv_lo)]
                    a = [x[:, h, st * P:(st + 1) * P] for x in (a_hi, a_lo)]
                    mm3(ps, a, [x[:, 0, :] for x in v], True, False)
                    if st == 1:
                        a = [x[:, h, SEQ:KEYS] for x in (a_hi, a_lo)]
                        mm = mm3(ps, a, [x[:, 1, :] for x in v], False, True)
                    else:
                        pe.matmul(ps, ones_r[:, :], v[0][:, 1, :], start=False, stop=False, skip_group_check=True)
                        mm = pe.matmul(ps, ones_r[:, :], v[1][:, 1, :], start=False, stop=True,
                                       skip_group_check=True)
                mm.then_inc(s_xo, 1)

            def gate_rows(p, k):
                pe.wait_ge(s_xtlo, after(2 * p + BATCH + k // 2 + 1))
                pe.wait_ge(s_relu, after(4 * p + k))
                for c in range(CH):
                    x = [x[:, k // 2, c, k % 2 * P:(k % 2 + 1) * P] for x in (xt_hi, xt_lo)]
                    mm = mm3(bank[0], x, [x[:, 0, c, :] for x in (wgo_hi, wgo_lo)], c == 0, c == CH - 1)
                mm.then_inc(s_gate, 1)

            def turn_wy(p, k):
                pe.wait_ge(s_wy, after(4 * p + k + 1))
                for c in range(CH):
                    mm = pe.transpose(bank[2 + k % 2][:, c * P:(c + 1) * P], gate[:, k, c * P:(c + 1) * P],
                                      ident[:, :])
                mm.then_inc(s_wyt, 1)

            def cross_output(p, k):
                pe.wait_ge(s_wytlo, after(4 * p + k + 1))
                pe.wait_ge(s_res, after(4 * p + k))
                for c in range(CH):
                    mm = mm3(bank[1], [x[:, k % 2, c, :] for x in (wyt_hi, wyt_lo)],
                             [x[:, 1, c, :] for x in (wgo_hi, wgo_lo)], c == 0, c == CH - 1)
                mm.then_inc(s_xout, 1)

            pe.wait_ge(s_wh, after(1))
            cross_values(0, 0, 0)
            cross_values(0, 0, 1)
            pe.wait_ge(s_xvlo, after(2))
            rows_2(0, 0)
            pe.wait_ge(s_xtlo, after(BATCH + 1))
            cross_values(0, 1, 0)
            cross_values(0, 1, 1)
            pe.wait_ge(s_xvlo, after(4))
            rows_2(0, 1)
            pe.wait_ge(s_alo, after(1))
            pe.wait_ge(s_golo, after(1))

            def pass_2(p, more):
                pe.wait_ge(s_xvlo, after(4 * p + 4))
                pe.wait_ge(s_yc, after(4 * p))
                cross_mix(p, 0)
                cross_mix(p, 1)
                gate_rows(p, 0)
                pe.wait_ge(s_xtlo, after(2 * p + BATCH + 2))
                if more:
                    cross_values(p + 1, 0, 0)
                    cross_values(p + 1, 0, 1)
                gate_rows(p, 1)
                if more:
                    pe.wait_ge(s_xvlo, after(4 * p + 6))
                    rows_2(p + 1, 0)
                gate_rows(p, 2)
                if more:
                    pe.wait_ge(s_xtlo, after(2 * p + BATCH + 3))
                    cross_values(p + 1, 1, 0)
                    cross_values(p + 1, 1, 1)
                gate_rows(p, 3)
                if more:
                    pe.wait_ge(s_xvlo, after(4 * p + 8))
                turn_wy(p, 0)
                turn_wy(p, 1)
                pe.wait_ge(s_golo, after(2))
                cross_output(p, 0)
                turn_wy(p, 2)
                cross_output(p, 1)
                turn_wy(p, 3)
                cross_output(p, 2)
                if more:
                    pe.wait_ge(s_wytlo, after(4 * p + 4))
                    rows_2(p + 1, 1)
                cross_output(p, 3)

            with pe.Fori(0, PAIRS - 1) as p:
                pass_2(p, True)
            pass_2(PAIRS - 1, False)

            pe.wait_ge(s_tot, after(1))
            pe.wait_ge(s_res, after(TILES))
            pe.matmul(bank[4][:, 0:3], ones_f[:, :], wtot[:, :], start=True, stop=True).then_inc(s_totps, 1)

            def rows_3(p, j):
                pe.wait_ge(s_xn, after(2 * p + 2 * BATCH + j + 1))
                transpose_rows(xn2, j, 2 - 2 * j)

            def up(p, f, first):
                if first:
                    pe.wait_ge(s_fw, after(3 * f + 2))
                if f >= 2:
                    pe.wait_ge(s_hid, after(FC * p + f - 1))
                else:
                    pe.wait_ge(s_xtlo, after(2 * p + 2 * BATCH + 2))
                for m in range(2):
                    for c in range(CH):
                        w = f_w[:, 3 * f + m, c * P:(c + 1) * P]
                        for i, x in enumerate((xt2_hi, xt2_lo)):
                            mm = pe.matmul(bank[f % 2 * 2 + m].rearrange("p (j n) -> p j n", j=2), w, x[:, :, c, :],
                                           start=(c == 0 and i == 0), stop=(c == CH - 1 and i == 1),
                                           skip_group_check=True)
                mm.then_inc(s_up, 1)

            def down(p, f, first):
                if first:
                    pe.wait_ge(s_fw, after(3 * f + 3))
                pe.wait_ge(s_hlo, after(FC * p + f + 1))
                if f == 0:
                    pe.wait_ge(s_y3, after(4 * p))
                for k in range(4):
                    for i, x in enumerate((hid_hi, hid_lo)):
                        mm = pe.matmul(bank[4 + k], x[:, f % 2, k * P:(k + 1) * P], f_w[:, 3 * f + 2, :],
                                       start=(f == 0 and i == 0), stop=(f == FC - 1 and i == 1),
                                       skip_group_check=True)
                mm.then_inc(s_down, 1)

            rows_3(0, 0)
            rows_3(0, 1)
            pe.wait_ge(s_thr, after(1))

            def pass_3(p, first, more):
                for f in range(FC):
                    up(p, f, first)
                    if more and f == FC - 1:
                        pe.wait_ge(s_hid, after(FC * p + FC - 1))
                        rows_3(p + 1, 0)
                    if f >= 1:
                        down(p, f - 1, first)
                if more:
                    pe.wait_ge(s_hid, after(FC * p + FC))
                    rows_3(p + 1, 1)
                down(p, FC - 1, first)

            pass_3(0, True, True)
            with pe.Fori(1, PAIRS - 1) as p:
                pass_3(p, False, True)
            pass_3(PAIRS - 1, False, False)

        SCALE = float(DH) ** -0.5

        @block.scalar
        def _(act):
            def split_w(hg, u):
                act.wait_ge(s_wdma[u % RING], (hg * (UNITS // RING) + u // RING + 1) * 16)
                act.wait_ge(s_k, after(hg * STEPS))
                if u >= UNIT_O:
                    act.wait_ge(s_o, after(hg * TILES))
                nc.scalar.copy(w_hi[:, u, :], w_raw[:, u % RING, :]).then_inc(s_whi, 1)

            def qk_hi(hg, b, h, part):
                n = hg * STEPS + GH * b.index + h
                act.wait_ge(s_k if part else s_q, after(n + 1))
                act.wait_ge(s_scores, after(n))
                nc.scalar.activation((k_hi if part else q_hi)[:, :], (ps_k if part else ps_q)[:, 0:SEQ],
                                     ACT.Identity, bias=bias[:, part, h:h + 1]
                                     ).then_inc(s_khi if part else s_qhi, 1)

            def v_split(hg, b, tt):
                act.wait_ge(s_v, after(hg * TILES + TPB * b.index + tt + 1))
                act.wait_ge(s_z, after(hg * STEPS + (0 if b.first else GH * (b.index - 1))))
                nc.scalar.copy(v_hi[:, b.slot, tt, :], ps_v[:, :]).then_inc(s_vhi, 1)

            def exps(hg, b, h):
                n = hg * STEPS + GH * b.index + h
                act.wait_ge(s_max, after(TPB * (n + 1)))
                act.wait_ge(s_pt, after(n))
                nc.scalar.activation(probs[:, 0:P], ps_s[:, 0:P], ACT.Exp, bias=negmax[:, 0:1], scale=-1.0,
                                     accum_out=rowsum[:, 0:1])
                nc.scalar.activation(probs[:, P:KEYS], ps_s[:, P:KEYS], ACT.Exp, bias=negmax[:, 1:2],
                                     scale=-1.0, accum_out=rowsum[:, 1:2]).then_inc(s_exp, 1)

            def pt_split(hg, b, h):
                n = hg * STEPS + GH * b.index + h
                act.wait_ge(s_pt, after(n + 1))
                act.wait_ge(s_z, after(n))
                nc.scalar.copy(pt_hi[:, :], ps_pt[:, 0:KEYS]).then_inc(s_pthi, 1)

            def z_split(hg, b, h):
                n = hg * STEPS + GH * b.index + h
                act.wait_ge(s_z, after(n + 1))
                act.wait_ge(s_o, after(hg * TILES + (0 if b.first else TPB * (b.index - 1))))
                nc.scalar.activation(z_hi[:, b.slot, h, :], ps_z[:, 0:SEQ], ACT.Identity,
                                     bias=bias[:, 2, h:h + 1]).then_inc(s_zhi, 1)

            def sum_abs(hg, b):
                n = hg * BATCH + b.index
                act.wait_ge(s_absdma[b.slot], (hg * PAIRS + b.half + 1) * 16)
                for m in range(3):
                    piece = w_abs[:, b.slot, m * ABS_COLS:(m + 1) * ABS_COLS]
                    mm = nc.scalar.activation(piece, piece, ACT.Abs, accum_out=pick(wsum, n)[:, m:m + 1])
                mm.then_inc(s_abs, 1)

            with act.Fori(0, GROUPS) as hg:
                act.wait_ge(s_bias, after(hg + 1))
                for u in range(6):
                    split_w(hg, u)
                qk_hi(hg, Batch(0), 0, 0)
                qk_hi(hg, Batch(0), 0, 1)
                for tt in range(TPB):
                    v_split(hg, Batch(0), tt)
                split_w(hg, 6)
                split_w(hg, 7)

                def body(b):
                    for h in range(GH):
                        exps(hg, b, h)
                        if b.first:
                            split_w(hg, 8 + 2 * h)
                            split_w(hg, 9 + 2 * h)
                        if not (b.last and h + 1 == GH):
                            nb, nh = (b, h + 1) if h + 1 < GH else (b.next(), 0)
                            qk_hi(hg, nb, nh, 0)
                            qk_hi(hg, nb, nh, 1)
                        pt_split(hg, b, h)
                        if h >= TPB and not b.last:
                            v_split(hg, b.next(), h - TPB)
                        z_split(hg, b, h)
                        if h == 0:
                            sum_abs(hg, b)

                over_batches(act, body)

            act.wait_ge(s_acc, after(GROUPS * TILES))
            act.wait_ge(s_const2, 48)

            def ctx_split(n, b):
                act.wait_ge(s_ctxdma[b.slot], (n // 2 + 1) * 16 if isinstance(n, int) else
                            (b.half + 1) * 16 if n is b.index else (b.half + 1 + PAIRS) * 16)
                nc.scalar.copy(ctx_hi[:, b.slot, :, :].rearrange("p c n -> p (c n)"), ctx_raw[:, b.slot, :]
                               ).then_inc(s_ctxhi, 1)

            def split_banks(hi, base, done):
                nc.scalar.copy(hi, psum[:, base:base + 2, :]).then_inc(done, 1)

            def xt_split(n, slot, base):
                act.wait_ge(s_xt, after(n + 1))
                split_banks(xt_hi[:, slot, :, :].rearrange("p (a c) n -> p a (c n)", a=2), base, s_xthi)

            def xq_split(b):
                act.wait_ge(s_xq, after(b.index + 1))
                if not (b.first or b.second):
                    act.wait_ge(s_xs, after(b.index - 1))
                split_banks(xq_hi[:, b.slot, :, :].rearrange("p (a h) n -> p a (h n)", a=2), 2, s_xqhi)

            act.wait_ge(s_g, after(1))
            nc.scalar.copy(g_hi[:, :, :].rearrange("p h e -> p (h e)"), bank[2]).then_inc(s_ghi, 1)
            nc.scalar.copy(wh_hi[:, :, :].rearrange("p h e -> p (h e)"), wx_raw[:, 0, :]).then_inc(s_whsplit, 1)
            ctx_split(0, Batch(0))
            xt_split(0, 0, 0)

            def pass_1(b):
                xq_split(b)
                if not b.last:
                    nb = b.next()
                    xt_split(nb.index, 0, 0)
                    if not (nb.first or nb.second):
                        act.wait_ge(s_xs, after(nb.index - 1))
                    ctx_split(nb.index, nb)

            over_batches(act, pass_1)
            act.wait_ge(s_xs, after(BATCH))
            for j in range(2):
                ctx_split(BATCH + j, Batch(j))
            act.wait_ge(s_araw, after(3))
            nc.scalar.copy(a_hi[:, :, :], a_raw[:, :, :]).then_inc(s_ahi, 1)

            def xv_split(p, j, tt):
                act.wait_ge(s_xv, after(4 * p + 2 * j + tt + 1))
                act.wait_ge(s_xo, after(2 * p))
                nc.scalar.copy(xv_hi[:, tt, :, j, :], bank[2 + tt].rearrange("p (h e) -> p h e", h=XH)
                               ).then_inc(s_xvhi, 1)

            def keep_rows(n, rows, j, p):
                act.wait_ge(s_xn, after(n + 1))
                nc.scalar.copy(pick(acc, 4 * p + 2 * j, TPB), rows[:, j, :, :]).then_inc(s_back, 1)

            def relu(p, k):
                act.wait_ge(s_gate, after(4 * p + k + 1))
                act.wait_ge(s_wyt, after(4 * p))
                act.wait_ge(s_golo, after(2))
                nc.scalar.activation(gate[:, k, :], bank[0], ACT.Relu).then_inc(s_relu, 1)

            def wyt_split(p, k):
                act.wait_ge(s_wyt, after(4 * p + k + 1))
                act.wait_ge(s_xout, after(4 * p + k - 1) if k else after(4 * p))
                nc.scalar.copy(wyt_hi[:, k % 2, :, :].rearrange("p c n -> p (c n)"), bank[2 + k % 2]
                               ).then_inc(s_wythi, 1)

            for tt in range(TPB):
                xv_split(0, 0, tt)
            xt_split(BATCH, 0, 2)
            keep_rows(BATCH, xn, 0, 0)
            for tt in range(TPB):
                xv_split(0, 1, tt)
            act.wait_ge(s_gdma, 48)
            nc.scalar.copy(wgo_hi[:, 0, :, :], wgo_raw[:, :, :]).then_inc(s_gohi, 1)
            xt_split(BATCH + 1, 1, 2)
            keep_rows(BATCH + 1, xn, 1, 0)
            act.wait_ge(s_odma, 16)
            nc.scalar.copy(wgo_hi[:, 1, :, :], wgo_raw[:, :, :]).then_inc(s_gohi, 1)

            def pass_2(p, more):
                if more:
                    for j in range(2):
                        act.wait_ge(s_xv, after(4 * p + 2 * j + 2))
                        ctx_split(2 * p + BATCH + 2 + j, Batch(2 + j, p))
                relu(p, 0)
                if more:
                    xv_split(p + 1, 0, 0)
                    xv_split(p + 1, 0, 1)
                relu(p, 1)
                if more:
                    xt_split(2 * p + BATCH + 2, 0, 2)
                    keep_rows(2 * p + BATCH + 2, xn, 0, p + 1)
                relu(p, 2)
                if more:
                    xv_split(p + 1, 1, 0)
                    xv_split(p + 1, 1, 1)
                relu(p, 3)
                for k in range(4):
                    wyt_split(p, k)
                if more:
                    xt_split(2 * p + BATCH + 3, 1, 2)
                    keep_rows(2 * p + BATCH + 3, xn, 1, p + 1)

            with act.Fori(0, PAIRS - 1) as p:
                pass_2(p, True)
            pass_2(PAIRS - 1, False)

            def xt2_split(p, j):
                act.wait_ge(s_xt, after(2 * p + 2 * BATCH + j + 1))
                split_banks(xt2_hi[:, j, :, :].rearrange("p (a c) n -> p a (c n)", a=2), 2 - 2 * j, s_xthi)

            def hidden(p, f):
                n = FC * p + f
                act.wait_ge(s_up, after(n + 1))
                act.wait_ge(s_hid, after(n - min(f, 1)))
                nc.scalar.activation(sig[:, f % 2, :], bank[f % 2 * 2], ACT.Sigmoid).then_inc(s_sig, 1)
                act.wait_ge(s_hid, after(n + 1))
                act.wait_ge(s_down, after(n - min(f, 1)))
                nc.scalar.copy(hid_hi[:, f % 2, :], hid[:, f % 2, :]).then_inc(s_hhi, 1)

            for j in range(2):
                xt2_split(0, j)
                keep_rows(2 * BATCH + j, xn2, j, 0)

            def pass_3(p, more):
                for f in range(FC):
                    hidden(p, f)
                    if more and f in (6, 7):
                        keep_rows(2 * p + 2 * BATCH + 2 + f - 6, xn2, f - 6, p + 1)
                if more:
                    for j in range(2):
                        xt2_split(p + 1, j)

            with act.Fori(0, PAIRS - 1) as p:
                pass_3(p, True)
            pass_3(PAIRS - 1, False)

        @block.vector
        def _(dve):
            def split_w(hg, u):
                dve.wait_ge(s_whi, after(hg * UNITS + u + 1))
                nc.vector.tensor_tensor(out=w_lo[:, u, :], in0=w_raw[:, u % RING, :],
                                        in1=w_hi[:, u, :].bitcast(F32), op=ALU.subtract).then_inc(s_wlo, 1)

            def low(out_ap, ps, bias_ap, hi_ap, done):
                nc.vector.scalar_tensor_tensor(out=out_ap, in0=ps, scalar=bias_ap, in1=hi_ap.bitcast(F32),
                                               op0=ALU.add, op1=ALU.subtract).then_inc(done, 1)

            def qk_lo(hg, b, h, part):
                n = hg * STEPS + GH * b.index + h
                dve.wait_ge(s_khi if part else s_qhi, after(n + 1))
                low((k_lo if part else q_lo)[:, :], (ps_k if part else ps_q)[:, 0:SEQ], bias[:, part, h:h + 1],
                    (k_hi if part else q_hi)[:, :], s_klo if part else s_qlo)

            def v_split(hg, b, tt):
                dve.wait_ge(s_vhi, after(hg * TILES + TPB * b.index + tt + 1))
                nc.vector.tensor_tensor(out=v_lo[:, b.slot, tt, :], in0=ps_v[:, :],
                                        in1=v_hi[:, b.slot, tt, :].bitcast(F32),
                                        op=ALU.subtract).then_inc(s_vlo, 1)

            def row_max(hg, b, h):
                n = hg * STEPS + GH * b.index + h
                dve.wait_ge(s_scores, after(n + 1))
                dve.nop(nofuse=True)
                for qt in range(TPB):
                    s = ps_s[:, qt * P:qt * P + (qt + 1) * P]
                    nc.vector.tensor_tensor_reduce(s, s, mask[:, SEQ - (qt + 1) * P:SEQ], -SCALE, 3e38,
                                                   ALU.add, ALU.min, negmax[:, qt:qt + 1]).then_inc(s_max, 1)

            def normalise(hg, b, h):
                n = hg * STEPS + GH * b.index + h
                dve.wait_ge(s_exp, after(n + 1))
                nc.vector.reciprocal(inv[:, :], rowsum[:, :]).then_inc(s_inv, 1)
                dve.wait_ge(s_inv, after(n + 1))
                nc.vector.tensor_scalar(probs[:, 0:P], probs[:, 0:P], inv[:, 0:1], None, ALU.mult)
                nc.vector.tensor_scalar(probs[:, P:KEYS], probs[:, P:KEYS], inv[:, 1:2], None,
                                        ALU.mult).then_inc(s_norm, 1)

            def pt_split(hg, b, h):
                n = hg * STEPS + GH * b.index + h
                dve.wait_ge(s_pthi, after(n + 1))
                nc.vector.tensor_tensor(out=pt_lo[:, :], in0=ps_pt[:, 0:KEYS], in1=pt_hi[:, :].bitcast(F32),
                                        op=ALU.subtract).then_inc(s_ptlo, 1)

            def z_split(hg, b, h):
                n = hg * STEPS + GH * b.index + h
                dve.wait_ge(s_zhi, after(n + 1))
                low(z_lo[:, b.slot, h, :], ps_z[:, 0:SEQ], bias[:, 2, h:h + 1], z_hi[:, b.slot, h, :], s_zlo)

            def add_output(hg, b, tt):
                n = TPB * b.index + tt
                dve.wait_ge(s_o, after(hg * TILES + n + 1))
                dve.wait_ge(s_accin[b.slot], 16 * (b.half + 1))
                a = acc[:, n, :] if isinstance(n, int) else acc[:, bass.ds(n, 1), :].rearrange("p o n -> p (o n)")
                nc.vector.tensor_tensor(out=a, in0=ps_o[:, :], in1=a, op=ALU.add).then_inc(s_acc, 1)

            dve.wait_ge(s_const, 48)
            with dve.Fori(0, GROUPS) as hg:
                dve.wait_ge(s_zhi, after(hg * STEPS))
                nc.vector.tensor_copy(bias[:, :, :].rearrange("p k h -> p (k h)"),
                                      bias_all[:, bass.ds(hg * 3 * GH, 3 * GH)]).then_inc(s_bias, 1)
                dve.wait_ge(s_bias, after(hg + 1))
                for u in range(6):
                    split_w(hg, u)
                qk_lo(hg, Batch(0), 0, 0)
                qk_lo(hg, Batch(0), 0, 1)
                for tt in range(TPB):
                    v_split(hg, Batch(0), tt)
                split_w(hg, 6)
                split_w(hg, 7)

                def body(b):
                    for h in range(GH):
                        row_max(hg, b, h)
                        if b.first:
                            split_w(hg, 8 + 2 * h)
                            split_w(hg, 9 + 2 * h)
                        more = not (b.last and h + 1 == GH)
                        nb, nh = (b, h + 1) if h + 1 < GH else (b.next(), 0)
                        if more:
                            qk_lo(hg, nb, nh, 0)
                        normalise(hg, b, h)
                        if more:
                            qk_lo(hg, nb, nh, 1)
                        pt_split(hg, b, h)
                        if h < TPB:
                            if not b.first:
                                add_output(hg, b.prev(), h)
                        elif not b.last:
                            v_split(hg, b.next(), h - TPB)
                        z_split(hg, b, h)

                over_batches(dve, body)
                for tt in range(TPB):
                    add_output(hg, Batch(BATCH - 1), tt)

            def minus(out_ap, a, hi, done):
                nc.vector.tensor_tensor(out=out_ap, in0=a, in1=hi.bitcast(F32), op=ALU.subtract).then_inc(done, 1)

            def row_stats(n, event, lag, k, ins, eps):
                count = len(ins)
                dve.nop(nofuse=True)
                for i, a in enumerate(ins):
                    nc.vector.bn_stats(bn_raw[:, k + i, :], a).then_inc(s_bn, 1)
                dve.wait_ge(s_bn, after(n + count))
                dve.nop(nofuse=True)
                for i in range(count):
                    nc.vector.bn_aggr(bn[:, k + i, :], bn_raw[:, k + i, :]).then_inc(s_aggr, 1)
                dve.wait_ge(s_aggr, after(n + count))
                if not isinstance(event, int) or event >= lag:
                    dve.wait_ge(s_rdev, after(event + 1 - lag))
                nc.vector.tensor_scalar(variance[:, k:k + count, :], bn[:, k:k + count, 1:2], eps, None, ALU.add
                                        ).then_inc(s_var, 1)

            def sum_stats(which, n, event, lag, tile, k, count):
                row_stats(n, event, lag, k, [pick(acc, tile + i) for i in range(count)], LN_EPS)
                st = stats[which][:, tile:tile + count, :] if isinstance(tile, int) else \
                    stats[which][:, bass.ds(tile, count), :]
                nc.vector.tensor_copy(st[:, :, 0:1], bn[:, k:k + count, 0:1]).then_inc(s_mean, 1)

            def normal_rows(which, tile, rows, slot):
                for tt in range(TPB):
                    st = pick(stats[which], tile + tt)
                    last = nc.vector.tensor_scalar(rows[:, slot, tt, :], pick(acc, tile + tt), st[:, 0:1], st[:, 1:2],
                                                   ALU.subtract, ALU.mult)
                last.then_inc(s_xn, 1)

            def stats_1(b):
                dve.wait_ge(s_bo, after(TPB * b.index + TPB))
                sum_stats(0, TPB * b.index, b.index, 1, TPB * b.index, 0, TPB)

            def norm_1(b):
                dve.wait_ge(s_rdev, after(b.index + 1))
                dve.wait_ge(s_mean, after(b.index + 1))
                if not (b.first or b.second):
                    dve.wait_ge(s_xt, after(b.index - 1))
                normal_rows(0, TPB * b.index, xn, b.slot)

            def xt_low(n, slot, base, hi, lo):
                dve.wait_ge(s_xthi, after(n + 1))
                minus(lo[:, slot, :, :].rearrange("p (a c) n -> p a (c n)", a=2), psum[:, base:base + 2, :],
                      hi[:, slot, :, :].rearrange("p (a c) n -> p a (c n)", a=2), s_xtlo)

            def xq_low(b):
                dve.wait_ge(s_xqhi, after(b.index + 1))
                minus(xq_lo[:, b.slot, :, :].rearrange("p (a h) n -> p a (h n)", a=2), psum[:, 2:4, :],
                      xq_hi[:, b.slot, :, :].rearrange("p (a h) n -> p a (h n)", a=2), s_xqlo)

            stats_1(Batch(0))
            norm_1(Batch(0))
            dve.wait_ge(s_ghi, after(1))
            minus(g_lo[:, :, :].rearrange("p h e -> p (h e)"), bank[2],
                  g_hi[:, :, :].rearrange("p h e -> p (h e)"), s_glo)
            dve.wait_ge(s_whsplit, after(1))
            minus(wh_lo[:, :, :].rearrange("p h e -> p (h e)"), wx_raw[:, 0, :],
                  wh_hi[:, :, :].rearrange("p h e -> p (h e)"), s_wh)
            xt_low(0, 0, 0, xt_hi, xt_lo)

            def pass_1(b):
                if not b.last:
                    stats_1(b.next())
                xq_low(b)
                if not b.last:
                    norm_1(b.next())
                    xt_low(b.next().index, 0, 0, xt_hi, xt_lo)

            over_batches(dve, pass_1)

            dve.wait_ge(s_xs, after(BATCH))
            nc.vector.tensor_tensor(out=a_raw[:, :, :], in0=psum[:, 4:8, 0:KEYS], in1=decay[:, :, :],
                                    op=ALU.mult).then_inc(s_araw, 1)
            dve.wait_ge(s_araw, after(1))
            flat = a_raw[:, :, :].rearrange("p h n -> p (h n)")
            nc.vector.scalar_tensor_tensor(out=flat, in0=flat, scalar=-1.0, in1=flat, op0=ALU.mult, op1=ALU.max
                                           ).then_inc(s_araw, 1)
            dve.wait_ge(s_araw, after(2))
            nc.vector.tensor_scalar(flat, flat, 1.0, None, ALU.max).then_inc(s_araw, 1)

            def norm_2(p, j):
                n = 2 * p + j
                if isinstance(p, int) and p == 0:
                    dve.wait_ge(s_xt, after(BATCH))
                else:
                    dve.wait_ge(s_xt, after(n + BATCH - 1))
                    dve.wait_ge(s_back, after(n - 1))
                normal_rows(0, TPB * n, xn, j)

            def xv_low(p, j, tt):
                dve.wait_ge(s_xvhi, after(4 * p + 2 * j + tt + 1))
                minus(xv_lo[:, tt, :, j, :], bank[2 + tt].rearrange("p (h e) -> p h e", h=XH),
                      xv_hi[:, tt, :, j, :], s_xvlo)

            norm_2(0, 0)
            norm_2(0, 1)
            for tt in range(TPB):
                xv_low(0, 0, tt)
            xt_low(BATCH, 0, 2, xt_hi, xt_lo)
            for tt in range(TPB):
                xv_low(0, 1, tt)
            dve.wait_ge(s_ahi, after(1))
            minus(a_lo[:, :, :], a_raw[:, :, :], a_hi[:, :, :], s_alo)
            dve.wait_ge(s_gohi, after(1))
            minus(wgo_lo[:, 0, :, :], wgo_raw[:, :, :], wgo_hi[:, 0, :, :], s_golo)
            xt_low(BATCH + 1, 1, 2, xt_hi, xt_lo)
            dve.wait_ge(s_gohi, after(2))
            minus(wgo_lo[:, 1, :, :], wgo_raw[:, :, :], wgo_hi[:, 1, :, :], s_golo)

            N1 = TILES
            S1 = BATCH

            def group(p, k):
                return psum[:, 4 + 2 * (k % 2):6 + 2 * (k % 2), :].rearrange(
                    "p a (h j e) -> p (a h) j e", h=2, j=2)[:, :, k // 2, :]

            def group_stats(p, k):
                dve.wait_ge(s_xo, after(2 * p + k % 2 + 1))
                row_stats(8 * p + N1 + k, 8 * p + S1 + k, 2, 2 + k % 2, [group(p, k)], GN_EPS)

            def group_norm(p, k):
                y = y_raw[:, k % 2, :]
                nc.vector.scalar_tensor_tensor(out=y.rearrange("p (h e) -> p h e", h=XH), in0=group(p, k),
                                               scalar=bn[:, 2 + k % 2, 0:1],
                                               in1=gamma[:, :].rearrange("p (h e) -> p h e", h=XH),
                                               op0=ALU.subtract, op1=ALU.mult).then_inc(s_yc, 1)
                dve.wait_ge(s_yc, after(4 * p + k + 1))
                dve.wait_ge(s_rdev, after(8 * p + S1 + k + 1))
                nc.vector.scalar_tensor_tensor(out=y, in0=y, scalar=rdev[:, k % 2, 0:1], in1=beta[:, :],
                                               op0=ALU.mult, op1=ALU.add).then_inc(s_ys, 1)

            def gated(p, k):
                dve.wait_ge(s_relu, after(4 * p + k + 1))
                dve.wait_ge(s_ys, after(4 * p + k + 1))
                nc.vector.tensor_tensor(out=gate[:, k, :], in0=gate[:, k, :], in1=y_raw[:, k % 2, :],
                                        op=ALU.mult).then_inc(s_wy, 1)

            def wyt_low(p, k):
                dve.wait_ge(s_wythi, after(4 * p + k + 1))
                minus(wyt_lo[:, k % 2, :, :].rearrange("p c n -> p (c n)"), bank[2 + k % 2],
                      wyt_hi[:, k % 2, :, :].rearrange("p c n -> p (c n)"), s_wytlo)

            def residual(p, k):
                tile = 4 * p + k
                dve.wait_ge(s_back, after(2 * p + k // 2 + 1))
                dve.wait_ge(s_xout, after(tile + 1))
                a = pick(acc, tile)
                nc.vector.tensor_tensor(out=a, in0=bank[1], in1=a, op=ALU.add).then_inc(s_res, 1)
                dve.wait_ge(s_res, after(tile + 1))
                sum_stats(1, 8 * p + N1 + 4 + k, 8 * p + S1 + 4 + k, 2, tile, k % 2, 1)

            def pass_2(p, more):
                group_stats(p, 0)
                group_stats(p, 1)
                group_norm(p, 0)
                gated(p, 0)
                group_norm(p, 1)
                if more:
                    xv_low(p + 1, 0, 0)
                    xv_low(p + 1, 0, 1)
                    norm_2(p + 1, 0)
                gated(p, 1)
                group_stats(p, 2)
                group_stats(p, 3)
                group_norm(p, 2)
                if more:
                    xt_low(2 * p + BATCH + 2, 0, 2, xt_hi, xt_lo)
                    norm_2(p + 1, 1)
                group_norm(p, 3)
                if more:
                    xv_low(p + 1, 1, 0)
                    xv_low(p + 1, 1, 1)
                wyt_low(p, 0)
                wyt_low(p, 1)
                gated(p, 2)
                gated(p, 3)
                residual(p, 0)
                wyt_low(p, 2)
                residual(p, 1)
                wyt_low(p, 3)
                residual(p, 2)
                if more:
                    xt_low(2 * p + BATCH + 3, 1, 2, xt_hi, xt_lo)
                residual(p, 3)

            with dve.Fori(0, PAIRS - 1) as p:
                pass_2(p, True)
            pass_2(PAIRS - 1, False)

            dve.wait_ge(s_abs, after(GROUPS * BATCH))
            nc.vector.tensor_reduce(wtot[:, :], wsum[:, :, :].rearrange("p b m -> p m b"), AX_X, ALU.add).then_inc(s_tot, 1)
            N2, S2 = 3 * TILES, BATCH + 2 * TILES

            def norm_3(p, j):
                n = 2 * p + j
                if not (isinstance(p, int) and p == 0):
                    dve.wait_ge(s_xt, after(n + 2 * BATCH - 1))
                    dve.wait_ge(s_back, after(n + BATCH - 1))
                else:
                    dve.wait_ge(s_rdev, after(S2))
                    dve.wait_ge(s_mean, after(BATCH + TILES))
                normal_rows(1, TPB * n, xn2, j)

            norm_3(0, 0)
            norm_3(0, 1)
            dve.wait_ge(s_totps, after(1))
            for i, sign in enumerate((0.5, -0.5)):
                nc.vector.tensor_scalar(thr[:, i, :], bank[4][:, 0:3], 1.0 / (DIM * FF), 1e-8, ALU.mult, ALU.add
                                        ).then_inc(s_thr, 1)
            dve.wait_ge(s_thr, after(2))
            for i, sign in enumerate((0.5, -0.5)):
                nc.vector.tensor_scalar(thr[:, i, :], thr[:, i, :], sign, None, ALU.mult).then_inc(s_thr, 1)
            dve.wait_ge(s_thr, after(4))

            def ternary(u):
                m = u % 3
                dve.wait_ge(s_fdma[u % RING], (u // RING + 1) * 16)
                nc.vector.tensor_scalar(f_neg[:, u % 2, :], f_raw[:, u % RING, :], thr[:, 1, m:m + 1], None,
                                        ALU.is_lt).then_inc(s_neg, 1)
                dve.wait_ge(s_neg, after(u + 1))
                nc.vector.scalar_tensor_tensor(out=f_w[:, u, :], in0=f_raw[:, u % RING, :],
                                               scalar=thr[:, 0, m:m + 1], in1=f_neg[:, u % 2, :],
                                               op0=ALU.is_gt, op1=ALU.subtract).then_inc(s_fw, 1)

            def hidden(p, f):
                n = FC * p + f
                dve.wait_ge(s_sig, after(n + 1))
                dve.wait_ge(s_hhi, after(n - min(f, 1)))
                nc.vector.tensor_tensor(out=hid[:, f % 2, :], in0=bank[f % 2 * 2 + 1], in1=sig[:, f % 2, :],
                                        op=ALU.mult).then_inc(s_hid, 1)

            def hidden_low(p, f):
                dve.wait_ge(s_hhi, after(FC * p + f + 1))
                minus(hid_lo[:, f % 2, :], hid[:, f % 2, :], hid_hi[:, f % 2, :], s_hlo)

            def finish(p):
                dve.wait_ge(s_down, after(FC * p + FC))
                dve.wait_ge(s_yout, after(64 * p))
                for k in range(4):
                    dve.wait_ge(s_back, after(2 * p + BATCH + k // 2 + 1))
                    nc.vector.tensor_tensor(out=y3[:, k, :], in0=bank[4 + k], in1=pick(acc, 4 * p + k), op=ALU.add
                                            ).then_inc(s_y3, 1)
                dve.wait_ge(s_y3, after(4 * p + 4))
                for k in range(0, 4, 2):
                    row_stats(4 * p + N2 + k, 2 * p + S2 + k // 2, 2, k, [y3[:, k + i, :] for i in range(2)], LN_EPS)
                for k in range(4):
                    dve.wait_ge(s_rdev, after(2 * p + S2 + k // 2 + 1))
                    nc.vector.tensor_scalar(y3[:, k, :], y3[:, k, :], bn[:, k, 0:1], rdev[:, k, 0:1],
                                            ALU.subtract, ALU.mult).then_inc(s_y3n, 1)

            xt_low(2 * BATCH, 0, 2, xt2_hi, xt2_lo)
            xt_low(2 * BATCH + 1, 1, 0, xt2_hi, xt2_lo)

            def pass_3(p, first, more):
                if first:
                    for u in range(3):
                        ternary(u)
                for f in range(FC):
                    if first and f + 1 < FC:
                        for m in range(3):
                            ternary(3 * (f + 1) + m)
                    hidden(p, f)
                    hidden_low(p, f)
                    if more and f in (4, 5):
                        norm_3(p + 1, f - 4)
                if more:
                    for j in range(2):
                        xt_low(2 * p + 2 * BATCH + 2 + j, j, 2 - 2 * j, xt2_hi, xt2_lo)
                finish(p)

            pass_3(0, True, True)
            with dve.Fori(1, PAIRS - 1) as p:
                pass_3(p, False, True)
            pass_3(PAIRS - 1, False, False)


def kernel(**inputs):
    import numpy as _np
    import concourse.bacc as _bacc
    from concourse import mybir as _mybir
    from concourse.bass_utils import run_bass_kernel_spmd as _run

    i = {k: _np.asarray(v) for k, v in inputs.items()}
    groups = []
    for g in range(GROUPS):
        hs = range(g * GH, (g + 1) * GH)
        q = [i["L0_attn_W_Q"][h].reshape(CH, P, DH).transpose(1, 0, 2).reshape(P, 512) for h in hs]
        k = [i["L0_attn_W_K"][h].reshape(CH, P, DH).transpose(1, 0, 2).reshape(P, 512) for h in hs]
        v = _np.concatenate([i["L0_attn_W_V"][h].reshape(CH, P, 1, DH) for h in hs], axis=2).reshape(CH, P, GH * DH)
        o = [i["L0_attn_W_O"][h] for h in hs]
        groups.append(_np.stack([q[0], k[0], *v, q[1], k[1], q[2], k[2], q[3], k[3], *o]))
    rows = _np.arange(P)
    gam = 1.0 - 2.0 ** (-5.0 - _np.arange(XH))
    expo = _np.arange(SEQ)[None, :] - _np.arange(SEQ)[:, None]
    full = _np.where(expo <= 0, gam[:, None, None] ** _np.minimum(expo, 0), 0.0)
    full = (full / _np.sqrt(full.sum(-1))[:, None, :] / _np.sqrt(float(DH))).transpose(2, 0, 1)
    by_chunks = lambda w: w.reshape(CH, P, -1).transpose(1, 0, 2)
    w1, w2, w3 = (i[f"L0_ffn_w{n}"] for n in (1, 2, 3))
    w_ffn = _np.stack([w1.reshape(FC, P, CH, P).transpose(0, 3, 2, 1).reshape(FC, P, 512),
                       w2.reshape(FC, P, CH, P).transpose(0, 3, 2, 1).reshape(FC, P, 512),
                       w3.T.reshape(FC, P, DIM)], axis=1)
    wh = i["L0_xattn_Wh"]
    in_rows = lambda v: _np.broadcast_to(v, (P, DIM))
    arrays = {
        "xT": i["x"].reshape(BATCH, SEQ, CH, P).transpose(0, 3, 2, 1).reshape(BATCH, P, CH * SEQ),
        "x": i["x"].reshape(TILES, P, DIM).transpose(1, 0, 2),
        "w_attn": _np.concatenate(groups),
        "biases": _np.stack([i[f"L0_attn_b_{k}"].reshape(GROUPS, GH, DH) for k in "QKV"], axis=1)
                  .reshape(GROUPS * 3 * GH, DH).T,
        "ctxT": i["ctx_2048"].reshape(BATCH, SEQ, CH, P).transpose(0, 3, 2, 1).reshape(BATCH, P, CH * SEQ),
        "w_head": _np.stack([wh.transpose(1, 0, 2).reshape(P, 512), wh.transpose(2, 0, 1).reshape(P, 512)], axis=1),
        "decay": _np.concatenate([full[:P], full[P:, :, P:]], axis=2).astype(_np.float32),
        "b_o": in_rows(i["L0_attn_b_O"]),
        "gamma": in_rows(i["L0_xattn_gn_gamma"]),
        "beta": in_rows(i["L0_xattn_gn_beta"]),
        "w_gate": by_chunks(i["L0_xattn_wg_w"]),
        "w_out": by_chunks(i["L0_xattn_wo_w"]),
        "w_ffn": w_ffn.reshape(3 * FC, P, 512),
        "w_abs": _np.stack([w.reshape(GROUPS * BATCH, P, ABS_COLS) for w in (w1, w2, w3)], axis=2)
                 .reshape(GROUPS * BATCH, P, 3 * ABS_COLS),
        "identity": _np.eye(P, dtype=_np.float32),
        "causal": _np.concatenate([_np.zeros((P, P)), _np.where(rows[None, :] <= rows[:, None], 0.0, MASKED)],
                                  axis=1).astype(_np.float32),
    }
    nc = _bacc.Bacc("TRN2", target_bir_lowering=False, num_devices=1)
    feed, t = {}, {}
    for name, a in arrays.items():
        a = _np.ascontiguousarray(a)
        feed[f"in_{name}"] = a
        t[name] = nc.dram_tensor(f"in_{name}", a.shape, _mybir.dt.from_np(a.dtype), kind="ExternalInput").ap()
    out = nc.dram_tensor("out_0", (BATCH, SEQ, DIM), F32, kind="ExternalOutput").ap()
    decoder_kernel(nc, t, out.rearrange("b (t p) d -> p (b t) d", p=P))
    r = _run(nc, [feed], core_ids=[0])
    return r.results[0]["out_0"]
```

```python
from contextlib import ExitStack

import concourse.bass as bass
from concourse import mybir

F32 = mybir.dt.float32
F32R = mybir.dt.float32r
ACT = mybir.ActivationFunctionType
ALU = mybir.AluOpType
AX_X = mybir.AxisListType.X

P = 128
BATCH, SEQ, DIM = 16, 256, 512
HEADS, DH = 16, 128
CH = DIM // P
TPB = SEQ // P
TILES = BATCH * TPB
GROUPS, GH = 4, 4
STEPS = BATCH * GH
UNITS = 16
RING = 4
KEYS = P + SEQ
MASKED = -1e30
LN_EPS = 1e-5
GN_EPS = 1e-3
XH = DIM // DH
PAIRS = BATCH // 2
FF = 1408
FC = FF // P
ABS_COLS = DIM * FF // P // (GROUPS * BATCH)
HALVES = (range(0, 2), range(2, 4))
SPLIT_LAST = ((0, 1, 2), (3, 4, 5), (6, 7), (8, 9))
SPLIT_FIRST = ((10, 11), (), (12, 13), (14, 15))
SPLIT_BEFORE = range(0, 10)


def after(events):
    return events + 1


class Batch:

    def __init__(self, c, it=0, hg=0):
        self.c, self.it, self.hg = c, it, hg
        self.slot = c % 2
        self.half = it + c // 2
        self.index = 2 * it + c
        at = c if isinstance(it, int) else None
        self.first, self.second, self.last = (at == 0), (at == 1), (at == BATCH - 1)
        self.all = BATCH * hg + self.index
        self.start = isinstance(self.all, int) and self.all < 2
        self.end = self.last and isinstance(hg, int) and hg == GROUPS - 1

    def next(self):
        return Batch(0, 0, self.hg + 1) if self.last else Batch(self.c + 1, self.it, self.hg)

    def prev(self):
        return Batch(BATCH - 1, 0, self.hg - 1) if self.first else Batch(self.c - 1, self.it, self.hg)


def over_batches(eng, body):
    body(Batch(0))
    with eng.Fori(0, (BATCH - 2) // 2) as it:
        body(Batch(1, it))
        body(Batch(2, it))
    body(Batch(BATCH - 1))


def over_batches_1(eng, body):
    body(Batch(0))
    with eng.Fori(0, (BATCH - 4) // 2) as it:
        body(Batch(1, it))
        body(Batch(2, it))
    for b in range(BATCH - 3, BATCH):
        body(Batch(b))


def over_groups(eng, body):
    def inner(hg):
        with eng.Fori(0, (BATCH - 2) // 2) as it:
            body(Batch(1, it, hg))
            body(Batch(2, it, hg))
        body(Batch(BATCH - 1, 0, hg))

    body(Batch(0))
    with eng.Fori(0, GROUPS - 1) as hg:
        inner(hg)
        body(Batch(0, 0, hg + 1))
    inner(GROUPS - 1)


def pick(tensor, n, count=1):
    if isinstance(n, int):
        return tensor[:, n, :] if count == 1 else tensor[:, n:n + count, :]
    found = tensor[:, bass.ds(n, count), :]
    return found.rearrange("p o n -> p (o n)") if count == 1 else found


def decoder_kernel(nc, t, out):
    with ExitStack() as ctx:
        def sb(name, shape, dt=F32, scope=ctx):
            return scope.enter_context(nc.sbuf_tensor(name, shape, dt))

        def sem(name):
            return ctx.enter_context(nc.semaphore(name))

        psum = ctx.enter_context(nc.psum_tensor("psum", [P, 8, 512], F32))
        bank = [psum[:, i, :] for i in range(8)]
        ps_q, ps_k, ps_v, ps_o, ps_s, ps_pt, ps_z = bank[:7]

        acc = sb("acc", [P, TILES, DIM])
        ident = sb("ident", [P, P])
        mask = sb("mask", [P, SEQ])
        bias_all = sb("bias_all", [P, GROUPS * 3 * GH])
        bo_rows = sb("bo_rows", [P, DIM])
        stats = [sb(f"stats{i}", [P, TILES, 2]) for i in range(2)]
        wsum = sb("wsum", [P, GROUPS * BATCH, 3])
        thr = sb("thr", [P, 2, 3])
        bn_raw = sb("bn_raw", [P, 4, 6])
        bn = sb("bn", [P, 4, 2])
        variance = sb("variance", [P, 4, 1])
        rdev = sb("rdev", [P, 4, 1])
        power = sb("power", [P, 2, 1])

        phase_a = ExitStack()
        w_raw = sb("w_raw", [P, RING, 512], F32, phase_a)
        w_hi = sb("w_hi", [P, UNITS, 512], F32R, phase_a)
        w_lo = sb("w_lo", [P, UNITS, 512], F32R, phase_a)
        x_raw = sb("x_raw", [P, 2, CH * SEQ], F32, phase_a)
        x_hi = sb("x_hi", [P, 2, CH, SEQ], F32R, phase_a)
        x_lo = sb("x_lo", [P, 2, CH, SEQ], F32R, phase_a)
        q_hi = sb("q_hi", [P, SEQ], F32R, phase_a)
        q_lo = sb("q_lo", [P, SEQ], F32R, phase_a)
        k_hi = sb("k_hi", [P, SEQ], F32R, phase_a)
        k_lo = sb("k_lo", [P, SEQ], F32R, phase_a)
        v_hi = sb("v_hi", [P, 2, TPB, GH * DH], F32R, phase_a)
        v_lo = sb("v_lo", [P, 2, TPB, GH * DH], F32R, phase_a)
        z_hi = sb("z_hi", [P, 2, GH, SEQ], F32R, phase_a)
        z_lo = sb("z_lo", [P, 2, GH, SEQ], F32R, phase_a)
        probs = sb("probs", [P, KEYS], F32, phase_a)
        pt_hi = sb("pt_hi", [P, KEYS], F32R, phase_a)
        pt_lo = sb("pt_lo", [P, KEYS], F32R, phase_a)
        negmax = sb("negmax", [P, TPB], F32, phase_a)
        rowsum = sb("rowsum", [P, TPB], F32, phase_a)
        inv = sb("inv", [P, TPB], F32, phase_a)
        w_abs = sb("w_abs", [P, 2, 3 * ABS_COLS], F32, phase_a)
        phase_a.close()

        cross = ExitStack()
        ctx_raw = sb("ctx_raw", [P, 2, CH * SEQ], F32, cross)
        ctx_hi = sb("ctx_hi", [P, 2, CH, SEQ], F32R, cross)
        ctx_lo = sb("ctx_lo", [P, 2, CH, SEQ], F32R, cross)
        xn = sb("xn", [P, 2, TPB, DIM], F32, cross)
        xt_hi = sb("xt_hi", [P, 2, CH, SEQ], F32R, cross)
        xt_lo = sb("xt_lo", [P, 2, CH, SEQ], F32R, cross)
        a_hi = sb("a_hi", [P, XH, KEYS], F32R, cross)
        a_lo = sb("a_lo", [P, XH, KEYS], F32R, cross)
        ones_r = sb("ones_r", [P, P], F32R, cross)
        wh_hi = sb("wh_hi", [P, XH, DH], F32R, cross)
        wh_lo = sb("wh_lo", [P, XH, DH], F32R, cross)
        cross_1 = ExitStack()
        wtot = sb("wtot", [P, 3], F32, cross_1)
        zeros = sb("zeros", [P, P], F32, cross_1)
        power_all = sb("power_all", [P, TILES, 1], F32, cross_1)
        wx_raw = sb("wx_raw", [P, 2, XH * DH], F32, cross_1)
        decay = sb("decay", [P, XH, KEYS], F32, cross_1)
        a_raw = sb("a_raw", [P, XH, KEYS], F32, cross_1)
        g_hi = sb("g_hi", [P, XH, DH], F32R, cross_1)
        g_lo = sb("g_lo", [P, XH, DH], F32R, cross_1)
        xq_hi = sb("xq_hi", [P, 2, XH, SEQ], F32R, cross_1)
        xq_lo = sb("xq_lo", [P, 2, XH, SEQ], F32R, cross_1)
        cross_1.close()
        cross_2 = ExitStack()
        wgo_hi = sb("wgo_hi", [P, 2, CH, DIM], F32R, cross_2)
        wgo_lo = sb("wgo_lo", [P, 2, CH, DIM], F32R, cross_2)
        gamma = sb("gamma", [P, DIM], F32, cross_2)
        beta = sb("beta", [P, DIM], F32, cross_2)
        xv_hi = sb("xv_hi", [P, TPB, XH, 2, DH], F32R, cross_2)
        xv_lo = sb("xv_lo", [P, TPB, XH, 2, DH], F32R, cross_2)
        gate = sb("gate", [P, 4, DIM], F32, cross_2)
        wgo_raw = gate
        y_raw = sb("y_raw", [P, 2, DIM], F32, cross_2)
        wyt_hi = sb("wyt_hi", [P, 2, CH, P], F32R, cross_2)
        wyt_lo = sb("wyt_lo", [P, 2, CH, P], F32R, cross_2)
        cross_2.close()
        cross.close()

        ffn = ExitStack()
        f_raw = sb("f_raw", [P, RING, 512], F32, ffn)
        f_neg = sb("f_neg", [P, 2, 512], F32, ffn)
        f_w = sb("f_w", [P, 3 * FC, 512], F32R, ffn)
        xn2 = sb("xn2", [P, 2, TPB, DIM], F32, ffn)
        xt2_hi = sb("xt2_hi", [P, 2, CH, SEQ], F32R, ffn)
        xt2_lo = sb("xt2_lo", [P, 2, CH, SEQ], F32R, ffn)
        sig = sb("sig", [P, 2, 512], F32, ffn)
        hid = sb("hid", [P, 2, 512], F32, ffn)
        hid_hi = sb("hid_hi", [P, 2, 512], F32R, ffn)
        hid_lo = sb("hid_lo", [P, 2, 512], F32R, ffn)
        y3 = sb("y3", [P, 4, DIM], F32, ffn)
        ffn.close()

        def bias_of(b, kind, h):
            column = (b.hg * 3 + kind) * GH + h
            return bias_all[:, column:column + 1] if isinstance(column, int) else bias_all[:, bass.ds(column, 1)]

        def unit_qk(kind, h):
            return kind if h == 0 else 6 + 2 * (h - 1) + kind

        UNIT_V, UNIT_O = 2, 12

        s_const = sem("s_const")
        s_primed = sem("s_primed")
        s_wdma = [sem(f"s_wdma{i}") for i in range(RING)]
        s_xdma = [sem(f"s_xdma{i}") for i in range(2)]
        s_accin = [sem(f"s_accin{i}") for i in range(2)]
        progress = (s_bias, s_whi, s_wlo, s_x, s_q, s_k, s_v, s_o, s_scores, s_pt, s_z,
         s_qhi, s_khi, s_vhi, s_exp, s_pthi, s_zhi,
         s_max, s_qlo, s_klo, s_vlo, s_inv, s_norm, s_ptlo, s_zlo, s_acc, s_xhi) = tuple(
            sem(n) for n in
            "s_bias s_whi s_wlo s_x s_q s_k s_v s_o s_scores s_pt s_z "
            "s_qhi s_khi s_vhi s_exp s_pthi s_zhi "
            "s_max s_qlo s_klo s_vlo s_inv s_norm s_ptlo s_zlo s_acc s_xhi".split())
        s_out = sem("s_out")
        s_ctxdma = [sem(f"s_ctxdma{i}") for i in range(2)]
        s_const2, s_gdma, s_odma = (sem(n) for n in "s_const2 s_gdma s_odma".split())
        s_absdma = [sem(f"s_absdma{i}") for i in range(2)]
        s_fdma = [sem(f"s_fdma{i}") for i in range(RING)]
        names = ("s_bo s_bn s_aggr s_var s_rdev s_mean s_xn s_xt s_xthi s_xtlo s_ctxhi s_ctxlo s_xq s_xqhi s_xqlo s_xs "
                 "s_g s_ghi s_glo s_whsplit s_wh s_araw s_ahi s_alo s_back s_xv s_xvhi s_xvlo s_xo s_gate s_relu "
                 "s_yc s_ys s_wy s_wyt s_wythi s_wytlo s_xout s_res s_gohi s_golo s_abs s_ones "
                 "s_tot s_totps s_thr s_neg s_fw s_up s_sig s_hid s_hhi s_hlo s_down s_y3 s_y3n s_yout").split()
        (s_bo, s_bn, s_aggr, s_var, s_rdev, s_mean, s_xn, s_xt, s_xthi, s_xtlo, s_ctxhi, s_ctxlo, s_xq, s_xqhi, s_xqlo, s_xs,
         s_g, s_ghi, s_glo, s_whsplit, s_wh, s_araw, s_ahi, s_alo, s_back, s_xv, s_xvhi, s_xvlo, s_xo, s_gate,
         s_relu, s_yc, s_ys, s_wy, s_wyt, s_wythi, s_wytlo, s_xout, s_res, s_gohi, s_golo, s_abs, s_ones,
         s_tot, s_totps, s_thr, s_neg, s_fw, s_up, s_sig, s_hid, s_hhi, s_hlo, s_down, s_y3, s_y3n,
         s_yout) = later = tuple(sem(n) for n in names)

        block = ctx.enter_context(nc.Block())

        @block.sync
        def _(sp):
            for dst, src in ((bias_all, "biases"), (ident, "identity"), (mask, "causal")):
                sp.dma_start(dst[:, :], t[src]).then_inc(s_const, 16)

            sp.dma_start(bo_rows[:, :], t["b_o"]).then_inc(s_const, 16)

            def load_w(hg, u):
                if not (isinstance(hg, int) and hg * UNITS + u < RING):
                    sp.wait_ge(s_wlo, after(hg * UNITS + u - RING + 1))
                sp.dma_start(w_raw[:, u % RING, :], pick(t["w_attn"].rearrange("u p n -> p u n"), hg * UNITS + u)
                             ).then_inc(s_wdma[u % RING], 16)

            def load_x(b, residual):
                if not b.start:
                    sp.wait_ge(s_x, after(b.all - 1))
                sp.dma_start(x_raw[:, b.slot, :], pick(t["xT"].rearrange("b p n -> p b n"), b.index)
                             ).then_inc(s_xdma[b.slot], 16)
                if not b.start:
                    sp.wait_ge(s_abs, after(b.all - 1))
                sp.dma_start(w_abs[:, b.slot, :], pick(t["w_abs"].rearrange("b p n -> p b n"), b.all)
                             ).then_inc(s_absdma[b.slot], 16)
                if residual:
                    if not b.start:
                        sp.wait_ge(s_accin[b.slot], 16 * b.half)
                    sp.dma_start(pick(acc, TPB * b.index, TPB), pick(t["x"], TPB * b.index, TPB)
                                 ).then_inc(s_accin[b.slot], 16)

            def inner_x(hg, residual):
                with sp.Fori(0, (BATCH - 2) // 2) as it:
                    load_x(Batch(2, it, hg), residual)
                    load_x(Batch(3, it, hg), residual)

            def ahead(hg):
                for u in range(RING):
                    load_w(hg + 1, u)
                load_x(Batch(0, 0, hg + 1), False)
                load_x(Batch(1, 0, hg + 1), False)
                for u in range(RING, UNITS):
                    load_w(hg + 1, u)

            sp.wait_ge(s_primed, 1)
            for u in range(2):
                load_w(0, u)
            load_x(Batch(0), True)
            for u in range(2, UNITS):
                load_w(0, u)
                if u == 9:
                    load_x(Batch(1), True)
            inner_x(0, True)
            ahead(0)
            with sp.Fori(1, GROUPS - 1) as hg:
                inner_x(hg, False)
                ahead(hg)
            inner_x(GROUPS - 1, False)

            sp.wait_ge(s_acc, after(GROUPS * TILES))
            for dst, src in ((wx_raw, "w_head"), (decay, "decay")):
                sp.dma_start(dst[:, :, :], t[src]).then_inc(s_const2, 16)

            def load_ctx(n, b):
                if not isinstance(n, int) or n >= 2:
                    sp.wait_ge(s_ctxlo, after(n - 1))
                sp.dma_start(ctx_raw[:, b.slot, :], pick(t["ctxT"].rearrange("b p n -> p b n"), b.index)
                             ).then_inc(s_ctxdma[b.slot], 16)

            over_batches(sp, lambda b: load_ctx(b.index, b))
            load_ctx(BATCH, Batch(0))
            load_ctx(BATCH + 1, Batch(1))
            sp.wait_ge(s_xs, after(BATCH))
            sp.wait_ge(s_alo, after(1))
            for dst, src in ((gamma, "gamma"), (beta, "beta")):
                sp.dma_start(dst[:, :], t[src]).then_inc(s_gdma, 16)
            sp.dma_start(wgo_raw[:, :, :], t["w_gate"]).then_inc(s_gdma, 16)

            sp.wait_ge(s_golo, after(1))
            sp.dma_start(wgo_raw[:, :, :], t["w_out"]).then_inc(s_odma, 16)
            with sp.Fori(0, PAIRS - 1) as p:
                load_ctx(2 * p + BATCH + 2, Batch(2, p))
                load_ctx(2 * p + BATCH + 3, Batch(3, p))

            sp.wait_ge(s_res, after(TILES))
            for u in range(3 * FC):
                if u >= RING:
                    sp.wait_ge(s_fw, after(u - RING + 1))
                sp.dma_start(f_raw[:, u % RING, :], t["w_ffn"][u, :, :]).then_inc(s_fdma[u % RING], 16)

            def store(p):
                for k in range(4):
                    sp.wait_ge(s_y3n, after(4 * p + k + 1))
                    sp.dma_start(pick(out, 4 * p + k), y3[:, k, :]).then_inc(s_yout, 16)

            with sp.Fori(0, PAIRS) as p:
                store(p)
            sp.wait_ge(s_yout, after(16 * TILES))

        @block.gpsimd
        def _(pool):
            for s in progress + later:
                pool.sem_inc(s, 1)
            pool.sem_inc(s_primed, 1)

            def split_x(b):
                pool.wait_ge(s_xdma[b.slot], (PAIRS * b.hg + b.half + 1) * 16)
                if not b.start:
                    pool.wait_ge(s_k, after(GH * (b.all - 1)))
                hi = x_hi[:, b.slot, :, :].rearrange("p c n -> p (c n)")
                pool.nop(nofuse=True)
                nc.gpsimd.tensor_copy(hi, x_raw[:, b.slot, :]).then_inc(s_xhi, 1)
                pool.wait_ge(s_xhi, after(b.all + 1))
                nc.gpsimd.tensor_tensor(out=x_lo[:, b.slot, :, :].rearrange("p c n -> p (c n)"),
                                        in0=x_raw[:, b.slot, :], in1=hi.bitcast(F32),
                                        op=ALU.subtract).then_inc(s_x, 1)

            def add_bo(b):
                pool.wait_ge(s_accin[b.slot], 16 * (b.half + 1))
                for tt in range(TPB):
                    a = pick(acc, TPB * b.index + tt)
                    nc.gpsimd.tensor_tensor(out=a, in0=a, in1=bo_rows[:, :], op=ALU.add).then_inc(s_bo, 1)


            def group_0(b):
                if b.first:
                    split_x(b)
                    pool.wait_ge(s_const, 64)
                add_bo(b)
                if not b.last:
                    split_x(b.next())

            over_batches(pool, group_0)
            with pool.Fori(1, GROUPS) as hg:
                split_x(Batch(0, 0, hg))
                with pool.Fori(0, (BATCH - 2) // 2) as it:
                    split_x(Batch(1, it, hg))
                    split_x(Batch(2, it, hg))
                split_x(Batch(BATCH - 1, 0, hg))

            pool.wait_ge(s_acc, after(GROUPS * TILES))
            for constant, value in ((power_all[:, :, :], -0.5), (power[:, :, :], -0.5),
                                    (ones_r[:, :].bitcast(F32), 1.0), (zeros[:, :], 0.0)):
                nc.gpsimd.memset(constant, value).then_inc(s_ones, 1)

            def inverse_root(n, k, count, out_ap):
                pool.wait_ge(s_var, after(n + 1))
                nc.gpsimd.tensor_tensor(out=out_ap, in0=variance[:, k:k + count, :], in1=power[:, 0:count, :],
                                        op=ALU.pow).then_inc(s_rdev, 1)

            def stat_column(which, tile, count, column):
                st = stats[which][:, tile:tile + count, :] if isinstance(tile, int) else \
                    stats[which][:, bass.ds(tile, count), :]
                return st[:, :, column:column + 1]

            def ctx_split(n, b):
                pool.wait_ge(s_ctxhi, after(n + 1))
                nc.gpsimd.tensor_tensor(out=ctx_lo[:, b.slot, :, :].rearrange("p c n -> p (c n)"),
                                        in0=ctx_raw[:, b.slot, :],
                                        in1=ctx_hi[:, b.slot, :, :].rearrange("p c n -> p (c n)").bitcast(F32),
                                        op=ALU.subtract).then_inc(s_ctxlo, 1)

            pool.wait_ge(s_ones, after(2))
            pool.wait_ge(s_var, after(1))
            nc.gpsimd.tensor_tensor(out=stats[0][:, :, 1:2], in0=stats[0][:, :, 1:2], in1=power_all[:, :, :],
                                    op=ALU.pow).then_inc(s_rdev, 1)
            over_batches(pool, lambda b: ctx_split(b.index, b))
            ctx_split(BATCH, Batch(0))
            ctx_split(BATCH + 1, Batch(1))

            def pass_2(p, more):
                n = 1 + 8 * p
                for k in range(4):
                    inverse_root(n + k, 2 + k % 2, 1, rdev[:, k % 2:k % 2 + 1, :])
                    if more and k < 2:
                        ctx_split(2 * p + BATCH + 2 + k, Batch(2 + k, p))
                for k in range(4):
                    inverse_root(n + 4 + k, k % 2, 1, stat_column(1, 4 * p + k, 1, 1))

            with pool.Fori(0, PAIRS - 1) as p:
                pass_2(p, True)
            pass_2(PAIRS - 1, False)

            with pool.Fori(0, PAIRS) as p:
                for k in range(0, 4, 2):
                    inverse_root(1 + 2 * TILES + 2 * p + k // 2, k, 2, rdev[:, k:k + 2, :])

        @block.tensor
        def _(pe):
            def mm3(out_ap, left, right, first, last):
                (lh, ll), (rh, rl) = left, right
                pe.matmul(out_ap, lh, rh, start=first, stop=False, skip_group_check=True)
                pe.matmul(out_ap, lh, rl, start=False, stop=False, skip_group_check=True)
                return pe.matmul(out_ap, ll, rh, start=False, stop=last, skip_group_check=True)

            def project(ps, kind, h, b, done):
                u = unit_qk(kind, h)
                for c in range(CH):
                    w = [x[:, u, c * DH:(c + 1) * DH] for x in (w_hi, w_lo)]
                    x = [x[:, b.slot, c, :] for x in (x_hi, x_lo)]
                    mm = mm3(ps[:, 0:SEQ], w, x, c == 0, c == CH - 1)
                mm.then_inc(done, 1)

            def queries_keys(b, h, part):
                n = GH * b.all + h
                if b.first:
                    pe.wait_ge(s_wlo, after(b.hg * UNITS + unit_qk(part, h) + 1))
                pe.wait_ge(s_x, after(b.all + 1))
                pe.wait_ge(s_klo if part else s_qlo, after(n))
                project(ps_k if part else ps_q, part, h, b, s_k if part else s_q)

            def values(b, tt, part):
                n = TPB * b.all + tt
                if part == 0 and b.first:
                    pe.wait_ge(s_wlo, after(b.hg * UNITS + UNIT_V + CH))
                if part == 0:
                    pe.wait_ge(s_x, after(b.all + 1))
                    pe.wait_ge(s_vlo, after(n))
                for c in HALVES[part]:
                    x = [x[:, b.slot, c, tt * P:(tt + 1) * P] for x in (x_hi, x_lo)]
                    w = [w[:, UNIT_V + c, :] for w in (w_hi, w_lo)]
                    mm = mm3(ps_v[:, :], x, w, c == 0, c == CH - 1)
                if part == 1:
                    mm.then_inc(s_v, 1)

            def scores(b, h):
                n = GH * b.all + h
                pe.wait_ge(s_qlo, after(n + 1))
                pe.wait_ge(s_klo, after(n + 1))
                pe.wait_ge(s_exp, after(n))
                for qt in range(TPB):
                    q = [x[:, qt * P:(qt + 1) * P] for x in (q_hi, q_lo)]
                    k = [x[:, 0:(qt + 1) * P] for x in (k_hi, k_lo)]
                    mm = mm3(ps_s[:, qt * P:qt * P + (qt + 1) * P], q, k, qt == 0, qt == TPB - 1)
                mm.then_inc(s_scores, 1)

            def transposes(b, h):
                n = GH * b.all + h
                pe.wait_ge(s_norm, after(n + 1))
                pe.wait_ge(s_ptlo, after(n))
                for i in range(KEYS // P):
                    mm = pe.transpose(ps_pt[:, i * P:(i + 1) * P], probs[:, i * P:(i + 1) * P], ident[:, :])
                mm.then_inc(s_pt, 1)

            def mix(b, h):
                n = GH * b.all + h
                pe.wait_ge(s_ptlo, after(n + 1))
                pe.wait_ge(s_vlo, after(TPB * b.all + TPB))
                pe.wait_ge(s_zlo, after(n))
                for kt in range(TPB):
                    v = [x[:, b.slot, kt, h * DH:(h + 1) * DH] for x in (v_hi, v_lo)]
                    p = [x[:, 0:SEQ] if kt == 0 else x[:, SEQ:KEYS] for x in (pt_hi, pt_lo)]
                    mm = mm3(ps_z[:, kt * P:SEQ], v, p, kt == 0, kt == TPB - 1)
                mm.then_inc(s_z, 1)

            def outputs(b, tt, part):
                if part == 0:
                    if b.first:
                        pe.wait_ge(s_wlo, after(b.hg * UNITS + UNIT_O + GH))
                    pe.wait_ge(s_zlo, after(GH * b.all + GH))
                    pe.wait_ge(s_acc, after(TPB * b.all + tt))
                for h in HALVES[part]:
                    z = [x[:, b.slot, h, tt * P:(tt + 1) * P] for x in (z_hi, z_lo)]
                    w = [x[:, UNIT_O + h, :] for x in (w_hi, w_lo)]
                    mm = mm3(ps_o[:, :], z, w, h == 0, h == GH - 1)
                if part == 1:
                    mm.then_inc(s_o, 1)

            pe.wait_ge(s_primed, 1)
            for part in range(2):
                queries_keys(Batch(0), 0, part)
            for tt in range(TPB):
                for part in range(2):
                    values(Batch(0), tt, part)

            def attend(b):
                for h in range(GH):
                    scores(b, h)
                    nb, nh = (b, h + 1) if h + 1 < GH else (b.next(), 0)
                    if not (b.end and h + 1 == GH):
                        queries_keys(nb, nh, 0)
                        queries_keys(nb, nh, 1)
                    for part in range(2):
                        if h < TPB and not (b.start and b.first):
                            outputs(b.prev(), h, part)
                        if h >= TPB and not b.end:
                            values(b.next(), h - TPB, part)
                        if part == 0:
                            transposes(b, h)
                    mix(b, h)

            over_groups(pe, attend)
            for tt in range(TPB):
                for part in range(2):
                    outputs(Batch(BATCH - 1, 0, GROUPS - 1), tt, part)

            def transpose_rows(rows, slot, base):
                for c in range(CH):
                    for tt in range(TPB):
                        mm = pe.transpose(bank[base + c // 2][:, c % 2 * SEQ + tt * P:c % 2 * SEQ + (tt + 1) * P],
                                          rows[:, slot, tt, c * P:(c + 1) * P], ident[:, :])
                mm.then_inc(s_xt, 1)

            pe.wait_ge(s_acc, after(GROUPS * TILES))
            pe.wait_ge(s_const2, 32)
            for h in range(XH):
                w = wx_raw[:, 1, h * DH:(h + 1) * DH]
                mm = pe.matmul(bank[2][:, h * DH:(h + 1) * DH], w, w, start=True, stop=True, skip_group_check=True)
            mm.then_inc(s_g, 1)

            pe.wait_ge(s_ones, after(4))
            pe.wait_ge(s_tot, after(1))
            pe.matmul(bank[3][:, 0:3], ones_r[:, :].bitcast(F32), wtot[:, :], start=True, stop=True
                      ).then_inc(s_totps, 1)

            def cross_rows(b):
                pe.wait_ge(s_xn, after(b.index + 1))
                pe.wait_ge(s_xtlo, after(b.index))
                transpose_rows(xn, b.slot, 0)

            def cross_queries(b):
                pe.wait_ge(s_xtlo, after(b.index + 1))
                pe.wait_ge(s_xqlo, after(b.index))
                for h in range(XH):
                    g = [x[:, h, :] for x in (g_hi, g_lo)]
                    x = [x[:, b.slot, h, :] for x in (xt_hi, xt_lo)]
                    mm = mm3(bank[2 + h // 2][:, h % 2 * SEQ:(h % 2 + 1) * SEQ], g, x, True, True)
                mm.then_inc(s_xq, 1)

            def cross_scores(b):
                pe.wait_ge(s_xqlo, after(b.index + 1))
                pe.wait_ge(s_ctxlo, after(b.index + 1))
                for h in range(XH):
                    for kt in range(TPB):
                        c = [x[:, b.slot, h, kt * P:(kt + 1) * P] for x in (ctx_hi, ctx_lo)]
                        q = [x[:, b.slot, h, kt * P:SEQ] for x in (xq_hi, xq_lo)]
                        mm = mm3(bank[4 + h][:, kt * SEQ:kt * SEQ + SEQ - kt * P], c, q, False, b.last)
                mm.then_inc(s_xs, 1)

            cross_rows(Batch(0))
            for h in range(XH):
                pe.matmul(bank[4 + h][:, 0:KEYS], zeros[:, :], decay[:, h, :], start=True, stop=False,
                          skip_group_check=True)
            pe.wait_ge(s_glo, after(1))

            def pass_1(b):
                if not b.last:
                    cross_rows(b.next())
                cross_queries(b)
                if not b.first:
                    cross_scores(b.prev())

            over_batches_1(pe, pass_1)

            def cross_values(p, j, tt):
                pe.wait_ge(s_ctxlo, after(2 * p + BATCH + j + 1))
                for h in range(XH):
                    c = [x[:, j, h, tt * P:(tt + 1) * P] for x in (ctx_hi, ctx_lo)]
                    w = [x[:, h, :] for x in (wh_hi, wh_lo)]
                    mm = mm3(bank[2 + tt][:, h * DH:(h + 1) * DH], c, w, True, True)
                mm.then_inc(s_xv, 1)

            def rows_2(p, j):
                pe.wait_ge(s_xn, after(2 * p + BATCH + j + 1))
                transpose_rows(xn, j, 0 if isinstance(p, int) and p == 0 else 2)

            def cross_mix(p, st):
                for h in range(XH):
                    ps = bank[4 + 2 * st + h // 2][:, h % 2 * 2 * DH:(h % 2 + 1) * 2 * DH]
                    v = [x[:, :, h, :, :].rearrange("p t j e -> p t (j e)") for x in (xv_hi, xv_lo)]
                    a = [x[:, h, st * P:(st + 1) * P] for x in (a_hi, a_lo)]
                    mm3(ps, a, [x[:, 0, :] for x in v], True, False)
                    if st == 1:
                        a = [x[:, h, SEQ:KEYS] for x in (a_hi, a_lo)]
                        mm = mm3(ps, a, [x[:, 1, :] for x in v], False, True)
                    else:
                        pe.matmul(ps, ones_r[:, :], v[0][:, 1, :], start=False, stop=False, skip_group_check=True)
                        mm = pe.matmul(ps, ones_r[:, :], v[1][:, 1, :], start=False, stop=True,
                                       skip_group_check=True)
                mm.then_inc(s_xo, 1)

            def gate_rows(p, k):
                pe.wait_ge(s_xtlo, after(2 * p + BATCH + k // 2 + 1))
                pe.wait_ge(s_relu, after(4 * p + k))
                for c in range(CH):
                    x = [x[:, k // 2, c, k % 2 * P:(k % 2 + 1) * P] for x in (xt_hi, xt_lo)]
                    mm = mm3(bank[0], x, [x[:, 0, c, :] for x in (wgo_hi, wgo_lo)], c == 0, c == CH - 1)
                mm.then_inc(s_gate, 1)

            def turn_wy(p, k):
                pe.wait_ge(s_wy, after(4 * p + k + 1))
                for c in range(CH):
                    mm = pe.transpose(bank[2 + k % 2][:, c * P:(c + 1) * P], gate[:, k, c * P:(c + 1) * P],
                                      ident[:, :])
                mm.then_inc(s_wyt, 1)

            def cross_output(p, k):
                pe.wait_ge(s_wytlo, after(4 * p + k + 1))
                pe.wait_ge(s_res, after(4 * p + k))
                for c in range(CH):
                    mm = mm3(bank[1], [x[:, k % 2, c, :] for x in (wyt_hi, wyt_lo)],
                             [x[:, 1, c, :] for x in (wgo_hi, wgo_lo)], c == 0, c == CH - 1)
                mm.then_inc(s_xout, 1)

            pe.wait_ge(s_xtlo, after(BATCH))
            rows_2(0, 0)
            cross_scores(Batch(BATCH - 1))
            pe.wait_ge(s_wh, after(1))
            pe.wait_ge(s_xqlo, after(BATCH))
            cross_values(0, 0, 0)
            cross_values(0, 0, 1)
            pe.wait_ge(s_xtlo, after(BATCH + 1))
            rows_2(0, 1)
            pe.wait_ge(s_xvlo, after(2))
            cross_values(0, 1, 0)
            cross_values(0, 1, 1)
            pe.wait_ge(s_xtlo, after(BATCH + 2))
            pe.wait_ge(s_alo, after(1))
            pe.wait_ge(s_golo, after(1))

            def pass_2(p, more):
                pe.wait_ge(s_xvlo, after(4 * p + 4))
                pe.wait_ge(s_yc, after(4 * p))
                cross_mix(p, 0)
                cross_mix(p, 1)
                gate_rows(p, 0)
                pe.wait_ge(s_xtlo, after(2 * p + BATCH + 2))
                if more:
                    cross_values(p + 1, 0, 0)
                    cross_values(p + 1, 0, 1)
                gate_rows(p, 1)
                if more:
                    pe.wait_ge(s_xvlo, after(4 * p + 6))
                    rows_2(p + 1, 0)
                gate_rows(p, 2)
                if more:
                    pe.wait_ge(s_xtlo, after(2 * p + BATCH + 3))
                    cross_values(p + 1, 1, 0)
                    cross_values(p + 1, 1, 1)
                gate_rows(p, 3)
                if more:
                    pe.wait_ge(s_xvlo, after(4 * p + 8))
                turn_wy(p, 0)
                turn_wy(p, 1)
                pe.wait_ge(s_golo, after(2))
                cross_output(p, 0)
                turn_wy(p, 2)
                cross_output(p, 1)
                turn_wy(p, 3)
                cross_output(p, 2)
                if more:
                    pe.wait_ge(s_wytlo, after(4 * p + 4))
                    rows_2(p + 1, 1)
                cross_output(p, 3)

            with pe.Fori(0, PAIRS - 1) as p:
                pass_2(p, True)
            pass_2(PAIRS - 1, False)

            pe.wait_ge(s_res, after(TILES))

            def rows_3(p, j):
                pe.wait_ge(s_xn, after(2 * p + 2 * BATCH + j + 1))
                transpose_rows(xn2, j, 2 - 2 * j)

            def up(p, f, first):
                if first:
                    pe.wait_ge(s_fw, after(3 * f + 2))
                if f >= 2:
                    pe.wait_ge(s_hid, after(FC * p + f - 1))
                else:
                    pe.wait_ge(s_xtlo, after(2 * p + 2 * BATCH + 2))
                for m in range(2):
                    for c in range(CH):
                        w = f_w[:, 3 * f + m, c * P:(c + 1) * P]
                        for i, x in enumerate((xt2_hi, xt2_lo)):
                            mm = pe.matmul(bank[f % 2 * 2 + m].rearrange("p (j n) -> p j n", j=2), w, x[:, :, c, :],
                                           start=(c == 0 and i == 0), stop=(c == CH - 1 and i == 1),
                                           skip_group_check=True)
                mm.then_inc(s_up, 1)

            def down(p, f, first):
                if first:
                    pe.wait_ge(s_fw, after(3 * f + 3))
                pe.wait_ge(s_hlo, after(FC * p + f + 1))
                if f == 0:
                    pe.wait_ge(s_y3, after(4 * p))
                for k in range(4):
                    for i, x in enumerate((hid_hi, hid_lo)):
                        mm = pe.matmul(bank[4 + k], x[:, f % 2, k * P:(k + 1) * P], f_w[:, 3 * f + 2, :],
                                       start=(f == 0 and i == 0), stop=(f == FC - 1 and i == 1),
                                       skip_group_check=True)
                mm.then_inc(s_down, 1)

            rows_3(0, 0)
            rows_3(0, 1)
            pe.wait_ge(s_thr, after(1))

            def pass_3(p, first, more):
                for f in range(FC):
                    up(p, f, first)
                    if more and f == FC - 1:
                        pe.wait_ge(s_hid, after(FC * p + FC - 1))
                        rows_3(p + 1, 0)
                    if f >= 1:
                        down(p, f - 1, first)
                if more:
                    pe.wait_ge(s_hid, after(FC * p + FC))
                    rows_3(p + 1, 1)
                down(p, FC - 1, first)

            pass_3(0, True, True)
            with pe.Fori(1, PAIRS - 1) as p:
                pass_3(p, False, True)
            pass_3(PAIRS - 1, False, False)

        SCALE = float(DH) ** -0.5

        @block.scalar
        def _(act):
            def split_w(hg, u):
                act.wait_ge(s_wdma[u % RING], (hg * (UNITS // RING) + u // RING + 1) * 16)
                if not isinstance(hg, int) or hg:
                    if u >= UNIT_O:
                        act.wait_ge(s_o, after(hg * TILES))
                    elif UNIT_V <= u < UNIT_V + CH:
                        act.wait_ge(s_v, after(hg * TILES))
                    else:
                        head = 0 if u < UNIT_V else 1 + (u - UNIT_V - CH) // 2
                        act.wait_ge(s_k, after(hg * STEPS - GH + head + 1))
                nc.scalar.copy(w_hi[:, u, :], w_raw[:, u % RING, :]).then_inc(s_whi, 1)

            def qk_hi(b, h, part):
                n = GH * b.all + h
                act.wait_ge(s_k if part else s_q, after(n + 1))
                act.wait_ge(s_scores, after(n))
                act.nop(nofuse=True)
                nc.scalar.activation((k_hi if part else q_hi)[:, :], (ps_k if part else ps_q)[:, 0:SEQ],
                                     ACT.Identity, bias=bias_of(b, part, h)
                                     ).then_inc(s_khi if part else s_qhi, 1)

            def v_split(b, tt):
                act.wait_ge(s_v, after(TPB * b.all + tt + 1))
                if not b.start:
                    act.wait_ge(s_z, after(GH * (b.all - 1)))
                nc.scalar.copy(v_hi[:, b.slot, tt, :], ps_v[:, :]).then_inc(s_vhi, 1)

            def exps(b, h):
                n = GH * b.all + h
                act.wait_ge(s_max, after(TPB * (n + 1)))
                act.wait_ge(s_pt, after(n))
                nc.scalar.activation(probs[:, 0:P], ps_s[:, 0:P], ACT.Exp, bias=negmax[:, 0:1], scale=-1.0,
                                     accum_out=rowsum[:, 0:1])
                nc.scalar.activation(probs[:, P:KEYS], ps_s[:, P:KEYS], ACT.Exp, bias=negmax[:, 1:2],
                                     scale=-1.0, accum_out=rowsum[:, 1:2]).then_inc(s_exp, 1)

            def pt_split(b, h):
                n = GH * b.all + h
                act.wait_ge(s_pt, after(n + 1))
                act.wait_ge(s_z, after(n))
                nc.scalar.copy(pt_hi[:, :], ps_pt[:, 0:KEYS]).then_inc(s_pthi, 1)

            def z_split(b, h):
                n = GH * b.all + h
                act.wait_ge(s_z, after(n + 1))
                if not b.start:
                    act.wait_ge(s_o, after(TPB * (b.all - 1)))
                act.nop(nofuse=True)
                nc.scalar.activation(z_hi[:, b.slot, h, :], ps_z[:, 0:SEQ], ACT.Identity,
                                     bias=bias_of(b, 2, h)).then_inc(s_zhi, 1)

            def sum_abs(b):
                act.wait_ge(s_absdma[b.slot], (PAIRS * b.hg + b.half + 1) * 16)
                for m in range(3):
                    piece = w_abs[:, b.slot, m * ABS_COLS:(m + 1) * ABS_COLS]
                    mm = nc.scalar.activation(piece, piece, ACT.Abs, accum_out=pick(wsum, b.all)[:, m:m + 1])
                mm.then_inc(s_abs, 1)

            act.wait_ge(s_primed, 1)
            act.wait_ge(s_const, 64)
            for u in SPLIT_BEFORE[:6]:
                split_w(0, u)
            qk_hi(Batch(0), 0, 0)
            qk_hi(Batch(0), 0, 1)
            for tt in range(TPB):
                v_split(Batch(0), tt)
            for u in SPLIT_BEFORE[6:]:
                split_w(0, u)

            def attend(b):
                for h in range(GH):
                    exps(b, h)
                    for u in SPLIT_FIRST[h] if b.first else ():
                        split_w(b.hg, u)
                    for u in SPLIT_LAST[h] if b.last and not b.end else ():
                        split_w(b.hg + 1, u)
                    if not (b.end and h + 1 == GH):
                        nb, nh = (b, h + 1) if h + 1 < GH else (b.next(), 0)
                        qk_hi(nb, nh, 0)
                        qk_hi(nb, nh, 1)
                    pt_split(b, h)
                    if h >= TPB and not b.end:
                        v_split(b.next(), h - TPB)
                    z_split(b, h)
                    if h == 0:
                        sum_abs(b)

            over_groups(act, attend)

            act.wait_ge(s_acc, after(GROUPS * TILES))
            act.wait_ge(s_const2, 32)

            def ctx_split(n, b):
                act.wait_ge(s_ctxdma[b.slot], (n // 2 + 1) * 16 if isinstance(n, int) else
                            (b.half + 1) * 16 if n is b.index else (b.half + 1 + PAIRS) * 16)
                nc.scalar.copy(ctx_hi[:, b.slot, :, :].rearrange("p c n -> p (c n)"), ctx_raw[:, b.slot, :]
                               ).then_inc(s_ctxhi, 1)

            def split_banks(hi, base, done):
                nc.scalar.copy(hi, psum[:, base:base + 2, :]).then_inc(done, 1)

            def xt_split(n, slot, base):
                act.wait_ge(s_xt, after(n + 1))
                split_banks(xt_hi[:, slot, :, :].rearrange("p (a c) n -> p a (c n)", a=2), base, s_xthi)

            def xq_split(b):
                act.wait_ge(s_xq, after(b.index + 1))
                if not b.start:
                    act.wait_ge(s_xs, after(b.index - 1))
                split_banks(xq_hi[:, b.slot, :, :].rearrange("p (a h) n -> p a (h n)", a=2), 2, s_xqhi)

            act.wait_ge(s_g, after(1))
            nc.scalar.copy(g_hi[:, :, :].rearrange("p h e -> p (h e)"), bank[2]).then_inc(s_ghi, 1)
            nc.scalar.copy(wh_hi[:, :, :].rearrange("p h e -> p (h e)"), wx_raw[:, 0, :]).then_inc(s_whsplit, 1)
            xt_split(0, 0, 0)

            def pass_1(b):
                if not b.start:
                    act.wait_ge(s_xs, after(b.index - 1))
                ctx_split(b.index, b)
                if not b.last:
                    if not b.first:
                        act.wait_ge(s_xq, after(b.index))
                    xt_split(b.next().index, b.next().slot, 0)
                xq_split(b)

            over_batches_1(act, pass_1)
            act.wait_ge(s_xs, after(BATCH - 1))
            ctx_split(BATCH, Batch(0))
            act.wait_ge(s_xq, after(BATCH - 1))
            xt_split(BATCH, 0, 0)
            act.wait_ge(s_xs, after(BATCH))
            ctx_split(BATCH + 1, Batch(1))
            act.wait_ge(s_araw, after(3))
            nc.scalar.copy(a_hi[:, :, :], a_raw[:, :, :]).then_inc(s_ahi, 1)

            def xv_split(p, j, tt):
                act.wait_ge(s_xv, after(4 * p + 2 * j + tt + 1))
                act.wait_ge(s_xo, after(2 * p))
                nc.scalar.copy(xv_hi[:, tt, :, j, :], bank[2 + tt].rearrange("p (h e) -> p h e", h=XH)
                               ).then_inc(s_xvhi, 1)

            def keep_rows(n, rows, j, p):
                act.wait_ge(s_xn, after(n + 1))
                nc.scalar.copy(pick(acc, 4 * p + 2 * j, TPB), rows[:, j, :, :]).then_inc(s_back, 1)

            def relu(p, k):
                act.wait_ge(s_gate, after(4 * p + k + 1))
                act.wait_ge(s_wyt, after(4 * p))
                act.wait_ge(s_golo, after(2))
                nc.scalar.activation(gate[:, k, :], bank[0], ACT.Relu).then_inc(s_relu, 1)

            def wyt_split(p, k):
                act.wait_ge(s_wyt, after(4 * p + k + 1))
                act.wait_ge(s_xout, after(4 * p + k - 1) if k else after(4 * p))
                nc.scalar.copy(wyt_hi[:, k % 2, :, :].rearrange("p c n -> p (c n)"), bank[2 + k % 2]
                               ).then_inc(s_wythi, 1)

            for tt in range(TPB):
                xv_split(0, 0, tt)
            keep_rows(BATCH, xn, 0, 0)
            for tt in range(TPB):
                xv_split(0, 1, tt)
            act.wait_ge(s_gdma, 48)
            nc.scalar.copy(wgo_hi[:, 0, :, :], wgo_raw[:, :, :]).then_inc(s_gohi, 1)
            xt_split(BATCH + 1, 1, 0)
            keep_rows(BATCH + 1, xn, 1, 0)
            act.wait_ge(s_odma, 16)
            nc.scalar.copy(wgo_hi[:, 1, :, :], wgo_raw[:, :, :]).then_inc(s_gohi, 1)

            def pass_2(p, more):
                if more:
                    for j in range(2):
                        act.wait_ge(s_xv, after(4 * p + 2 * j + 2))
                        ctx_split(2 * p + BATCH + 2 + j, Batch(2 + j, p))
                relu(p, 0)
                if more:
                    xv_split(p + 1, 0, 0)
                    xv_split(p + 1, 0, 1)
                relu(p, 1)
                if more:
                    xt_split(2 * p + BATCH + 2, 0, 2)
                    keep_rows(2 * p + BATCH + 2, xn, 0, p + 1)
                relu(p, 2)
                if more:
                    xv_split(p + 1, 1, 0)
                    xv_split(p + 1, 1, 1)
                relu(p, 3)
                for k in range(4):
                    wyt_split(p, k)
                if more:
                    xt_split(2 * p + BATCH + 3, 1, 2)
                    keep_rows(2 * p + BATCH + 3, xn, 1, p + 1)

            with act.Fori(0, PAIRS - 1) as p:
                pass_2(p, True)
            pass_2(PAIRS - 1, False)

            def xt2_split(p, j):
                act.wait_ge(s_xt, after(2 * p + 2 * BATCH + j + 1))
                split_banks(xt2_hi[:, j, :, :].rearrange("p (a c) n -> p a (c n)", a=2), 2 - 2 * j, s_xthi)

            def hidden(p, f):
                n = FC * p + f
                act.wait_ge(s_up, after(n + 1))
                act.wait_ge(s_hid, after(n - min(f, 1)))
                nc.scalar.activation(sig[:, f % 2, :], bank[f % 2 * 2], ACT.Sigmoid).then_inc(s_sig, 1)
                act.wait_ge(s_hid, after(n + 1))
                act.wait_ge(s_down, after(n - min(f, 1)))
                nc.scalar.copy(hid_hi[:, f % 2, :], hid[:, f % 2, :]).then_inc(s_hhi, 1)

            for j in range(2):
                xt2_split(0, j)
                keep_rows(2 * BATCH + j, xn2, j, 0)

            def pass_3(p, more):
                for f in range(FC):
                    hidden(p, f)
                    if more and f in (6, 7):
                        keep_rows(2 * p + 2 * BATCH + 2 + f - 6, xn2, f - 6, p + 1)
                if more:
                    for j in range(2):
                        xt2_split(p + 1, j)

            with act.Fori(0, PAIRS - 1) as p:
                pass_3(p, True)
            pass_3(PAIRS - 1, False)

        @block.vector
        def _(dve):
            def split_w(hg, u):
                dve.wait_ge(s_whi, after(hg * UNITS + u + 1))
                nc.vector.tensor_tensor(out=w_lo[:, u, :], in0=w_raw[:, u % RING, :],
                                        in1=w_hi[:, u, :].bitcast(F32), op=ALU.subtract).then_inc(s_wlo, 1)

            def low(out_ap, ps, bias_ap, hi_ap, done):
                nc.vector.scalar_tensor_tensor(out=out_ap, in0=ps, scalar=bias_ap, in1=hi_ap.bitcast(F32),
                                               op0=ALU.add, op1=ALU.subtract).then_inc(done, 1)

            def qk_lo(b, h, part):
                n = GH * b.all + h
                dve.wait_ge(s_khi if part else s_qhi, after(n + 1))
                low((k_lo if part else q_lo)[:, :], (ps_k if part else ps_q)[:, 0:SEQ], bias_of(b, part, h),
                    (k_hi if part else q_hi)[:, :], s_klo if part else s_qlo)

            def v_split(b, tt):
                dve.wait_ge(s_vhi, after(TPB * b.all + tt + 1))
                nc.vector.tensor_tensor(out=v_lo[:, b.slot, tt, :], in0=ps_v[:, :],
                                        in1=v_hi[:, b.slot, tt, :].bitcast(F32),
                                        op=ALU.subtract).then_inc(s_vlo, 1)

            def row_max(b, h):
                n = GH * b.all + h
                dve.wait_ge(s_scores, after(n + 1))
                dve.nop(nofuse=True)
                for qt in range(TPB):
                    s = ps_s[:, qt * P:qt * P + (qt + 1) * P]
                    nc.vector.tensor_tensor_reduce(s, s, mask[:, SEQ - (qt + 1) * P:SEQ], -SCALE, 3e38,
                                                   ALU.add, ALU.min, negmax[:, qt:qt + 1]).then_inc(s_max, 1)

            def normalise(b, h):
                n = GH * b.all + h
                dve.wait_ge(s_exp, after(n + 1))
                nc.vector.reciprocal(inv[:, :], rowsum[:, :]).then_inc(s_inv, 1)
                dve.wait_ge(s_inv, after(n + 1))
                nc.vector.tensor_scalar(probs[:, 0:P], probs[:, 0:P], inv[:, 0:1], None, ALU.mult)
                nc.vector.tensor_scalar(probs[:, P:KEYS], probs[:, P:KEYS], inv[:, 1:2], None,
                                        ALU.mult).then_inc(s_norm, 1)

            def pt_split(b, h):
                n = GH * b.all + h
                dve.wait_ge(s_pthi, after(n + 1))
                nc.vector.tensor_tensor(out=pt_lo[:, :], in0=ps_pt[:, 0:KEYS], in1=pt_hi[:, :].bitcast(F32),
                                        op=ALU.subtract).then_inc(s_ptlo, 1)

            def z_split(b, h):
                n = GH * b.all + h
                dve.wait_ge(s_zhi, after(n + 1))
                low(z_lo[:, b.slot, h, :], ps_z[:, 0:SEQ], bias_of(b, 2, h), z_hi[:, b.slot, h, :], s_zlo)

            def add_output(b, tt):
                n = TPB * b.index + tt
                dve.wait_ge(s_o, after(TPB * b.all + tt + 1))
                dve.wait_ge(s_bo, after(n + 1))
                nc.vector.tensor_tensor(out=pick(acc, n), in0=ps_o[:, :], in1=pick(acc, n), op=ALU.add
                                        ).then_inc(s_acc, 1)

            def row_stats(n, k, ins):
                dve.nop(nofuse=True)
                for i, a in enumerate(ins):
                    nc.vector.bn_stats(bn_raw[:, k + i, :], a).then_inc(s_bn, 1)
                dve.wait_ge(s_bn, after(n + len(ins)))
                dve.nop(nofuse=True)
                for i in range(len(ins)):
                    nc.vector.bn_aggr(bn[:, k + i, :], bn_raw[:, k + i, :]).then_inc(s_aggr, 1)
                dve.wait_ge(s_aggr, after(n + len(ins)))

            def stats_1(b):
                n = TPB * b.index
                dve.wait_ge(s_acc, after(TPB * b.all + TPB))
                row_stats(n, 0, [pick(acc, n + tt) for tt in range(TPB)])
                st = stats[0][:, n:n + TPB, :] if isinstance(n, int) else stats[0][:, bass.ds(n, TPB), :]
                nc.vector.tensor_copy(st, bn[:, 0:TPB, :]).then_inc(s_mean, 1)

            dve.wait_ge(s_primed, 1)
            dve.wait_ge(s_const, 64)
            for u in SPLIT_BEFORE[:6]:
                split_w(0, u)
            qk_lo(Batch(0), 0, 0)
            qk_lo(Batch(0), 0, 1)
            for tt in range(TPB):
                v_split(Batch(0), tt)
            for u in SPLIT_BEFORE[6:]:
                split_w(0, u)

            def attend(b):
                for h in range(GH):
                    row_max(b, h)
                    for u in SPLIT_FIRST[h] if b.first else ():
                        split_w(b.hg, u)
                    for u in SPLIT_LAST[h] if b.last and not b.end else ():
                        split_w(b.hg + 1, u)
                    more = not (b.end and h + 1 == GH)
                    nb, nh = (b, h + 1) if h + 1 < GH else (b.next(), 0)
                    if more:
                        qk_lo(nb, nh, 0)
                    normalise(b, h)
                    if more:
                        qk_lo(nb, nh, 1)
                    pt_split(b, h)
                    if h < TPB:
                        if not (b.start and b.first):
                            add_output(b.prev(), h)
                    elif not b.end:
                        v_split(b.next(), h - TPB)
                    z_split(b, h)
                    if h == TPB and isinstance(b.hg, int) and b.hg == GROUPS - 1 and not b.first:
                        stats_1(b.prev())

            over_groups(dve, attend)
            b = Batch(BATCH - 1, 0, GROUPS - 1)
            for tt in range(TPB):
                add_output(b, tt)
            stats_1(b)
            dve.wait_ge(s_mean, after(BATCH))
            nc.vector.tensor_scalar(stats[0][:, :, 1:2], stats[0][:, :, 1:2], LN_EPS, None, ALU.add
                                    ).then_inc(s_var, 1)

            def minus(out_ap, a, hi, done):
                nc.vector.tensor_tensor(out=out_ap, in0=a, in1=hi.bitcast(F32), op=ALU.subtract).then_inc(done, 1)

            def row_variance(n, event, lag, k, ins, eps):
                row_stats(n, k, ins)
                dve.wait_ge(s_rdev, after(event + 1 - lag))
                nc.vector.tensor_scalar(variance[:, k:k + len(ins), :], bn[:, k:k + len(ins), 1:2], eps, None, ALU.add
                                        ).then_inc(s_var, 1)

            def sum_stats(which, n, event, lag, tile, k, count):
                row_variance(n, event, lag, k, [pick(acc, tile + i) for i in range(count)], LN_EPS)
                st = stats[which][:, tile:tile + count, :] if isinstance(tile, int) else \
                    stats[which][:, bass.ds(tile, count), :]
                nc.vector.tensor_copy(st[:, :, 0:1], bn[:, k:k + count, 0:1]).then_inc(s_mean, 1)

            def normal_rows(which, tile, rows, slot):
                for tt in range(TPB):
                    st = pick(stats[which], tile + tt)
                    last = nc.vector.tensor_scalar(rows[:, slot, tt, :], pick(acc, tile + tt), st[:, 0:1], st[:, 1:2],
                                                   ALU.subtract, ALU.mult)
                last.then_inc(s_xn, 1)

            def norm_1(b):
                if not b.start:
                    dve.wait_ge(s_xt, after(b.index - 1))
                normal_rows(0, TPB * b.index, xn, b.slot)

            def xt_low(n, slot, base, hi, lo):
                dve.wait_ge(s_xthi, after(n + 1))
                minus(lo[:, slot, :, :].rearrange("p (a c) n -> p a (c n)", a=2), psum[:, base:base + 2, :],
                      hi[:, slot, :, :].rearrange("p (a c) n -> p a (c n)", a=2), s_xtlo)

            def xq_low(b):
                dve.wait_ge(s_xqhi, after(b.index + 1))
                minus(xq_lo[:, b.slot, :, :].rearrange("p (a h) n -> p a (h n)", a=2), psum[:, 2:4, :],
                      xq_hi[:, b.slot, :, :].rearrange("p (a h) n -> p a (h n)", a=2), s_xqlo)

            dve.wait_ge(s_rdev, after(1))
            norm_1(Batch(0))
            norm_1(Batch(1))
            dve.wait_ge(s_abs, after(GROUPS * BATCH))
            nc.vector.tensor_reduce(wtot[:, :], wsum[:, :, :].rearrange("p b m -> p m b"), AX_X, ALU.add).then_inc(s_tot, 1)
            dve.wait_ge(s_totps, after(1))
            for i, sign in enumerate((0.5, -0.5)):
                nc.vector.tensor_scalar(thr[:, i, :], bank[3][:, 0:3], 1.0 / (DIM * FF), 1e-8, ALU.mult, ALU.add
                                        ).then_inc(s_thr, 1)
            dve.wait_ge(s_thr, after(2))
            for i, sign in enumerate((0.5, -0.5)):
                nc.vector.tensor_scalar(thr[:, i, :], thr[:, i, :], sign, None, ALU.mult).then_inc(s_thr, 1)
            dve.wait_ge(s_thr, after(4))
            dve.wait_ge(s_ghi, after(1))
            minus(g_lo[:, :, :].rearrange("p h e -> p (h e)"), bank[2],
                  g_hi[:, :, :].rearrange("p h e -> p (h e)"), s_glo)
            xt_low(0, 0, 0, xt_hi, xt_lo)
            dve.wait_ge(s_whsplit, after(1))
            minus(wh_lo[:, :, :].rearrange("p h e -> p (h e)"), wx_raw[:, 0, :],
                  wh_hi[:, :, :].rearrange("p h e -> p (h e)"), s_wh)

            def pass_1(b):
                if not b.last:
                    xt_low(b.next().index, b.next().slot, 0, xt_hi, xt_lo)
                xq_low(b)
                if isinstance(b.index, int) and b.index >= BATCH - 2:
                    dve.wait_ge(s_xt, after(b.index + 1))
                    normal_rows(0, TPB * b.slot, xn, b.slot)
                else:
                    norm_1(b.next().next())

            over_batches_1(dve, pass_1)

            dve.wait_ge(s_xs, after(BATCH))
            nc.vector.tensor_tensor(out=a_raw[:, :, :], in0=psum[:, 4:8, 0:KEYS], in1=decay[:, :, :],
                                    op=ALU.mult).then_inc(s_araw, 1)
            dve.wait_ge(s_araw, after(1))
            flat = a_raw[:, :, :].rearrange("p h n -> p (h n)")
            nc.vector.scalar_tensor_tensor(out=flat, in0=flat, scalar=-1.0, in1=flat, op0=ALU.mult, op1=ALU.max
                                           ).then_inc(s_araw, 1)
            dve.wait_ge(s_araw, after(2))
            nc.vector.tensor_scalar(flat, flat, 1.0, None, ALU.max).then_inc(s_araw, 1)

            def norm_2(p, j):
                n = 2 * p + j
                dve.wait_ge(s_xt, after(n + BATCH - 1))
                dve.wait_ge(s_back, after(n - 1))
                normal_rows(0, TPB * n, xn, j)

            def xv_low(p, j, tt):
                dve.wait_ge(s_xvhi, after(4 * p + 2 * j + tt + 1))
                minus(xv_lo[:, tt, :, j, :], bank[2 + tt].rearrange("p (h e) -> p h e", h=XH),
                      xv_hi[:, tt, :, j, :], s_xvlo)

            xt_low(BATCH, 0, 0, xt_hi, xt_lo)
            for tt in range(TPB):
                xv_low(0, 0, tt)
            for tt in range(TPB):
                xv_low(0, 1, tt)
            dve.wait_ge(s_ahi, after(1))
            minus(a_lo[:, :, :], a_raw[:, :, :], a_hi[:, :, :], s_alo)
            dve.wait_ge(s_gohi, after(1))
            minus(wgo_lo[:, 0, :, :], wgo_raw[:, :, :], wgo_hi[:, 0, :, :], s_golo)
            xt_low(BATCH + 1, 1, 0, xt_hi, xt_lo)
            dve.wait_ge(s_gohi, after(2))
            minus(wgo_lo[:, 1, :, :], wgo_raw[:, :, :], wgo_hi[:, 1, :, :], s_golo)

            N1 = TILES
            S1 = 1

            def group(p, k):
                return psum[:, 4 + 2 * (k % 2):6 + 2 * (k % 2), :].rearrange(
                    "p a (h j e) -> p (a h) j e", h=2, j=2)[:, :, k // 2, :]

            def group_stats(p, k):
                dve.wait_ge(s_xo, after(2 * p + k % 2 + 1))
                row_variance(8 * p + N1 + k, 8 * p + S1 + k, 2, 2 + k % 2, [group(p, k)], GN_EPS)

            def group_norm(p, k):
                y = y_raw[:, k % 2, :]
                nc.vector.scalar_tensor_tensor(out=y.rearrange("p (h e) -> p h e", h=XH), in0=group(p, k),
                                               scalar=bn[:, 2 + k % 2, 0:1],
                                               in1=gamma[:, :].rearrange("p (h e) -> p h e", h=XH),
                                               op0=ALU.subtract, op1=ALU.mult).then_inc(s_yc, 1)
                dve.wait_ge(s_yc, after(4 * p + k + 1))
                dve.wait_ge(s_rdev, after(8 * p + S1 + k + 1))
                nc.vector.scalar_tensor_tensor(out=y, in0=y, scalar=rdev[:, k % 2, 0:1], in1=beta[:, :],
                                               op0=ALU.mult, op1=ALU.add).then_inc(s_ys, 1)

            def gated(p, k):
                dve.wait_ge(s_relu, after(4 * p + k + 1))
                dve.wait_ge(s_ys, after(4 * p + k + 1))
                nc.vector.tensor_tensor(out=gate[:, k, :], in0=gate[:, k, :], in1=y_raw[:, k % 2, :],
                                        op=ALU.mult).then_inc(s_wy, 1)

            def wyt_low(p, k):
                dve.wait_ge(s_wythi, after(4 * p + k + 1))
                minus(wyt_lo[:, k % 2, :, :].rearrange("p c n -> p (c n)"), bank[2 + k % 2],
                      wyt_hi[:, k % 2, :, :].rearrange("p c n -> p (c n)"), s_wytlo)

            def residual(p, k):
                tile = 4 * p + k
                dve.wait_ge(s_back, after(2 * p + k // 2 + 1))
                dve.wait_ge(s_xout, after(tile + 1))
                a = pick(acc, tile)
                nc.vector.tensor_tensor(out=a, in0=bank[1], in1=a, op=ALU.add).then_inc(s_res, 1)
                dve.wait_ge(s_res, after(tile + 1))
                sum_stats(1, 8 * p + N1 + 4 + k, 8 * p + S1 + 4 + k, 2, tile, k % 2, 1)

            def pass_2(p, more):
                group_stats(p, 0)
                group_stats(p, 1)
                group_norm(p, 0)
                gated(p, 0)
                group_norm(p, 1)
                if more:
                    xv_low(p + 1, 0, 0)
                    xv_low(p + 1, 0, 1)
                    norm_2(p + 1, 0)
                gated(p, 1)
                group_stats(p, 2)
                group_stats(p, 3)
                group_norm(p, 2)
                if more:
                    xt_low(2 * p + BATCH + 2, 0, 2, xt_hi, xt_lo)
                    norm_2(p + 1, 1)
                group_norm(p, 3)
                if more:
                    xv_low(p + 1, 1, 0)
                    xv_low(p + 1, 1, 1)
                wyt_low(p, 0)
                wyt_low(p, 1)
                gated(p, 2)
                gated(p, 3)
                residual(p, 0)
                wyt_low(p, 2)
                residual(p, 1)
                wyt_low(p, 3)
                residual(p, 2)
                if more:
                    xt_low(2 * p + BATCH + 3, 1, 2, xt_hi, xt_lo)
                residual(p, 3)

            with dve.Fori(0, PAIRS - 1) as p:
                pass_2(p, True)
            pass_2(PAIRS - 1, False)

            N2, S2 = 3 * TILES, 1 + 2 * TILES

            def norm_3(p, j):
                n = 2 * p + j
                if not (isinstance(p, int) and p == 0):
                    dve.wait_ge(s_xt, after(n + 2 * BATCH - 1))
                    dve.wait_ge(s_back, after(n + BATCH - 1))
                else:
                    dve.wait_ge(s_rdev, after(S2))
                    dve.wait_ge(s_mean, after(BATCH + TILES))
                normal_rows(1, TPB * n, xn2, j)

            norm_3(0, 0)
            norm_3(0, 1)
            def ternary(u):
                m = u % 3
                dve.wait_ge(s_fdma[u % RING], (u // RING + 1) * 16)
                nc.vector.tensor_scalar(f_neg[:, u % 2, :], f_raw[:, u % RING, :], thr[:, 1, m:m + 1], None,
                                        ALU.is_lt).then_inc(s_neg, 1)
                dve.wait_ge(s_neg, after(u + 1))
                nc.vector.scalar_tensor_tensor(out=f_w[:, u, :], in0=f_raw[:, u % RING, :],
                                               scalar=thr[:, 0, m:m + 1], in1=f_neg[:, u % 2, :],
                                               op0=ALU.is_gt, op1=ALU.subtract).then_inc(s_fw, 1)

            def hidden(p, f):
                n = FC * p + f
                dve.wait_ge(s_sig, after(n + 1))
                dve.wait_ge(s_hhi, after(n - min(f, 1)))
                nc.vector.tensor_tensor(out=hid[:, f % 2, :], in0=bank[f % 2 * 2 + 1], in1=sig[:, f % 2, :],
                                        op=ALU.mult).then_inc(s_hid, 1)

            def hidden_low(p, f):
                dve.wait_ge(s_hhi, after(FC * p + f + 1))
                minus(hid_lo[:, f % 2, :], hid[:, f % 2, :], hid_hi[:, f % 2, :], s_hlo)

            def finish(p):
                dve.wait_ge(s_down, after(FC * p + FC))
                dve.wait_ge(s_yout, after(64 * p))
                for k in range(4):
                    dve.wait_ge(s_back, after(2 * p + BATCH + k // 2 + 1))
                    nc.vector.tensor_tensor(out=y3[:, k, :], in0=bank[4 + k], in1=pick(acc, 4 * p + k), op=ALU.add
                                            ).then_inc(s_y3, 1)
                dve.wait_ge(s_y3, after(4 * p + 4))
                for k in range(0, 4, 2):
                    row_variance(4 * p + N2 + k, 2 * p + S2 + k // 2, 2, k, [y3[:, k + i, :] for i in range(2)], LN_EPS)
                for k in range(4):
                    dve.wait_ge(s_rdev, after(2 * p + S2 + k // 2 + 1))
                    nc.vector.tensor_scalar(y3[:, k, :], y3[:, k, :], bn[:, k, 0:1], rdev[:, k, 0:1],
                                            ALU.subtract, ALU.mult).then_inc(s_y3n, 1)

            xt_low(2 * BATCH, 0, 2, xt2_hi, xt2_lo)
            xt_low(2 * BATCH + 1, 1, 0, xt2_hi, xt2_lo)

            def pass_3(p, first, more):
                if first:
                    for u in range(3):
                        ternary(u)
                for f in range(FC):
                    if first and f + 1 < FC:
                        for m in range(3):
                            ternary(3 * (f + 1) + m)
                    hidden(p, f)
                    hidden_low(p, f)
                    if more and f in (4, 5):
                        norm_3(p + 1, f - 4)
                if more:
                    for j in range(2):
                        xt_low(2 * p + 2 * BATCH + 2 + j, j, 2 - 2 * j, xt2_hi, xt2_lo)
                finish(p)

            pass_3(0, True, True)
            with dve.Fori(1, PAIRS - 1) as p:
                pass_3(p, False, True)
            pass_3(PAIRS - 1, False, False)


def kernel(**inputs):
    import numpy as _np
    import concourse.bacc as _bacc
    from concourse import mybir as _mybir
    from concourse.bass_utils import run_bass_kernel_spmd as _run

    i = {k: _np.asarray(v) for k, v in inputs.items()}
    groups = []
    for g in range(GROUPS):
        hs = range(g * GH, (g + 1) * GH)
        q = [i["L0_attn_W_Q"][h].reshape(CH, P, DH).transpose(1, 0, 2).reshape(P, 512) for h in hs]
        k = [i["L0_attn_W_K"][h].reshape(CH, P, DH).transpose(1, 0, 2).reshape(P, 512) for h in hs]
        v = _np.concatenate([i["L0_attn_W_V"][h].reshape(CH, P, 1, DH) for h in hs], axis=2).reshape(CH, P, GH * DH)
        o = [i["L0_attn_W_O"][h] for h in hs]
        groups.append(_np.stack([q[0], k[0], *v, q[1], k[1], q[2], k[2], q[3], k[3], *o]))
    rows = _np.arange(P)
    gam = 1.0 - 2.0 ** (-5.0 - _np.arange(XH))
    expo = _np.arange(SEQ)[None, :] - _np.arange(SEQ)[:, None]
    full = _np.where(expo <= 0, gam[:, None, None] ** _np.minimum(expo, 0), 0.0)
    full = (full / _np.sqrt(full.sum(-1))[:, None, :] / _np.sqrt(float(DH))).transpose(2, 0, 1)
    by_chunks = lambda w: w.reshape(CH, P, -1).transpose(1, 0, 2)
    w1, w2, w3 = (i[f"L0_ffn_w{n}"] for n in (1, 2, 3))
    w_ffn = _np.stack([w1.reshape(FC, P, CH, P).transpose(0, 3, 2, 1).reshape(FC, P, 512),
                       w2.reshape(FC, P, CH, P).transpose(0, 3, 2, 1).reshape(FC, P, 512),
                       w3.T.reshape(FC, P, DIM)], axis=1)
    wh = i["L0_xattn_Wh"]
    in_rows = lambda v: _np.broadcast_to(v, (P, DIM))
    arrays = {
        "xT": i["x"].reshape(BATCH, SEQ, CH, P).transpose(0, 3, 2, 1).reshape(BATCH, P, CH * SEQ),
        "x": i["x"].reshape(TILES, P, DIM).transpose(1, 0, 2),
        "w_attn": _np.concatenate(groups),
        "biases": _np.stack([i[f"L0_attn_b_{k}"].reshape(GROUPS, GH, DH) for k in "QKV"], axis=1)
                  .reshape(GROUPS * 3 * GH, DH).T,
        "ctxT": i["ctx_2048"].reshape(BATCH, SEQ, CH, P).transpose(0, 3, 2, 1).reshape(BATCH, P, CH * SEQ),
        "w_head": _np.stack([wh.transpose(1, 0, 2).reshape(P, 512), wh.transpose(2, 0, 1).reshape(P, 512)], axis=1),
        "decay": _np.concatenate([full[:P], full[P:, :, P:]], axis=2).astype(_np.float32),
        "b_o": in_rows(i["L0_attn_b_O"]),
        "gamma": in_rows(i["L0_xattn_gn_gamma"]),
        "beta": in_rows(i["L0_xattn_gn_beta"]),
        "w_gate": by_chunks(i["L0_xattn_wg_w"]),
        "w_out": by_chunks(i["L0_xattn_wo_w"]),
        "w_ffn": w_ffn.reshape(3 * FC, P, 512),
        "w_abs": _np.stack([w.reshape(GROUPS * BATCH, P, ABS_COLS) for w in (w1, w2, w3)], axis=2)
                 .reshape(GROUPS * BATCH, P, 3 * ABS_COLS),
        "identity": _np.eye(P, dtype=_np.float32),
        "causal": _np.concatenate([_np.zeros((P, P)), _np.where(rows[None, :] <= rows[:, None], 0.0, MASKED)],
                                  axis=1).astype(_np.float32),
    }
    nc = _bacc.Bacc("TRN2", target_bir_lowering=False, num_devices=1)
    feed, t = {}, {}
    for name, a in arrays.items():
        a = _np.ascontiguousarray(a)
        feed[f"in_{name}"] = a
        t[name] = nc.dram_tensor(f"in_{name}", a.shape, _mybir.dt.from_np(a.dtype), kind="ExternalInput").ap()
    out = nc.dram_tensor("out_0", (BATCH, SEQ, DIM), F32, kind="ExternalOutput").ap()
    decoder_kernel(nc, t, out.rearrange("b (t p) d -> p (b t) d", p=P))
    r = _run(nc, [feed], core_ids=[0])
    return r.results[0]["out_0"]
```

```python
from contextlib import ExitStack

import concourse.bass as bass
from concourse import mybir

F32 = mybir.dt.float32
F32R = mybir.dt.float32r
ACT = mybir.ActivationFunctionType
ALU = mybir.AluOpType
AX_X = mybir.AxisListType.X

P = 128
BATCH, SEQ, DIM = 16, 256, 512
HEADS, DH = 16, 128
CH = DIM // P
TPB = SEQ // P
TILES = BATCH * TPB
GROUPS, GH = 4, 4
STEPS = BATCH * GH
UNITS = 16
RING = 4
KEYS = P + SEQ
MASKED = -1e30
LN_EPS = 1e-5
GN_EPS = 1e-3
XH = DIM // DH
PAIRS = BATCH // 2
FF = 1408
FC = FF // P
ABS_COLS = DIM * FF // P // (GROUPS * BATCH)
HALVES = (range(0, 2), range(2, 4))
SPLIT_LAST = ((0, 1, 2), (3, 4, 5), (6, 7), (8, 9))
SPLIT_FIRST = ((10, 11), (), (12, 13, 14, 15), ())
SPLIT_BEFORE = range(0, 10)



def after(events):
    return events + 1


class Batch:

    def __init__(self, c, it=0, hg=0):
        self.c, self.it, self.hg = c, it, hg
        self.slot = c % 2
        self.half = it + c // 2
        self.index = 2 * it + c
        at = c if isinstance(it, int) else None
        self.first, self.last = (at == 0), (at == BATCH - 1)
        self.all = BATCH * hg + self.index
        self.start = isinstance(self.all, int) and self.all < 2
        self.end = self.last and isinstance(hg, int) and hg == GROUPS - 1

    def next(self):
        return Batch(0, 0, self.hg + 1) if self.last else Batch(self.c + 1, self.it, self.hg)

    def prev(self):
        return Batch(BATCH - 1, 0, self.hg - 1) if self.first else Batch(self.c - 1, self.it, self.hg)


def over_batches(eng, body):
    body(Batch(0))
    with eng.Fori(0, (BATCH - 2) // 2) as it:
        body(Batch(1, it))
        body(Batch(2, it))
    body(Batch(BATCH - 1))


def over_batches_1(eng, body):
    body(Batch(0))
    with eng.Fori(0, (BATCH - 4) // 2) as it:
        body(Batch(1, it))
        body(Batch(2, it))
    for b in range(BATCH - 3, BATCH):
        body(Batch(b))


def over_groups(eng, body):
    def inner(hg):
        with eng.Fori(0, (BATCH - 2) // 2) as it:
            body(Batch(1, it, hg))
            body(Batch(2, it, hg))
        body(Batch(BATCH - 1, 0, hg))

    body(Batch(0))
    with eng.Fori(0, GROUPS - 1) as hg:
        inner(hg)
        body(Batch(0, 0, hg + 1))
    inner(GROUPS - 1)


def pick(tensor, n, count=1):
    if isinstance(n, int):
        return tensor[:, n, :] if count == 1 else tensor[:, n:n + count, :]
    found = tensor[:, bass.ds(n, count), :]
    return found.rearrange("p o n -> p (o n)") if count == 1 else found


def decoder_kernel(nc, t, out):
    with ExitStack() as ctx:
        def sb(name, shape, dt=F32, scope=ctx):
            return scope.enter_context(nc.sbuf_tensor(name, shape, dt))

        def sem(name):
            return ctx.enter_context(nc.semaphore(name))

        psum = ctx.enter_context(nc.psum_tensor("psum", [P, 8, 512], F32))
        bank = [psum[:, i, :] for i in range(8)]
        ps_q, ps_k, ps_v, ps_o, ps_s, ps_pt, ps_z = bank[:7]

        acc = sb("acc", [P, TILES, DIM])
        ident = sb("ident", [P, P])
        mask = sb("mask", [P, SEQ])
        bias_all = sb("bias_all", [P, GROUPS * 3 * GH])
        bo_rows = sb("bo_rows", [P, DIM])
        stats = [sb(f"stats{i}", [P, TILES, 2]) for i in range(2)]
        wsum = sb("wsum", [P, GROUPS * BATCH, 3])
        thr = sb("thr", [P, 2, 3])
        bn_raw = sb("bn_raw", [P, 4, 6])
        bn = sb("bn", [P, 4, 2])
        variance = sb("variance", [P, 4, 1])
        rdev = sb("rdev", [P, 4, 1])
        power = sb("power", [P, 2, 1])

        phase_a = ExitStack()
        w_raw = sb("w_raw", [P, RING, 512], F32, phase_a)
        w_hi = sb("w_hi", [P, UNITS, 512], F32R, phase_a)
        w_lo = sb("w_lo", [P, UNITS, 512], F32R, phase_a)
        x_raw = sb("x_raw", [P, 2, CH * SEQ], F32, phase_a)
        x_hi = sb("x_hi", [P, 2, CH, SEQ], F32R, phase_a)
        x_lo = sb("x_lo", [P, 2, CH, SEQ], F32R, phase_a)
        q_hi = sb("q_hi", [P, SEQ], F32R, phase_a)
        q_lo = sb("q_lo", [P, SEQ], F32R, phase_a)
        k_hi = sb("k_hi", [P, SEQ], F32R, phase_a)
        k_lo = sb("k_lo", [P, SEQ], F32R, phase_a)
        v_hi = sb("v_hi", [P, 2, TPB, GH * DH], F32R, phase_a)
        v_lo = sb("v_lo", [P, 2, TPB, GH * DH], F32R, phase_a)
        z_hi = sb("z_hi", [P, 2, GH, SEQ], F32R, phase_a)
        z_lo = sb("z_lo", [P, 2, GH, SEQ], F32R, phase_a)
        probs = sb("probs", [P, KEYS], F32, phase_a)
        pt_hi = sb("pt_hi", [P, KEYS], F32R, phase_a)
        pt_lo = sb("pt_lo", [P, KEYS], F32R, phase_a)
        negmax = sb("negmax", [P, TPB], F32, phase_a)
        rowsum = sb("rowsum", [P, TPB], F32, phase_a)
        inv = sb("inv", [P, TPB], F32, phase_a)
        w_abs = sb("w_abs", [P, 2, 3 * ABS_COLS], F32, phase_a)
        phase_a.close()

        cross = ExitStack()
        ctx_raw = sb("ctx_raw", [P, 2, CH * SEQ], F32, cross)
        ctx_hi = sb("ctx_hi", [P, 2, CH, SEQ], F32R, cross)
        ctx_lo = sb("ctx_lo", [P, 2, CH, SEQ], F32R, cross)
        xn = sb("xn", [P, 2, TPB, DIM], F32, cross)
        xt_hi = sb("xt_hi", [P, 2, CH, SEQ], F32R, cross)
        xt_lo = sb("xt_lo", [P, 2, CH, SEQ], F32R, cross)
        a_hi = sb("a_hi", [P, XH, KEYS], F32R, cross)
        a_lo = sb("a_lo", [P, XH, KEYS], F32R, cross)
        ones_r = sb("ones_r", [P, P], F32R, cross)
        wh_hi = sb("wh_hi", [P, XH, DH], F32R, cross)
        wh_lo = sb("wh_lo", [P, XH, DH], F32R, cross)
        cross_1 = ExitStack()
        wtot = sb("wtot", [P, 3], F32, cross_1)
        zeros = sb("zeros", [P, P], F32, cross_1)
        xq_hi = sb("xq_hi", [P, 2, XH, SEQ], F32R, cross_1)
        xq_lo = sb("xq_lo", [P, 2, XH, SEQ], F32R, cross_1)
        wx_raw = sb("wx_raw", [P, 2, XH * DH], F32, cross_1)
        decay = sb("decay", [P, XH, KEYS], F32, cross_1)
        a_raw = sb("a_raw", [P, XH, KEYS], F32, cross_1)
        g_hi = sb("g_hi", [P, XH, DH], F32R, cross_1)
        g_lo = sb("g_lo", [P, XH, DH], F32R, cross_1)
        cross_1.close()
        cross_2 = ExitStack()
        xv_hi = sb("xv_hi", [P, TPB, XH, 2, DH], F32R, cross_2)
        xv_lo = sb("xv_lo", [P, TPB, XH, 2, DH], F32R, cross_2)
        gate = sb("gate", [P, 4, DIM], F32, cross_2)
        y_raw = sb("y_raw", [P, 2, DIM], F32, cross_2)
        wyt_hi = sb("wyt_hi", [P, 2, CH, P], F32R, cross_2)
        wyt_lo = sb("wyt_lo", [P, 2, CH, P], F32R, cross_2)
        gamma = sb("gamma", [P, DIM], F32, cross_2)
        beta = sb("beta", [P, DIM], F32, cross_2)
        wgo_hi = sb("wgo_hi", [P, 2, CH, DIM], F32R, cross_2)
        unsplit = ExitStack()
        wgo_raw = sb("wgo_raw", [P, 2, CH, DIM], F32, unsplit)
        unsplit.close()
        wgo_lo = sb("wgo_lo", [P, 2, CH, DIM], F32R, cross_2)
        cross_2.close()
        cross.close()

        ffn = ExitStack()
        f_raw = sb("f_raw", [P, RING, 512], F32, ffn)
        xn2 = sb("xn2", [P, 2, TPB, DIM], F32, ffn)
        f_neg = sb("f_neg", [P, 2, 512], F32, ffn)
        sig = sb("sig", [P, 2, 512], F32, ffn)
        xt2_hi = sb("xt2_hi", [P, 2, CH, SEQ], F32R, ffn)
        xt2_lo = sb("xt2_lo", [P, 2, CH, SEQ], F32R, ffn)
        f_w = sb("f_w", [P, 3 * FC, 512], F32R, ffn)
        hid = sb("hid", [P, 2, 512], F32, ffn)
        hid_hi = sb("hid_hi", [P, 2, 512], F32R, ffn)
        hid_lo = sb("hid_lo", [P, 2, 512], F32R, ffn)
        y3 = sb("y3", [P, 4, DIM], F32, ffn)
        ffn.close()

        def bias_of(b, kind, h):
            column = (b.hg * 3 + kind) * GH + h
            return bias_all[:, column:column + 1] if isinstance(column, int) else bias_all[:, bass.ds(column, 1)]

        UNIT_V, UNIT_QK, UNIT_O = 0, 4, 12

        def unit_qk(kind, h):
            return UNIT_QK + 2 * h + kind

        s_primed = sem("s_primed")
        s_const = sem("s_const")
        s_wdma = [sem(f"s_wdma{i}") for i in range(RING)]
        s_xdma = [sem(f"s_xdma{i}") for i in range(2)]
        s_absdma = [sem(f"s_absdma{i}") for i in range(2)]
        s_accin = [sem(f"s_accin{i}") for i in range(2)]
        s_const2, s_gdma = sem("s_const2"), sem("s_gdma")
        s_ctxdma = [sem(f"s_ctxdma{i}") for i in range(2)]
        s_wgo = [sem(f"s_wgo{i}") for i in range(2)]
        s_fdma = [sem(f"s_fdma{i}") for i in range(RING)]

        def events(names, among):
            made = [sem(n) for n in names.split()]
            among.extend(made)
            return made

        progress, later = [], []
        s_xhi, s_x, s_whi, s_wlo = events("s_xhi s_x s_whi s_wlo", progress)
        s_q, s_qhi, s_qlo, s_k, s_khi, s_klo = events("s_q s_qhi s_qlo s_k s_khi s_klo", progress)
        s_v, s_vhi, s_vlo = events("s_v s_vhi s_vlo", progress)
        s_scores, s_max, s_exp, s_inv, s_norm = events("s_scores s_max s_exp s_inv s_norm", progress)
        s_pt, s_pthi, s_ptlo, s_z, s_zhi, s_zlo = events("s_pt s_pthi s_ptlo s_z s_zhi s_zlo", progress)
        s_o, s_acc = events("s_o s_acc", progress)
        s_bo, s_abs, s_ones = events("s_bo s_abs s_ones", later)
        s_bn, s_aggr, s_mean, s_var, s_rdev, s_xn, s_back = events(
            "s_bn s_aggr s_mean s_var s_rdev s_xn s_back", later)
        s_xt, s_xthi, s_xtlo = events("s_xt s_xthi s_xtlo", later)
        s_ctxhi, s_ctxlo, s_gohi, s_golo = events("s_ctxhi s_ctxlo s_gohi s_golo", later)
        s_g, s_ghi, s_glo, s_whsplit, s_wh = events("s_g s_ghi s_glo s_whsplit s_wh", later)
        s_xq, s_xqhi, s_xqlo, s_xs = events("s_xq s_xqhi s_xqlo s_xs", later)
        s_araw, s_ahi, s_alo = events("s_araw s_ahi s_alo", later)
        s_xv, s_xvhi, s_xvlo, s_xo = events("s_xv s_xvhi s_xvlo s_xo", later)
        s_yc, s_ys, s_gate, s_relu, s_wy = events("s_yc s_ys s_gate s_relu s_wy", later)
        s_wyt, s_wythi, s_wytlo, s_xout, s_res = events("s_wyt s_wythi s_wytlo s_xout s_res", later)
        s_tot, s_totps, s_thr, s_neg, s_fw = events("s_tot s_totps s_thr s_neg s_fw", later)
        s_up, s_sig, s_hid, s_hhi, s_hlo, s_down = events("s_up s_sig s_hid s_hhi s_hlo s_down", later)
        s_y3, s_y3n, s_yout = events("s_y3 s_y3n s_yout", later)

        block = ctx.enter_context(nc.Block())

        @block.sync
        def _(sp):
            def load_w(hg, u):
                if not (isinstance(hg, int) and hg * UNITS + u < RING):
                    sp.wait_ge(s_wlo, after(hg * UNITS + u - RING + 1))
                sp.dma_start(w_raw[:, u % RING, :], pick(t["w_attn"].rearrange("u p n -> p u n"), hg * UNITS + u)
                             ).then_inc(s_wdma[u % RING], 16)

            def load_abs(b):
                if not b.start:
                    sp.wait_ge(s_abs, after(b.all - 1))
                sp.dma_start(w_abs[:, b.slot, :], pick(t["w_abs"].rearrange("b p n -> p b n"), b.all)
                             ).then_inc(s_absdma[b.slot], 16)

            def load_residual(b):
                if not b.start:
                    sp.wait_ge(s_accin[b.slot], 16 * b.half)
                sp.dma_start(pick(acc, TPB * b.index, TPB), pick(t["x"], TPB * b.index, TPB)
                             ).then_inc(s_accin[b.slot], 16)

            def load_x(b, residual):
                if not b.start:
                    sp.wait_ge(s_x, after(b.all - 1))
                sp.dma_start(x_raw[:, b.slot, :], pick(t["xT"].rearrange("b p n -> p b n"), b.index)
                             ).then_inc(s_xdma[b.slot], 16)
                if residual:
                    load_residual(b)

            def inner_x(hg, residual):
                with sp.Fori(0, (BATCH - 2) // 2) as it:
                    for c in (2, 3):
                        load_x(Batch(c, it, hg), residual)
                        load_abs(Batch(c, it, hg))

            def ahead(hg):
                for u in range(RING):
                    load_w(hg + 1, u)
                load_x(Batch(0, 0, hg + 1), False)
                load_abs(Batch(0, 0, hg + 1))
                load_x(Batch(1, 0, hg + 1), False)
                for u in range(RING, UNITS):
                    load_w(hg + 1, u)
                load_abs(Batch(1, 0, hg + 1))

            load_x(Batch(0), False)
            for u in range(2):
                load_w(0, u)
            for dst, src in ((bias_all, "biases"), (ident, "identity"), (mask, "causal"), (bo_rows, "b_o")):
                sp.dma_start(dst[:, :], t[src]).then_inc(s_const, 16)
                if src == "biases":
                    load_w(0, 2)
                    load_w(0, 3)
            load_residual(Batch(0))
            sp.wait_ge(s_primed, 2)
            for u in range(RING, UNITS):
                load_w(0, u)
                if u == 9:
                    load_x(Batch(1), True)
            load_abs(Batch(0))
            load_abs(Batch(1))
            inner_x(0, True)
            ahead(0)
            with sp.Fori(1, GROUPS - 1) as hg:
                inner_x(hg, False)
                ahead(hg)
            inner_x(GROUPS - 1, False)

            sp.wait_ge(s_k, after(GROUPS * STEPS))
            for dst, src in ((wx_raw, "w_head"), (decay, "decay")):
                sp.dma_start(dst[:, :, :], t[src]).then_inc(s_const2, 16)

            def load_ctx(n, b):
                if not isinstance(n, int) or n >= 2:
                    sp.wait_ge(s_ctxlo, after(n - 1))
                sp.dma_start(ctx_raw[:, b.slot, :], pick(t["ctxT"].rearrange("b p n -> p b n"), b.index)
                             ).then_inc(s_ctxdma[b.slot], 16)

            def pass_1(b):
                load_ctx(b.index, b)
                if b.first:
                    sp.wait_ge(s_acc, after(GROUPS * TILES))
                    sp.dma_start(wgo_raw[:, 0, :, :], t["w_gate"]).then_inc(s_wgo[0], 16)
                elif b.last:
                    sp.dma_start(wgo_raw[:, 1, :, :], t["w_out"]).then_inc(s_wgo[1], 16)

            over_batches(sp, pass_1)
            load_ctx(BATCH, Batch(0))
            load_ctx(BATCH + 1, Batch(1))
            sp.wait_ge(s_xs, after(BATCH))
            sp.wait_ge(s_alo, after(1))
            for dst, src in ((gamma, "gamma"), (beta, "beta")):
                sp.dma_start(dst[:, :], t[src]).then_inc(s_gdma, 16)
            with sp.Fori(0, PAIRS - 1) as p:
                load_ctx(2 * p + BATCH + 2, Batch(2, p))
                load_ctx(2 * p + BATCH + 3, Batch(3, p))

            sp.wait_ge(s_xv, after(4 * PAIRS))
            for u in range(3 * FC):
                if u >= RING:
                    sp.wait_ge(s_fw, after(u - RING + 1))
                sp.dma_start(f_raw[:, u % RING, :], t["w_ffn"][u, :, :]).then_inc(s_fdma[u % RING], 16)

            def store(p):
                for k in range(4):
                    sp.wait_ge(s_y3n, after(4 * p + k + 1))
                    sp.dma_start(pick(out, 4 * p + k), y3[:, k, :]).then_inc(s_yout, 16)

            with sp.Fori(0, PAIRS) as p:
                store(p)
            sp.wait_ge(s_yout, after(16 * TILES))

        @block.gpsimd
        def _(pool):
            for group in progress, later:
                for s in group:
                    pool.sem_inc(s, 1)
                pool.sem_inc(s_primed, 1)

            def split_x(b):
                pool.wait_ge(s_xdma[b.slot], (PAIRS * b.hg + b.half + 1) * 16)
                if not b.start:
                    pool.wait_ge(s_k, after(GH * (b.all - 1)))
                hi = x_hi[:, b.slot, :, :].rearrange("p c n -> p (c n)")
                pool.nop(nofuse=True)
                nc.gpsimd.tensor_copy(hi, x_raw[:, b.slot, :]).then_inc(s_xhi, 1)
                pool.wait_ge(s_xhi, after(b.all + 1))
                nc.gpsimd.tensor_tensor(out=x_lo[:, b.slot, :, :].rearrange("p c n -> p (c n)"),
                                        in0=x_raw[:, b.slot, :], in1=hi.bitcast(F32),
                                        op=ALU.subtract).then_inc(s_x, 1)

            def add_bo(b):
                pool.wait_ge(s_accin[b.slot], 16 * (b.half + 1))
                for tt in range(TPB):
                    a = pick(acc, TPB * b.index + tt)
                    nc.gpsimd.tensor_tensor(out=a, in0=a, in1=bo_rows[:, :], op=ALU.add).then_inc(s_bo, 1)


            def group_0(b):
                if b.first:
                    pool.wait_ge(s_const, 64)
                    pool.wait_ge(s_x, after(1))
                add_bo(b)
                if not b.last:
                    split_x(b.next())

            over_batches(pool, group_0)
            power_all = bo_rows[:, 0:TILES].rearrange("p (t o) -> p t o", o=1)
            pool.wait_ge(s_bo, after(TILES))
            for constant in power_all, power[:, :, :]:
                nc.gpsimd.memset(constant, -0.5).then_inc(s_ones, 1)
            with pool.Fori(1, GROUPS) as hg:
                split_x(Batch(0, 0, hg))
                with pool.Fori(0, (BATCH - 2) // 2) as it:
                    split_x(Batch(1, it, hg))
                    split_x(Batch(2, it, hg))
                split_x(Batch(BATCH - 1, 0, hg))

            def inverse_1(first, last):
                pool.wait_ge(s_mean, after(last))
                st = stats[0][:, TPB * first:TPB * last, 1:2]
                return nc.gpsimd.tensor_tensor(out=st, in0=st, in1=power_all[:, 0:TPB * (last - first), :], op=ALU.pow)

            pool.wait_ge(s_ones, after(2))
            inverse_1(0, BATCH - 2)
            pool.wait_ge(s_acc, after(GROUPS * TILES))
            for constant, value in ((ones_r[:, :].bitcast(F32), 1.0), (zeros[:, :], 0.0)):
                nc.gpsimd.memset(constant, value).then_inc(s_ones, 1)
            inverse_1(BATCH - 2, BATCH).then_inc(s_rdev, 1)

            def inverse_root(n, k, count, out_ap):
                pool.wait_ge(s_var, after(n + 1))
                nc.gpsimd.tensor_tensor(out=out_ap, in0=variance[:, k:k + count, :], in1=power[:, 0:count, :],
                                        op=ALU.pow).then_inc(s_rdev, 1)

            def stat_column(which, tile, count, column):
                st = stats[which][:, tile:tile + count, :] if isinstance(tile, int) else \
                    stats[which][:, bass.ds(tile, count), :]
                return st[:, :, column:column + 1]

            def ctx_split(n, b):
                pool.wait_ge(s_ctxhi, after(n + 1))
                nc.gpsimd.tensor_tensor(out=ctx_lo[:, b.slot, :, :].rearrange("p c n -> p (c n)"),
                                        in0=ctx_raw[:, b.slot, :],
                                        in1=ctx_hi[:, b.slot, :, :].rearrange("p c n -> p (c n)").bitcast(F32),
                                        op=ALU.subtract).then_inc(s_ctxlo, 1)

            def wgo_split(i):
                pool.wait_ge(s_gohi, after(i + 1))
                nc.gpsimd.tensor_tensor(out=wgo_lo[:, i, :, :], in0=wgo_raw[:, i, :, :],
                                        in1=wgo_hi[:, i, :, :].bitcast(F32), op=ALU.subtract).then_inc(s_golo, 1)

            def pass_1(b):
                ctx_split(b.index, b)
                if isinstance(b.index, int) and b.index == BATCH - 3:
                    wgo_split(0)

            over_batches_1(pool, pass_1)
            ctx_split(BATCH, Batch(0))
            ctx_split(BATCH + 1, Batch(1))
            wgo_split(1)

            def pass_2(p, more):
                n = 8 * p
                for k in range(4):
                    inverse_root(n + k, 2 + k % 2, 1, rdev[:, k % 2:k % 2 + 1, :])
                    if more and k < 2:
                        ctx_split(2 * p + BATCH + 2 + k, Batch(2 + k, p))
                for k in range(4):
                    inverse_root(n + 4 + k, k % 2, 1, stat_column(1, 4 * p + k, 1, 1))

            with pool.Fori(0, PAIRS - 1) as p:
                pass_2(p, True)
            pass_2(PAIRS - 1, False)

            with pool.Fori(0, PAIRS) as p:
                for k in range(0, 4, 2):
                    inverse_root(2 * TILES + 2 * p + k // 2, k, 2, rdev[:, k:k + 2, :])

        @block.tensor
        def _(pe):
            def mm3(out_ap, left, right, first, last):
                (lh, ll), (rh, rl) = left, right
                pe.matmul(out_ap, lh, rh, start=first, stop=False, skip_group_check=True)
                pe.matmul(out_ap, lh, rl, start=False, stop=False, skip_group_check=True)
                return pe.matmul(out_ap, ll, rh, start=False, stop=last, skip_group_check=True)

            def project(ps, kind, h, b, done):
                u = unit_qk(kind, h)
                for c in range(CH):
                    w = [x[:, u, c * DH:(c + 1) * DH] for x in (w_hi, w_lo)]
                    x = [x[:, b.slot, c, :] for x in (x_hi, x_lo)]
                    mm = mm3(ps[:, 0:SEQ], w, x, c == 0, c == CH - 1)
                mm.then_inc(done, 1)

            def queries_keys(b, h, part):
                if b.first:
                    pe.wait_ge(s_wlo, after(b.hg * UNITS + unit_qk(part, h) + 1))
                if h == 0 and part == 0:
                    pe.wait_ge(s_x, after(b.all + 1))
                project(ps_k if part else ps_q, part, h, b, s_k if part else s_q)

            def values(b, tt, part):
                n = TPB * b.all + tt
                if part == 0:
                    pe.wait_ge(s_x, after(b.all + 1))
                    pe.wait_ge(s_vlo, after(n))
                for c in HALVES[part]:
                    if b.first:
                        pe.wait_ge(s_wlo, after(b.hg * UNITS + UNIT_V + c + 1))
                    x = [x[:, b.slot, c, tt * P:(tt + 1) * P] for x in (x_hi, x_lo)]
                    w = [w[:, UNIT_V + c, :] for w in (w_hi, w_lo)]
                    mm = mm3(ps_v[:, :], x, w, c == 0, c == CH - 1)
                if part == 1:
                    mm.then_inc(s_v, 1)

            def scores(b, h):
                n = GH * b.all + h
                pe.wait_ge(s_klo, after(n + 1))
                for qt in range(TPB):
                    q = [x[:, qt * P:(qt + 1) * P] for x in (q_hi, q_lo)]
                    k = [x[:, 0:(qt + 1) * P] for x in (k_hi, k_lo)]
                    mm = mm3(ps_s[:, qt * P:qt * P + (qt + 1) * P], q, k, qt == 0, qt == TPB - 1)
                mm.then_inc(s_scores, 1)

            def transposes(b, h):
                n = GH * b.all + h
                pe.wait_ge(s_norm, after(n + 1))
                for i in range(KEYS // P):
                    mm = pe.transpose(ps_pt[:, i * P:(i + 1) * P], probs[:, i * P:(i + 1) * P], ident[:, :])
                mm.then_inc(s_pt, 1)

            def mix(b, h):
                n = GH * b.all + h
                pe.wait_ge(s_ptlo, after(n + 1))
                if h == 0:
                    pe.wait_ge(s_vlo, after(TPB * b.all + TPB))
                pe.wait_ge(s_zlo, after(n))
                for kt in range(TPB):
                    v = [x[:, b.slot, kt, h * DH:(h + 1) * DH] for x in (v_hi, v_lo)]
                    p = [x[:, 0:SEQ] if kt == 0 else x[:, SEQ:KEYS] for x in (pt_hi, pt_lo)]
                    mm = mm3(ps_z[:, kt * P:SEQ], v, p, kt == 0, kt == TPB - 1)
                mm.then_inc(s_z, 1)

            def outputs(b, tt, part):
                if part == 0:
                    if tt == 0:
                        pe.wait_ge(s_zlo, after(GH * b.all + GH))
                    pe.wait_ge(s_acc, after(TPB * b.all + tt))
                for h in HALVES[part]:
                    if b.first:
                        pe.wait_ge(s_wlo, after(b.hg * UNITS + UNIT_O + h + 1))
                    z = [x[:, b.slot, h, tt * P:(tt + 1) * P] for x in (z_hi, z_lo)]
                    w = [x[:, UNIT_O + h, :] for x in (w_hi, w_lo)]
                    mm = mm3(ps_o[:, :], z, w, h == 0, h == GH - 1)
                if part == 1:
                    mm.then_inc(s_o, 1)

            pe.wait_ge(s_primed, 2)
            for tt in range(TPB):
                for part in range(2):
                    values(Batch(0), tt, part)
            for part in range(2):
                queries_keys(Batch(0), 0, part)

            def attend(b):
                for h in range(GH):
                    scores(b, h)
                    nb, nh = (b, h + 1) if h + 1 < GH else (b.next(), 0)
                    if not (b.end and h + 1 == GH):
                        queries_keys(nb, nh, 0)
                        queries_keys(nb, nh, 1)
                    for part in range(2):
                        if h < TPB and not (b.start and b.first):
                            outputs(b.prev(), h, part)
                        if h >= TPB and not b.end:
                            values(b.next(), h - TPB, part)
                        if part == 0:
                            transposes(b, h)
                    mix(b, h)

            over_groups(pe, attend)
            for tt in range(TPB):
                for part in range(2):
                    outputs(Batch(BATCH - 1, 0, GROUPS - 1), tt, part)

            def transpose_rows(rows, slot, base):
                for c in range(CH):
                    for tt in range(TPB):
                        mm = pe.transpose(bank[base + c // 2][:, c % 2 * SEQ + tt * P:c % 2 * SEQ + (tt + 1) * P],
                                          rows[:, slot, tt, c * P:(c + 1) * P], ident[:, :])
                mm.then_inc(s_xt, 1)

            pe.wait_ge(s_const2, 32)
            for h in range(XH):
                w = wx_raw[:, 1, h * DH:(h + 1) * DH]
                mm = pe.matmul(bank[2][:, h * DH:(h + 1) * DH], w, w, start=True, stop=True, skip_group_check=True)
            mm.then_inc(s_g, 1)

            pe.wait_ge(s_acc, after(GROUPS * TILES))
            pe.wait_ge(s_ones, after(4))
            for h in range(XH):
                pe.matmul(bank[4 + h][:, 0:KEYS], zeros[:, :], decay[:, h, :], start=True, stop=False,
                          skip_group_check=True)
            pe.wait_ge(s_tot, after(1))
            pe.matmul(bank[3][:, 0:3], ones_r[:, :].bitcast(F32), wtot[:, :], start=True, stop=True
                      ).then_inc(s_totps, 1)

            def cross_rows(b):
                pe.wait_ge(s_xn, after(b.index + 1))
                pe.wait_ge(s_xtlo, after(b.index))
                transpose_rows(xn, b.slot, 0)

            def cross_queries(b):
                pe.wait_ge(s_xtlo, after(b.index + 1))
                pe.wait_ge(s_xqlo, after(b.index))
                for h in range(XH):
                    g = [x[:, h, :] for x in (g_hi, g_lo)]
                    x = [x[:, b.slot, h, :] for x in (xt_hi, xt_lo)]
                    mm = mm3(bank[2 + h // 2][:, h % 2 * SEQ:(h % 2 + 1) * SEQ], g, x, True, True)
                mm.then_inc(s_xq, 1)

            def cross_scores(b):
                pe.wait_ge(s_xqlo, after(b.index + 1))
                pe.wait_ge(s_ctxlo, after(b.index + 1))
                for h in range(XH):
                    for kt in range(TPB):
                        c = [x[:, b.slot, h, kt * P:(kt + 1) * P] for x in (ctx_hi, ctx_lo)]
                        q = [x[:, b.slot, h, kt * P:SEQ] for x in (xq_hi, xq_lo)]
                        mm = mm3(bank[4 + h][:, kt * SEQ:kt * SEQ + SEQ - kt * P], c, q, False, b.last)
                mm.then_inc(s_xs, 1)

            cross_rows(Batch(0))
            pe.wait_ge(s_glo, after(1))

            def pass_1(b):
                if not b.last:
                    cross_rows(b.next())
                cross_queries(b)
                if not b.first:
                    cross_scores(b.prev())

            over_batches_1(pe, pass_1)

            def cross_values(p, j, tt):
                pe.wait_ge(s_ctxlo, after(2 * p + BATCH + j + 1))
                for h in range(XH):
                    c = [x[:, j, h, tt * P:(tt + 1) * P] for x in (ctx_hi, ctx_lo)]
                    w = [x[:, h, :] for x in (wh_hi, wh_lo)]
                    mm = mm3(bank[2 + tt][:, h * DH:(h + 1) * DH], c, w, True, True)
                mm.then_inc(s_xv, 1)

            def rows_2(p, j):
                pe.wait_ge(s_xn, after(2 * p + BATCH + j + 1))
                transpose_rows(xn, j, 0 if isinstance(p, int) and p == 0 else 2)

            def cross_mix(p, st):
                for h in range(XH):
                    ps = bank[4 + 2 * st + h // 2][:, h % 2 * 2 * DH:(h % 2 + 1) * 2 * DH]
                    v = [x[:, :, h, :, :].rearrange("p t j e -> p t (j e)") for x in (xv_hi, xv_lo)]
                    a = [x[:, h, st * P:(st + 1) * P] for x in (a_hi, a_lo)]
                    mm3(ps, a, [x[:, 0, :] for x in v], True, False)
                    if st == 1:
                        a = [x[:, h, SEQ:KEYS] for x in (a_hi, a_lo)]
                        mm = mm3(ps, a, [x[:, 1, :] for x in v], False, True)
                    else:
                        pe.matmul(ps, ones_r[:, :], v[0][:, 1, :], start=False, stop=False, skip_group_check=True)
                        mm = pe.matmul(ps, ones_r[:, :], v[1][:, 1, :], start=False, stop=True,
                                       skip_group_check=True)
                mm.then_inc(s_xo, 1)

            def gate_rows(p, k, parts=range(2)):
                pe.wait_ge(s_xtlo, after(2 * p + BATCH + k // 2 + 1))
                if k:
                    pe.wait_ge(s_relu, after(4 * p + k))
                else:
                    pe.wait_ge(s_res, after(4 * p))
                for c in [c for part in parts for c in HALVES[part]]:
                    x = [x[:, k // 2, c, k % 2 * P:(k % 2 + 1) * P] for x in (xt_hi, xt_lo)]
                    mm = mm3(bank[0], x, [x[:, 0, c, :] for x in (wgo_hi, wgo_lo)], c == 0, c == CH - 1)
                if parts[-1] == 1:
                    mm.then_inc(s_gate, 1)

            def rows_3(p, j):
                pe.wait_ge(s_xn, after(2 * p + 2 * BATCH + j + 1))
                transpose_rows(xn2, j, 2 - 2 * j)

            def turn_wy(p, k):
                pe.wait_ge(s_wy, after(4 * p + k + 1))
                for c in range(CH):
                    mm = pe.transpose(bank[2 + k % 2][:, c * P:(c + 1) * P], gate[:, k, c * P:(c + 1) * P],
                                      ident[:, :])
                mm.then_inc(s_wyt, 1)

            def cross_output(p, k):
                pe.wait_ge(s_wytlo, after(4 * p + k + 1))
                if k == 1:
                    pe.wait_ge(s_relu, after(4 * p + 4))
                elif k:
                    pe.wait_ge(s_res, after(4 * p + k - 1))
                for c in range(CH):
                    mm = mm3(bank[1 - k % 2], [x[:, k % 2, c, :] for x in (wyt_hi, wyt_lo)],
                             [x[:, 1, c, :] for x in (wgo_hi, wgo_lo)], c == 0, c == CH - 1)
                mm.then_inc(s_xout, 1)

            pe.wait_ge(s_xtlo, after(BATCH))
            rows_2(0, 0)
            cross_scores(Batch(BATCH - 1))
            pe.wait_ge(s_wh, after(1))
            pe.wait_ge(s_xqlo, after(BATCH))
            cross_values(0, 0, 0)
            cross_values(0, 0, 1)
            pe.wait_ge(s_xtlo, after(BATCH + 1))
            rows_2(0, 1)
            pe.wait_ge(s_xvlo, after(2))
            cross_values(0, 1, 0)
            cross_values(0, 1, 1)
            pe.wait_ge(s_xtlo, after(BATCH + 2))
            pe.wait_ge(s_alo, after(1))
            pe.wait_ge(s_golo, after(1))

            def pass_2(p, more):
                pe.wait_ge(s_xvlo, after(4 * p + 4))
                pe.wait_ge(s_yc, after(4 * p))
                cross_mix(p, 0)
                cross_mix(p, 1)
                gate_rows(p, 0)
                pe.wait_ge(s_xtlo, after(2 * p + BATCH + 2))
                if more:
                    cross_values(p + 1, 0, 0)
                    cross_values(p + 1, 0, 1)
                gate_rows(p, 1)
                if more:
                    pe.wait_ge(s_xvlo, after(4 * p + 6))
                    rows_2(p + 1, 0)
                gate_rows(p, 2)
                if more:
                    pe.wait_ge(s_xtlo, after(2 * p + BATCH + 3))
                    cross_values(p + 1, 1, 0)
                    cross_values(p + 1, 1, 1)
                gate_rows(p, 3, [0])
                if more:
                    pe.wait_ge(s_xvlo, after(4 * p + 8))
                turn_wy(p, 0)
                gate_rows(p, 3, [1])
                turn_wy(p, 1)
                pe.wait_ge(s_golo, after(2))
                cross_output(p, 0)
                turn_wy(p, 2)
                cross_output(p, 1)
                turn_wy(p, 3)
                cross_output(p, 2)
                if more:
                    pe.wait_ge(s_wytlo, after(4 * p + 4))
                    rows_2(p + 1, 1)
                else:
                    pe.wait_ge(s_wytlo, after(4 * PAIRS))
                    rows_3(0, 0)
                cross_output(p, 3)

            with pe.Fori(0, PAIRS - 1) as p:
                pass_2(p, True)
            pass_2(PAIRS - 1, False)

            def up(p, f, first):
                if first:
                    pe.wait_ge(s_fw, after(3 * f + 2))
                if f >= 2:
                    pe.wait_ge(s_hid, after(FC * p + f - 1))
                else:
                    pe.wait_ge(s_xtlo, after(2 * p + 2 * BATCH + 2))
                for m in range(2):
                    for c in range(CH):
                        w = f_w[:, 3 * f + m, c * P:(c + 1) * P]
                        for i, x in enumerate((xt2_hi, xt2_lo)):
                            mm = pe.matmul(bank[f % 2 * 2 + m].rearrange("p (j n) -> p j n", j=2), w, x[:, :, c, :],
                                           start=(c == 0 and i == 0), stop=(c == CH - 1 and i == 1),
                                           skip_group_check=True)
                mm.then_inc(s_up, 1)

            def down(p, f, first):
                if first:
                    pe.wait_ge(s_fw, after(3 * f + 3))
                pe.wait_ge(s_hlo, after(FC * p + f + 1))
                if f == 0:
                    pe.wait_ge(s_y3, after(4 * p))
                for k in range(4):
                    for i, x in enumerate((hid_hi, hid_lo)):
                        mm = pe.matmul(bank[4 + k], x[:, f % 2, k * P:(k + 1) * P], f_w[:, 3 * f + 2, :],
                                       start=(f == 0 and i == 0), stop=(f == FC - 1 and i == 1),
                                       skip_group_check=True)
                mm.then_inc(s_down, 1)

            pe.wait_ge(s_res, after(TILES))
            rows_3(0, 1)
            pe.wait_ge(s_thr, after(1))

            def pass_3(p, first, more):
                for f in range(FC):
                    up(p, f, first)
                    if more and f == FC - 1:
                        pe.wait_ge(s_hid, after(FC * p + FC - 1))
                        rows_3(p + 1, 0)
                    if f >= 1:
                        down(p, f - 1, first)
                if more:
                    pe.wait_ge(s_hid, after(FC * p + FC))
                    rows_3(p + 1, 1)
                down(p, FC - 1, first)

            pass_3(0, True, True)
            with pe.Fori(1, PAIRS - 1) as p:
                pass_3(p, False, True)
            pass_3(PAIRS - 1, False, False)

        SCALE = float(DH) ** -0.5

        @block.scalar
        def _(act):
            def split_w(hg, u):
                act.wait_ge(s_wdma[u % RING], (hg * (UNITS // RING) + u // RING + 1) * 16)
                if not isinstance(hg, int) or hg:
                    if u >= UNIT_O:
                        act.wait_ge(s_o, after(hg * TILES))
                    elif UNIT_V <= u < UNIT_V + CH:
                        act.wait_ge(s_v, after(hg * TILES))
                    else:
                        act.wait_ge(s_k, after(hg * STEPS - GH + (u - UNIT_QK) // 2 + 1))
                nc.scalar.copy(w_hi[:, u, :], w_raw[:, u % RING, :]).then_inc(s_whi, 1)

            def qk_hi(b, h, part):
                n = GH * b.all + h
                act.wait_ge(s_k if part else s_q, after(n + 1))
                act.nop(nofuse=True)
                nc.scalar.activation((k_hi if part else q_hi)[:, :], (ps_k if part else ps_q)[:, 0:SEQ],
                                     ACT.Identity, bias=bias_of(b, part, h)
                                     ).then_inc(s_khi if part else s_qhi, 1)

            def v_split(b, tt):
                act.wait_ge(s_v, after(TPB * b.all + tt + 1))
                nc.scalar.copy(v_hi[:, b.slot, tt, :], ps_v[:, :]).then_inc(s_vhi, 1)

            def exps(b, h):
                n = GH * b.all + h
                act.wait_ge(s_max, after(TPB * (n + 1)))
                nc.scalar.activation(probs[:, 0:P], ps_s[:, 0:P], ACT.Exp, bias=negmax[:, 0:1], scale=-1.0,
                                     accum_out=rowsum[:, 0:1])
                nc.scalar.activation(probs[:, P:KEYS], ps_s[:, P:KEYS], ACT.Exp, bias=negmax[:, 1:2],
                                     scale=-1.0, accum_out=rowsum[:, 1:2]).then_inc(s_exp, 1)

            def pt_split(b, h):
                n = GH * b.all + h
                act.wait_ge(s_pt, after(n + 1))
                nc.scalar.copy(pt_hi[:, :], ps_pt[:, 0:KEYS]).then_inc(s_pthi, 1)

            def z_split(b, h):
                n = GH * b.all + h
                act.wait_ge(s_z, after(n + 1))
                act.nop(nofuse=True)
                nc.scalar.activation(z_hi[:, b.slot, h, :], ps_z[:, 0:SEQ], ACT.Identity,
                                     bias=bias_of(b, 2, h)).then_inc(s_zhi, 1)

            def sum_abs(b):
                act.wait_ge(s_absdma[b.slot], (PAIRS * b.hg + b.half + 1) * 16)
                for m in range(3):
                    piece = w_abs[:, b.slot, m * ABS_COLS:(m + 1) * ABS_COLS]
                    last = nc.scalar.activation(piece, piece, ACT.Abs, accum_out=pick(wsum, b.all)[:, m:m + 1])
                last.then_inc(s_abs, 1)

            act.wait_ge(s_primed, 1)
            act.wait_ge(s_xdma[0], 16)
            nc.scalar.copy(x_hi[:, 0, :, :].rearrange("p c n -> p (c n)"), x_raw[:, 0, :]).then_inc(s_xhi, 1)
            for u in SPLIT_BEFORE[:6]:
                split_w(0, u)
            act.wait_ge(s_const, 64)
            act.wait_ge(s_primed, 2)
            for tt in range(TPB):
                v_split(Batch(0), tt)
            qk_hi(Batch(0), 0, 0)
            qk_hi(Batch(0), 0, 1)
            for u in SPLIT_BEFORE[6:]:
                split_w(0, u)

            def attend(b):
                for h in range(GH):
                    exps(b, h)
                    if not (b.end and h + 1 == GH):
                        nb, nh = (b, h + 1) if h + 1 < GH else (b.next(), 0)
                        qk_hi(nb, nh, 0)
                        qk_hi(nb, nh, 1)
                    pt_split(b, h)
                    for u in SPLIT_FIRST[h] if b.first else ():
                        split_w(b.hg, u)
                    for u in SPLIT_LAST[h] if b.last and not b.end else ():
                        split_w(b.hg + 1, u)
                    if h >= TPB and not b.end:
                        v_split(b.next(), h - TPB)
                    z_split(b, h)
                    if h == 1:
                        sum_abs(b)

            over_groups(act, attend)

            act.wait_ge(s_acc, after(GROUPS * TILES))
            act.wait_ge(s_const2, 32)

            def ctx_split(n, b):
                act.wait_ge(s_ctxdma[b.slot], (n // 2 + 1) * 16 if isinstance(n, int) else
                            (b.half + 1) * 16 if n is b.index else (b.half + 1 + PAIRS) * 16)
                nc.scalar.copy(ctx_hi[:, b.slot, :, :].rearrange("p c n -> p (c n)"), ctx_raw[:, b.slot, :]
                               ).then_inc(s_ctxhi, 1)

            def split_banks(hi, base, done):
                nc.scalar.copy(hi, psum[:, base:base + 2, :]).then_inc(done, 1)

            def xt_split(n, slot, base):
                act.wait_ge(s_xt, after(n + 1))
                split_banks(xt_hi[:, slot, :, :].rearrange("p (a c) n -> p a (c n)", a=2), base, s_xthi)

            def xq_split(b):
                act.wait_ge(s_xq, after(b.index + 1))
                if not b.start:
                    act.wait_ge(s_xs, after(b.index - 1))
                split_banks(xq_hi[:, b.slot, :, :].rearrange("p (a h) n -> p a (h n)", a=2), 2, s_xqhi)

            act.wait_ge(s_g, after(1))
            nc.scalar.copy(g_hi[:, :, :].rearrange("p h e -> p (h e)"), bank[2]).then_inc(s_ghi, 1)
            nc.scalar.copy(wh_hi[:, :, :].rearrange("p h e -> p (h e)"), wx_raw[:, 0, :]).then_inc(s_whsplit, 1)
            xt_split(0, 0, 0)

            def pass_1(b):
                if not b.start:
                    act.wait_ge(s_xs, after(b.index - 1))
                ctx_split(b.index, b)
                if not b.last:
                    if not b.first:
                        act.wait_ge(s_xq, after(b.index))
                    xt_split(b.next().index, b.next().slot, 0)
                xq_split(b)
                if isinstance(b.index, int) and b.index == BATCH - 3:
                    wgo_split(0)

            def wgo_split(i):
                act.wait_ge(s_wgo[i], 16)
                nc.scalar.copy(wgo_hi[:, i, :, :], wgo_raw[:, i, :, :]).then_inc(s_gohi, 1)

            over_batches_1(act, pass_1)
            act.wait_ge(s_xs, after(BATCH - 1))
            ctx_split(BATCH, Batch(0))
            act.wait_ge(s_xq, after(BATCH - 1))
            xt_split(BATCH, 0, 0)
            act.wait_ge(s_xs, after(BATCH))
            ctx_split(BATCH + 1, Batch(1))
            act.wait_ge(s_araw, after(3))
            nc.scalar.copy(a_hi[:, :, :], a_raw[:, :, :]).then_inc(s_ahi, 1)

            def xv_split(p, j, tt):
                act.wait_ge(s_xv, after(4 * p + 2 * j + tt + 1))
                act.wait_ge(s_xo, after(2 * p))
                nc.scalar.copy(xv_hi[:, tt, :, j, :], bank[2 + tt].rearrange("p (h e) -> p h e", h=XH)
                               ).then_inc(s_xvhi, 1)

            def keep_rows(n, rows, j, p):
                act.wait_ge(s_xn, after(n + 1))
                nc.scalar.copy(pick(acc, 4 * p + 2 * j, TPB), rows[:, j, :, :]).then_inc(s_back, 1)

            def xt2_split(p, j):
                act.wait_ge(s_xt, after(2 * p + 2 * BATCH + j + 1))
                split_banks(xt2_hi[:, j, :, :].rearrange("p (a c) n -> p a (c n)", a=2), 2 - 2 * j, s_xthi)

            def relu(p, k):
                act.wait_ge(s_gate, after(4 * p + k + 1))
                act.wait_ge(s_wyt, after(4 * p))
                nc.scalar.activation(gate[:, k, :], bank[0], ACT.Relu).then_inc(s_relu, 1)

            def wyt_split(p, k):
                act.wait_ge(s_wyt, after(4 * p + k + 1))
                act.wait_ge(s_xout, after(4 * p + k - 1) if k else after(4 * p))
                nc.scalar.copy(wyt_hi[:, k % 2, :, :].rearrange("p c n -> p (c n)"), bank[2 + k % 2]
                               ).then_inc(s_wythi, 1)

            for tt in range(TPB):
                xv_split(0, 0, tt)
            keep_rows(BATCH, xn, 0, 0)
            for tt in range(TPB):
                xv_split(0, 1, tt)
            xt_split(BATCH + 1, 1, 0)
            keep_rows(BATCH + 1, xn, 1, 0)
            wgo_split(1)

            def pass_2(p, more):
                if more:
                    for j in range(2):
                        act.wait_ge(s_xv, after(4 * p + 2 * j + 2))
                        ctx_split(2 * p + BATCH + 2 + j, Batch(2 + j, p))
                relu(p, 0)
                if more:
                    xv_split(p + 1, 0, 0)
                    xv_split(p + 1, 0, 1)
                relu(p, 1)
                if more:
                    xt_split(2 * p + BATCH + 2, 0, 2)
                    keep_rows(2 * p + BATCH + 2, xn, 0, p + 1)
                relu(p, 2)
                if more:
                    xv_split(p + 1, 1, 0)
                    xv_split(p + 1, 1, 1)
                wyt_split(p, 0)
                relu(p, 3)
                for k in range(1, 4):
                    wyt_split(p, k)
                if more:
                    xt_split(2 * p + BATCH + 3, 1, 2)
                    keep_rows(2 * p + BATCH + 3, xn, 1, p + 1)

            with act.Fori(0, PAIRS - 1) as p:
                pass_2(p, True)
            pass_2(PAIRS - 1, False)

            def hidden(p, f):
                n = FC * p + f
                act.wait_ge(s_up, after(n + 1))
                act.wait_ge(s_hid, after(n - min(f, 1)))
                nc.scalar.activation(sig[:, f % 2, :], bank[f % 2 * 2], ACT.Sigmoid).then_inc(s_sig, 1)
                act.wait_ge(s_hid, after(n + 1))
                act.wait_ge(s_down, after(n - min(f, 1)))
                nc.scalar.copy(hid_hi[:, f % 2, :], hid[:, f % 2, :]).then_inc(s_hhi, 1)

            for j in range(2):
                xt2_split(0, j)
                keep_rows(2 * BATCH + j, xn2, j, 0)

            def pass_3(p, more):
                for f in range(FC):
                    hidden(p, f)
                    if more and f in (6, 7):
                        keep_rows(2 * p + 2 * BATCH + 2 + f - 6, xn2, f - 6, p + 1)
                if more:
                    for j in range(2):
                        xt2_split(p + 1, j)

            with act.Fori(0, PAIRS - 1) as p:
                pass_3(p, True)
            pass_3(PAIRS - 1, False)

        @block.vector
        def _(dve):
            def split_w(hg, u):
                dve.wait_ge(s_whi, after(hg * UNITS + u + 1))
                nc.vector.tensor_tensor(out=w_lo[:, u, :], in0=w_raw[:, u % RING, :],
                                        in1=w_hi[:, u, :].bitcast(F32), op=ALU.subtract).then_inc(s_wlo, 1)

            def low(out_ap, ps, bias_ap, hi_ap, done):
                nc.vector.scalar_tensor_tensor(out=out_ap, in0=ps, scalar=bias_ap, in1=hi_ap.bitcast(F32),
                                               op0=ALU.add, op1=ALU.subtract).then_inc(done, 1)

            def qk_lo(b, h, part):
                n = GH * b.all + h
                dve.wait_ge(s_khi if part else s_qhi, after(n + 1))
                low((k_lo if part else q_lo)[:, :], (ps_k if part else ps_q)[:, 0:SEQ], bias_of(b, part, h),
                    (k_hi if part else q_hi)[:, :], s_klo if part else s_qlo)

            def v_split(b, tt):
                dve.wait_ge(s_vhi, after(TPB * b.all + tt + 1))
                nc.vector.tensor_tensor(out=v_lo[:, b.slot, tt, :], in0=ps_v[:, :],
                                        in1=v_hi[:, b.slot, tt, :].bitcast(F32),
                                        op=ALU.subtract).then_inc(s_vlo, 1)

            def row_max(b, h):
                n = GH * b.all + h
                dve.wait_ge(s_scores, after(n + 1))
                dve.nop(nofuse=True)
                for qt in range(TPB):
                    s = ps_s[:, qt * P:qt * P + (qt + 1) * P]
                    nc.vector.tensor_tensor_reduce(s, s, mask[:, SEQ - (qt + 1) * P:SEQ], -SCALE, 3e38,
                                                   ALU.add, ALU.min, negmax[:, qt:qt + 1]).then_inc(s_max, 1)

            def normalise(b, h):
                n = GH * b.all + h
                dve.wait_ge(s_exp, after(n + 1))
                nc.vector.reciprocal(inv[:, :], rowsum[:, :]).then_inc(s_inv, 1)
                dve.wait_ge(s_inv, after(n + 1))
                nc.vector.tensor_scalar(probs[:, 0:P], probs[:, 0:P], inv[:, 0:1], None, ALU.mult)
                nc.vector.tensor_scalar(probs[:, P:KEYS], probs[:, P:KEYS], inv[:, 1:2], None,
                                        ALU.mult).then_inc(s_norm, 1)

            def pt_split(b, h):
                n = GH * b.all + h
                dve.wait_ge(s_pthi, after(n + 1))
                nc.vector.tensor_tensor(out=pt_lo[:, :], in0=ps_pt[:, 0:KEYS], in1=pt_hi[:, :].bitcast(F32),
                                        op=ALU.subtract).then_inc(s_ptlo, 1)

            def z_split(b, h):
                n = GH * b.all + h
                dve.wait_ge(s_zhi, after(n + 1))
                low(z_lo[:, b.slot, h, :], ps_z[:, 0:SEQ], bias_of(b, 2, h), z_hi[:, b.slot, h, :], s_zlo)

            def add_output(b, tt):
                n = TPB * b.index + tt
                dve.wait_ge(s_o, after(TPB * b.all + tt + 1))
                dve.wait_ge(s_bo, after(n + 1))
                nc.vector.tensor_tensor(out=pick(acc, n), in0=ps_o[:, :], in1=pick(acc, n), op=ALU.add
                                        ).then_inc(s_acc, 1)

            def row_stats(n, k, ins):
                dve.nop(nofuse=True)
                for i, a in enumerate(ins):
                    nc.vector.bn_stats(bn_raw[:, k + i, :], a).then_inc(s_bn, 1)
                dve.wait_ge(s_bn, after(n + len(ins)))
                dve.nop(nofuse=True)
                for i in range(len(ins)):
                    nc.vector.bn_aggr(bn[:, k + i, :], bn_raw[:, k + i, :]).then_inc(s_aggr, 1)
                dve.wait_ge(s_aggr, after(n + len(ins)))

            def row_stats_1(b, tt):
                dve.wait_ge(s_acc, after(TPB * b.all + tt + 1))
                dve.nop(nofuse=True)
                nc.vector.bn_stats(bn_raw[:, tt, :], pick(acc, TPB * b.index + tt)).then_inc(s_bn, 1)

            def keep_stats_1(b):
                n = TPB * b.index
                dve.wait_ge(s_bn, after(n + TPB))
                dve.nop(nofuse=True)
                for tt in range(TPB):
                    nc.vector.bn_aggr(bn[:, tt, :], bn_raw[:, tt, :]).then_inc(s_aggr, 1)
                dve.wait_ge(s_aggr, after(n + TPB))
                st = stats[0][:, n:n + TPB, :] if isinstance(n, int) else stats[0][:, bass.ds(n, TPB), :]
                nc.vector.tensor_copy(st[:, :, 0:1], bn[:, 0:TPB, 0:1])
                nc.vector.tensor_scalar(st[:, :, 1:2], bn[:, 0:TPB, 1:2], LN_EPS, None, ALU.add).then_inc(s_mean, 1)

            dve.wait_ge(s_primed, 1)
            dve.wait_ge(s_xhi, after(1))
            nc.vector.tensor_tensor(out=x_lo[:, 0, :, :].rearrange("p c n -> p (c n)"), in0=x_raw[:, 0, :],
                                    in1=x_hi[:, 0, :, :].rearrange("p c n -> p (c n)").bitcast(F32),
                                    op=ALU.subtract).then_inc(s_x, 1)
            for u in SPLIT_BEFORE[:6]:
                split_w(0, u)
            dve.wait_ge(s_const, 64)
            dve.wait_ge(s_primed, 2)
            for tt in range(TPB):
                v_split(Batch(0), tt)
            qk_lo(Batch(0), 0, 0)
            qk_lo(Batch(0), 0, 1)
            for u in SPLIT_BEFORE[6:]:
                split_w(0, u)

            def attend(b):
                for h in range(GH):
                    row_max(b, h)
                    if isinstance(b.hg, int) and b.hg == GROUPS - 1 and not b.first:
                        if 1 <= h <= TPB:
                            row_stats_1(b.prev(), h - 1)
                        elif h == GH - 1:
                            keep_stats_1(b.prev())
                    if b.first and not (h == 0 and b.start):
                        for u in SPLIT_FIRST[h - 1] if h else SPLIT_LAST[GH - 1]:
                            split_w(b.hg, u)
                    if b.last and h and not b.end:
                        for u in SPLIT_LAST[h - 1]:
                            split_w(b.hg + 1, u)
                    more = not (b.end and h + 1 == GH)
                    nb, nh = (b, h + 1) if h + 1 < GH else (b.next(), 0)
                    if more:
                        qk_lo(nb, nh, 0)
                    normalise(b, h)
                    if more:
                        qk_lo(nb, nh, 1)
                    pt_split(b, h)
                    if h < TPB:
                        if not (b.start and b.first):
                            add_output(b.prev(), h)
                    elif not b.end:
                        v_split(b.next(), h - TPB)
                    z_split(b, h)

            over_groups(dve, attend)
            b = Batch(BATCH - 1, 0, GROUPS - 1)
            for tt in range(TPB):
                add_output(b, tt)
                row_stats_1(b, tt)
            keep_stats_1(b)

            def minus(out_ap, a, hi, done):
                nc.vector.tensor_tensor(out=out_ap, in0=a, in1=hi.bitcast(F32), op=ALU.subtract).then_inc(done, 1)

            def row_variance(n, event, lag, k, ins, eps):
                row_stats(n, k, ins)
                dve.wait_ge(s_rdev, after(event + 1 - lag))
                nc.vector.tensor_scalar(variance[:, k:k + len(ins), :], bn[:, k:k + len(ins), 1:2], eps, None, ALU.add
                                        ).then_inc(s_var, 1)

            def sum_stats(which, n, event, lag, tile, k, count):
                row_variance(n, event, lag, k, [pick(acc, tile + i) for i in range(count)], LN_EPS)
                st = stats[which][:, tile:tile + count, :] if isinstance(tile, int) else \
                    stats[which][:, bass.ds(tile, count), :]
                nc.vector.tensor_copy(st[:, :, 0:1], bn[:, k:k + count, 0:1]).then_inc(s_mean, 1)

            def normal_rows(which, tile, rows, slot):
                for tt in range(TPB):
                    st = pick(stats[which], tile + tt)
                    last = nc.vector.tensor_scalar(rows[:, slot, tt, :], pick(acc, tile + tt), st[:, 0:1], st[:, 1:2],
                                                   ALU.subtract, ALU.mult)
                last.then_inc(s_xn, 1)

            def norm_1(b):
                if not b.start:
                    dve.wait_ge(s_xt, after(b.index - 1))
                normal_rows(0, TPB * b.index, xn, b.slot)

            def xt_low(n, slot, base, hi, lo):
                dve.wait_ge(s_xthi, after(n + 1))
                minus(lo[:, slot, :, :].rearrange("p (a c) n -> p a (c n)", a=2), psum[:, base:base + 2, :],
                      hi[:, slot, :, :].rearrange("p (a c) n -> p a (c n)", a=2), s_xtlo)

            def xq_low(b):
                dve.wait_ge(s_xqhi, after(b.index + 1))
                minus(xq_lo[:, b.slot, :, :].rearrange("p (a h) n -> p a (h n)", a=2), psum[:, 2:4, :],
                      xq_hi[:, b.slot, :, :].rearrange("p (a h) n -> p a (h n)", a=2), s_xqlo)

            dve.wait_ge(s_abs, after(GROUPS * BATCH))
            nc.vector.tensor_reduce(wtot[:, :], wsum[:, :, :].rearrange("p b m -> p m b"), AX_X, ALU.add).then_inc(s_tot, 1)
            dve.wait_ge(s_totps, after(1))
            for i, sign in enumerate((0.5, -0.5)):
                nc.vector.tensor_scalar(thr[:, i, :], bank[3][:, 0:3], 1.0 / (DIM * FF), 1e-8, ALU.mult, ALU.add
                                        ).then_inc(s_thr, 1)
            dve.wait_ge(s_thr, after(2))
            for i, sign in enumerate((0.5, -0.5)):
                nc.vector.tensor_scalar(thr[:, i, :], thr[:, i, :], sign, None, ALU.mult).then_inc(s_thr, 1)
            dve.wait_ge(s_thr, after(4))
            dve.wait_ge(s_rdev, after(1))
            norm_1(Batch(0))
            norm_1(Batch(1))
            dve.wait_ge(s_ghi, after(1))
            minus(g_lo[:, :, :].rearrange("p h e -> p (h e)"), bank[2],
                  g_hi[:, :, :].rearrange("p h e -> p (h e)"), s_glo)
            xt_low(0, 0, 0, xt_hi, xt_lo)
            dve.wait_ge(s_whsplit, after(1))
            minus(wh_lo[:, :, :].rearrange("p h e -> p (h e)"), wx_raw[:, 0, :],
                  wh_hi[:, :, :].rearrange("p h e -> p (h e)"), s_wh)

            def pass_1(b):
                if isinstance(b.index, int) and b.index >= BATCH - 2:
                    dve.wait_ge(s_xt, after(b.index + 1))
                    normal_rows(0, TPB * b.slot, xn, b.slot)
                else:
                    norm_1(b.next().next())
                if not b.last:
                    xt_low(b.next().index, b.next().slot, 0, xt_hi, xt_lo)
                xq_low(b)

            over_batches_1(dve, pass_1)

            dve.wait_ge(s_xs, after(BATCH))
            nc.vector.tensor_tensor(out=a_raw[:, :, :], in0=psum[:, 4:8, 0:KEYS], in1=decay[:, :, :],
                                    op=ALU.mult).then_inc(s_araw, 1)
            dve.wait_ge(s_araw, after(1))
            flat = a_raw[:, :, :].rearrange("p h n -> p (h n)")
            nc.vector.scalar_tensor_tensor(out=flat, in0=flat, scalar=-1.0, in1=flat, op0=ALU.mult, op1=ALU.max
                                           ).then_inc(s_araw, 1)
            dve.wait_ge(s_araw, after(2))
            nc.vector.tensor_scalar(flat, flat, 1.0, None, ALU.max).then_inc(s_araw, 1)

            def norm_2(p, j):
                n = 2 * p + j
                dve.wait_ge(s_xt, after(n + BATCH - 1))
                dve.wait_ge(s_back, after(n - 1))
                normal_rows(0, TPB * n, xn, j)

            def xv_low(p, j, tt):
                dve.wait_ge(s_xvhi, after(4 * p + 2 * j + tt + 1))
                minus(xv_lo[:, tt, :, j, :], bank[2 + tt].rearrange("p (h e) -> p h e", h=XH),
                      xv_hi[:, tt, :, j, :], s_xvlo)

            xt_low(BATCH, 0, 0, xt_hi, xt_lo)
            dve.wait_ge(s_ahi, after(1))
            minus(a_lo[:, :, :], a_raw[:, :, :], a_hi[:, :, :], s_alo)
            for tt in range(TPB):
                xv_low(0, 0, tt)
            for tt in range(TPB):
                xv_low(0, 1, tt)
            xt_low(BATCH + 1, 1, 0, xt_hi, xt_lo)
            dve.wait_ge(s_gdma, 32)

            N1 = TILES
            S1 = 1

            def group(p, k):
                return psum[:, 4 + 2 * (k % 2):6 + 2 * (k % 2), :].rearrange(
                    "p a (h j e) -> p (a h) j e", h=2, j=2)[:, :, k // 2, :]

            def norm_3(p, j):
                n = 2 * p + j
                if isinstance(p, int) and p == 0:
                    if j == 0:
                        dve.wait_ge(s_xv, after(4 * PAIRS))
                        dve.wait_ge(s_rdev, after(1 + 8))
                        dve.wait_ge(s_mean, after(BATCH + 4))
                else:
                    dve.wait_ge(s_xt, after(n + 2 * BATCH - 1))
                    dve.wait_ge(s_back, after(n + BATCH - 1))
                normal_rows(1, TPB * n, xn2, j)

            def ternary(u):
                m = u % 3
                dve.wait_ge(s_fdma[u % RING], (u // RING + 1) * 16)
                nc.vector.tensor_scalar(f_neg[:, u % 2, :], f_raw[:, u % RING, :], thr[:, 1, m:m + 1], None,
                                        ALU.is_lt).then_inc(s_neg, 1)
                dve.wait_ge(s_neg, after(u + 1))
                nc.vector.scalar_tensor_tensor(out=f_w[:, u, :], in0=f_raw[:, u % RING, :],
                                               scalar=thr[:, 0, m:m + 1], in1=f_neg[:, u % 2, :],
                                               op0=ALU.is_gt, op1=ALU.subtract).then_inc(s_fw, 1)

            def group_stats(p, k):
                dve.wait_ge(s_xo, after(2 * p + k % 2 + 1))
                row_variance(8 * p + N1 + k, 8 * p + S1 + k, 2, 2 + k % 2, [group(p, k)], GN_EPS)

            def group_norm(p, k):
                y = y_raw[:, k % 2, :]
                nc.vector.scalar_tensor_tensor(out=y.rearrange("p (h e) -> p h e", h=XH), in0=group(p, k),
                                               scalar=bn[:, 2 + k % 2, 0:1],
                                               in1=gamma[:, :].rearrange("p (h e) -> p h e", h=XH),
                                               op0=ALU.subtract, op1=ALU.mult).then_inc(s_yc, 1)
                dve.wait_ge(s_yc, after(4 * p + k + 1))
                dve.wait_ge(s_rdev, after(8 * p + S1 + k + 1))
                nc.vector.scalar_tensor_tensor(out=y, in0=y, scalar=rdev[:, k % 2, 0:1], in1=beta[:, :],
                                               op0=ALU.mult, op1=ALU.add).then_inc(s_ys, 1)

            def gated(p, k):
                dve.wait_ge(s_relu, after(4 * p + k + 1))
                dve.wait_ge(s_ys, after(4 * p + k + 1))
                nc.vector.tensor_tensor(out=gate[:, k, :], in0=gate[:, k, :], in1=y_raw[:, k % 2, :],
                                        op=ALU.mult).then_inc(s_wy, 1)

            def wyt_low(p, k):
                dve.wait_ge(s_wythi, after(4 * p + k + 1))
                minus(wyt_lo[:, k % 2, :, :].rearrange("p c n -> p (c n)"), bank[2 + k % 2],
                      wyt_hi[:, k % 2, :, :].rearrange("p c n -> p (c n)"), s_wytlo)

            def residual(p, k):
                tile = 4 * p + k
                dve.wait_ge(s_back, after(2 * p + k // 2 + 1))
                dve.wait_ge(s_xout, after(tile + 1))
                a = pick(acc, tile)
                nc.vector.tensor_tensor(out=a, in0=bank[1 - k % 2], in1=a, op=ALU.add).then_inc(s_res, 1)
                dve.wait_ge(s_res, after(tile + 1))
                sum_stats(1, 8 * p + N1 + 4 + k, 8 * p + S1 + 4 + k, 2, tile, k % 2, 1)

            def pass_2(p, more):
                group_stats(p, 0)
                group_stats(p, 1)
                group_norm(p, 0)
                gated(p, 0)
                group_norm(p, 1)
                if more:
                    xv_low(p + 1, 0, 0)
                    xv_low(p + 1, 0, 1)
                    norm_2(p + 1, 0)
                gated(p, 1)
                group_stats(p, 2)
                if more:
                    xt_low(2 * p + BATCH + 2, 0, 2, xt_hi, xt_lo)
                group_stats(p, 3)
                group_norm(p, 2)
                if more:
                    xv_low(p + 1, 1, 0)
                    xv_low(p + 1, 1, 1)
                group_norm(p, 3)
                wyt_low(p, 0)
                gated(p, 2)
                if more:
                    norm_2(p + 1, 1)
                wyt_low(p, 1)
                gated(p, 3)
                if not more:
                    norm_3(0, 0)
                residual(p, 0)
                wyt_low(p, 2)
                residual(p, 1)
                if not more:
                    norm_3(0, 1)
                wyt_low(p, 3)
                residual(p, 2)
                if not more:
                    for u in range(2):
                        ternary(u)
                if more:
                    xt_low(2 * p + BATCH + 3, 1, 2, xt_hi, xt_lo)
                else:
                    xt_low(2 * BATCH, 0, 2, xt2_hi, xt2_lo)
                residual(p, 3)

            with dve.Fori(0, PAIRS - 1) as p:
                pass_2(p, True)
            pass_2(PAIRS - 1, False)

            N2, S2 = 3 * TILES, 1 + 2 * TILES

            def hidden(p, f):
                n = FC * p + f
                dve.wait_ge(s_sig, after(n + 1))
                dve.wait_ge(s_hhi, after(n - min(f, 1)))
                nc.vector.tensor_tensor(out=hid[:, f % 2, :], in0=bank[f % 2 * 2 + 1], in1=sig[:, f % 2, :],
                                        op=ALU.mult).then_inc(s_hid, 1)

            def hidden_low(p, f):
                dve.wait_ge(s_hhi, after(FC * p + f + 1))
                minus(hid_lo[:, f % 2, :], hid[:, f % 2, :], hid_hi[:, f % 2, :], s_hlo)

            def last_sums(p):
                dve.wait_ge(s_down, after(FC * p + FC))
                dve.wait_ge(s_yout, after(64 * p))
                for k in range(4):
                    dve.wait_ge(s_back, after(2 * p + BATCH + k // 2 + 1))
                    nc.vector.tensor_tensor(out=y3[:, k, :], in0=bank[4 + k], in1=pick(acc, 4 * p + k), op=ALU.add
                                            ).then_inc(s_y3, 1)

            def last_stats(p, k):
                dve.wait_ge(s_y3, after(4 * p + k + 2))
                row_variance(4 * p + N2 + k, 2 * p + S2 + k // 2, 2, k, [y3[:, k + i, :] for i in range(2)], LN_EPS)

            def last_rows(p, k):
                dve.wait_ge(s_rdev, after(2 * p + S2 + k // 2 + 1))
                for i in range(k, k + 2):
                    nc.vector.tensor_scalar(y3[:, i, :], y3[:, i, :], bn[:, i, 0:1], rdev[:, i, 0:1],
                                            ALU.subtract, ALU.mult).then_inc(s_y3n, 1)

            xt_low(2 * BATCH + 1, 1, 0, xt2_hi, xt2_lo)
            ternary(2)

            def pass_3(p, first, more):
                for f in range(FC):
                    if first and f + 1 < FC:
                        for m in range(3):
                            ternary(3 * (f + 1) + m)
                    hidden(p, f)
                    hidden_low(p, f)
                    if not first and f < 4:
                        (last_stats, last_rows)[f // 2](p - 1, f % 2 * 2)
                    if more and f in (4, 5):
                        norm_3(p + 1, f - 4)
                if more:
                    for j in range(2):
                        xt_low(2 * p + 2 * BATCH + 2 + j, j, 2 - 2 * j, xt2_hi, xt2_lo)
                last_sums(p)

            dve.wait_ge(s_rdev, after(S2))
            pass_3(0, True, True)
            with dve.Fori(1, PAIRS - 1) as p:
                pass_3(p, False, True)
            pass_3(PAIRS - 1, False, False)
            for step in last_stats, last_rows:
                for k in range(0, 4, 2):
                    step(PAIRS - 1, k)


def kernel(**inputs):
    import numpy as _np
    import concourse.bacc as _bacc
    from concourse import mybir as _mybir
    from concourse.bass_utils import run_bass_kernel_spmd as _run

    i = {k: _np.asarray(v) for k, v in inputs.items()}
    groups = []
    for g in range(GROUPS):
        hs = range(g * GH, (g + 1) * GH)
        q = [i["L0_attn_W_Q"][h].reshape(CH, P, DH).transpose(1, 0, 2).reshape(P, 512) for h in hs]
        k = [i["L0_attn_W_K"][h].reshape(CH, P, DH).transpose(1, 0, 2).reshape(P, 512) for h in hs]
        v = _np.concatenate([i["L0_attn_W_V"][h].reshape(CH, P, 1, DH) for h in hs], axis=2).reshape(CH, P, GH * DH)
        o = [i["L0_attn_W_O"][h] for h in hs]
        groups.append(_np.stack([*v, q[0], k[0], q[1], k[1], q[2], k[2], q[3], k[3], *o]))
    rows = _np.arange(P)
    gam = 1.0 - 2.0 ** (-5.0 - _np.arange(XH))
    expo = _np.arange(SEQ)[None, :] - _np.arange(SEQ)[:, None]
    full = _np.where(expo <= 0, gam[:, None, None] ** _np.minimum(expo, 0), 0.0)
    full = (full / _np.sqrt(full.sum(-1))[:, None, :] / _np.sqrt(float(DH))).transpose(2, 0, 1)
    by_chunks = lambda w: w.reshape(CH, P, -1).transpose(1, 0, 2)
    w1, w2, w3 = (i[f"L0_ffn_w{n}"] for n in (1, 2, 3))
    w_ffn = _np.stack([w1.reshape(FC, P, CH, P).transpose(0, 3, 2, 1).reshape(FC, P, 512),
                       w2.reshape(FC, P, CH, P).transpose(0, 3, 2, 1).reshape(FC, P, 512),
                       w3.T.reshape(FC, P, DIM)], axis=1)
    wh = i["L0_xattn_Wh"]
    in_rows = lambda v: _np.broadcast_to(v, (P, DIM))
    arrays = {
        "xT": i["x"].reshape(BATCH, SEQ, CH, P).transpose(0, 3, 2, 1).reshape(BATCH, P, CH * SEQ),
        "x": i["x"].reshape(TILES, P, DIM).transpose(1, 0, 2),
        "w_attn": _np.concatenate(groups),
        "biases": _np.stack([i[f"L0_attn_b_{k}"].reshape(GROUPS, GH, DH) for k in "QKV"], axis=1)
                  .reshape(GROUPS * 3 * GH, DH).T,
        "ctxT": i["ctx_2048"].reshape(BATCH, SEQ, CH, P).transpose(0, 3, 2, 1).reshape(BATCH, P, CH * SEQ),
        "w_head": _np.stack([wh.transpose(1, 0, 2).reshape(P, 512), wh.transpose(2, 0, 1).reshape(P, 512)], axis=1),
        "decay": _np.concatenate([full[:P], full[P:, :, P:]], axis=2).astype(_np.float32),
        "b_o": in_rows(i["L0_attn_b_O"]),
        "gamma": in_rows(i["L0_xattn_gn_gamma"]),
        "beta": in_rows(i["L0_xattn_gn_beta"]),
        "w_gate": by_chunks(i["L0_xattn_wg_w"]),
        "w_out": by_chunks(i["L0_xattn_wo_w"]),
        "w_ffn": w_ffn.reshape(3 * FC, P, 512),
        "w_abs": _np.stack([w.reshape(GROUPS * BATCH, P, ABS_COLS) for w in (w1, w2, w3)], axis=2)
                 .reshape(GROUPS * BATCH, P, 3 * ABS_COLS),
        "identity": _np.eye(P, dtype=_np.float32),
        "causal": _np.concatenate([_np.zeros((P, P)), _np.where(rows[None, :] <= rows[:, None], 0.0, MASKED)],
                                  axis=1).astype(_np.float32),
    }
    nc = _bacc.Bacc("TRN2", target_bir_lowering=False, num_devices=1)
    feed, t = {}, {}
    for name, a in arrays.items():
        a = _np.ascontiguousarray(a)
        feed[f"in_{name}"] = a
        t[name] = nc.dram_tensor(f"in_{name}", a.shape, _mybir.dt.from_np(a.dtype), kind="ExternalInput").ap()
    out = nc.dram_tensor("out_0", (BATCH, SEQ, DIM), F32, kind="ExternalOutput").ap()
    decoder_kernel(nc, t, out.rearrange("b (t p) d -> p (b t) d", p=P))
    r = _run(nc, [feed], core_ids=[0])
    return r.results[0]["out_0"]
```
